# Optimizing a Trainium2 kernel written in Bass

```python
import numpy as np
import jax
import jax.numpy as jnp

def _softmax(x, axis=-1):
    return jax.nn.softmax(x, axis=axis)

def _gelu(x):
    return jax.nn.gelu(x, approximate=True)

def _silu(x):
    return jax.nn.silu(x)

def _sigmoid(x):
    return jax.nn.sigmoid(x)

def _layernorm(x, axis=-1, eps=1e-05):
    m = jnp.mean(x, axis=axis, keepdims=True)
    v = jnp.var(x, axis=axis, keepdims=True)
    return (x - m) / jnp.sqrt(v + eps)

def _scatter_add(tgt, idx, src, axis=0):
    return tgt.at[idx].add(src)

def _segment_sum(src, seg, n):
    return jax.ops.segment_sum(src, seg, n)
kernel_name = 'mk_recurrent_d1_jaxref_r8_0afde5'

def setup_inputs(seed: int=0):
    np.random.seed(seed)
    _w = jnp.asarray

    def _L0_attn_setup():
        import jax, jax.numpy as jnp
        import numpy as np
        B, T, C, FFN, N_LAYER, LAYER_ID = (4, 256, 128, 512, 24, 1)
        EPS = 1e-05

        def _ln(z, g, b):
            m = jnp.mean(z, axis=-1, keepdims=True)
            v = jnp.mean(jnp.square(z - m), axis=-1, keepdims=True)
            return (z - m) * jax.lax.rsqrt(v + EPS) * g + b

        def _shift(z):
            return jnp.pad(z, ((0, 0), (1, 0), (0, 0)))[:, :-1]

        def _wkv(time_decay, u, k, v):
            w = -jnp.exp(time_decay)
            kt = jnp.moveaxis(k, 1, 0)
            vt = jnp.moveaxis(v, 1, 0)
            aa = jnp.zeros_like(kt[0])
            bb = jnp.zeros_like(kt[0])
            pp = jnp.full_like(kt[0], -1e+38)

            def step(carry, kv):
                aa, bb, pp = carry
                kk, vv = kv
                ww = u + kk
                p = jnp.maximum(pp, ww)
                e1 = jnp.exp(pp - p)
                e2 = jnp.exp(ww - p)
                out = (e1 * aa + e2 * vv) / (e1 * bb + e2)
                ww2 = pp + w
                p2 = jnp.maximum(ww2, kk)
                e1b = jnp.exp(ww2 - p2)
                e2b = jnp.exp(kk - p2)
                return ((e1b * aa + e2b * vv, e1b * bb + e2b, p2), out)
            _, out = jax.lax.scan(step, (aa, bb, pp), (kt, vt))
            return jnp.moveaxis(out, 0, 1)
        key = jax.random.key(seed)
        ks = jax.random.split(key, 10)
        scale = 0.02

        def w(k, shape):
            return jax.random.normal(k, shape, jnp.float32) * scale
        r01 = LAYER_ID / (N_LAYER - 1)
        r10 = 1.0 - LAYER_ID / N_LAYER
        ddd = np.arange(C, dtype=np.float64) / C
        h = np.arange(C, dtype=np.float64)
        decay = -5.0 + 8.0 * (h / (C - 1)) ** (0.7 + 1.3 * r01)
        zigzag = np.array([(i + 1) % 3 - 1 for i in range(C)], dtype=np.float64) * 0.5
        tfirst = np.log(0.3) + zigzag
        return {'x': jax.random.normal(ks[0], (B, T, C), jnp.float32), 'ln1_w': jnp.ones((C,), jnp.float32), 'ln1_b': jnp.zeros((C,), jnp.float32), 'ln2_w': jnp.ones((C,), jnp.float32), 'ln2_b': jnp.zeros((C,), jnp.float32), 'time_decay': jnp.asarray(decay, jnp.float32), 'time_first': jnp.asarray(tfirst, jnp.float32), 'tmk': jnp.asarray(ddd ** r10, jnp.float32), 'tmv': jnp.asarray(ddd ** r10 + 0.3 * r01, jnp.float32), 'tmr': jnp.asarray(ddd ** (0.5 * r10), jnp.float32), 'att_kw': w(ks[1], (C, C)), 'att_vw': w(ks[2], (C, C)), 'att_rw': w(ks[3], (C, C)), 'att_ow': w(ks[4], (C, C)), 'f_tmk': jnp.asarray(ddd ** r10, jnp.float32), 'f_tmr': jnp.asarray(ddd ** r10, jnp.float32), 'f_kw': w(ks[5], (FFN, C)), 'f_rw': w(ks[6], (C, C)), 'f_vw': w(ks[7], (C, FFN))}
    _L0_attn_in = _L0_attn_setup()

    def _L0_ffn_setup():
        import jax, jax.numpy as jnp
        import numpy as np
        B, S, H, F, E = (1, 256, 128, 256, 8)

        def _swiglu(x, wg, wu, wd):
            return jax.nn.silu(x @ wg.T) * (x @ wu.T) @ wd.T
        key = jax.random.key(seed)
        ks = jax.random.split(key, 8)
        sc = 1.0 / np.sqrt(H)
        scf = 1.0 / np.sqrt(F)
        return {'hidden_states': jax.random.normal(ks[0], (B, S, H), jnp.float32), 'gate_w': jax.random.normal(ks[1], (E, H), jnp.float32) * sc, 'shared_gate': jax.random.normal(ks[2], (F, H), jnp.float32) * sc, 'shared_up': jax.random.normal(ks[3], (F, H), jnp.float32) * sc, 'shared_down': jax.random.normal(ks[4], (H, F), jnp.float32) * scf, 'r_gate': jax.random.normal(ks[5], (E, F, H), jnp.float32) * sc, 'r_up': jax.random.normal(ks[6], (E, F, H), jnp.float32) * sc, 'r_down': jax.random.normal(ks[7], (E, H, F), jnp.float32) * scf}
    _L0_ffn_in = _L0_ffn_setup()
    _d = {'L0_attn_x': _L0_attn_in['x'], 'L0_attn_ln1_w': _L0_attn_in['ln1_w'], 'L0_attn_ln1_b': _L0_attn_in['ln1_b'], 'L0_attn_ln2_w': _L0_attn_in['ln2_w'], 'L0_attn_ln2_b': _L0_attn_in['ln2_b'], 'L0_attn_time_decay': _L0_attn_in['time_decay'], 'L0_attn_time_first': _L0_attn_in['time_first'], 'L0_attn_tmk': _L0_attn_in['tmk'], 'L0_attn_tmv': _L0_attn_in['tmv'], 'L0_attn_tmr': _L0_attn_in['tmr'], 'L0_attn_att_kw': _L0_attn_in['att_kw'], 'L0_attn_att_vw': _L0_attn_in['att_vw'], 'L0_attn_att_rw': _L0_attn_in['att_rw'], 'L0_attn_att_ow': _L0_attn_in['att_ow'], 'L0_attn_f_tmk': _L0_attn_in['f_tmk'], 'L0_attn_f_tmr': _L0_attn_in['f_tmr'], 'L0_attn_f_kw': _L0_attn_in['f_kw'], 'L0_attn_f_rw': _L0_attn_in['f_rw'], 'L0_attn_f_vw': _L0_attn_in['f_vw'], 'L0_ffn_gate_w': _L0_ffn_in['gate_w'], 'L0_ffn_shared_gate': _L0_ffn_in['shared_gate'], 'L0_ffn_shared_up': _L0_ffn_in['shared_up'], 'L0_ffn_shared_down': _L0_ffn_in['shared_down'], 'L0_ffn_r_gate': _L0_ffn_in['r_gate'], 'L0_ffn_r_up': _L0_ffn_in['r_up'], 'L0_ffn_r_down': _L0_ffn_in['r_down']}
    _x0 = _d['L0_attn_x']
    _d['L0_attn_x'] = jax.random.normal(jax.random.fold_in(jax.random.key(seed), 1), (32, 256, 128), dtype=_x0.dtype)
    del _x0
    return _d

def reference(L0_attn_x, L0_attn_ln1_w, L0_attn_ln1_b, L0_attn_ln2_w, L0_attn_ln2_b, L0_attn_time_decay, L0_attn_time_first, L0_attn_tmk, L0_attn_tmv, L0_attn_tmr, L0_attn_att_kw, L0_attn_att_vw, L0_attn_att_rw, L0_attn_att_ow, L0_attn_f_tmk, L0_attn_f_tmr, L0_attn_f_kw, L0_attn_f_rw, L0_attn_f_vw, L0_ffn_gate_w, L0_ffn_shared_gate, L0_ffn_shared_up, L0_ffn_shared_down, L0_ffn_r_gate, L0_ffn_r_up, L0_ffn_r_down):

    def _L0_attn_ref(x, ln1_w, ln1_b, ln2_w, ln2_b, time_decay, time_first, tmk, tmv, tmr, att_kw, att_vw, att_rw, att_ow, f_tmk, f_tmr, f_kw, f_rw, f_vw):
        import jax, jax.numpy as jnp
        import numpy as np
        B, T, C, FFN, N_LAYER, LAYER_ID = (4, 256, 128, 512, 24, 1)
        EPS = 1e-05

        def _ln(z, g, b):
            m = jnp.mean(z, axis=-1, keepdims=True)
            v = jnp.mean(jnp.square(z - m), axis=-1, keepdims=True)
            return (z - m) * jax.lax.rsqrt(v + EPS) * g + b

        def _shift(z):
            return jnp.pad(z, ((0, 0), (1, 0), (0, 0)))[:, :-1]

        def _wkv(time_decay, u, k, v):
            w = -jnp.exp(time_decay)
            kt = jnp.moveaxis(k, 1, 0)
            vt = jnp.moveaxis(v, 1, 0)
            aa = jnp.zeros_like(kt[0])
            bb = jnp.zeros_like(kt[0])
            pp = jnp.full_like(kt[0], -1e+38)

            def step(carry, kv):
                aa, bb, pp = carry
                kk, vv = kv
                ww = u + kk
                p = jnp.maximum(pp, ww)
                e1 = jnp.exp(pp - p)
                e2 = jnp.exp(ww - p)
                out = (e1 * aa + e2 * vv) / (e1 * bb + e2)
                ww2 = pp + w
                p2 = jnp.maximum(ww2, kk)
                e1b = jnp.exp(ww2 - p2)
                e2b = jnp.exp(kk - p2)
                return ((e1b * aa + e2b * vv, e1b * bb + e2b, p2), out)
            _, out = jax.lax.scan(step, (aa, bb, pp), (kt, vt))
            return jnp.moveaxis(out, 0, 1)
        h = _ln(x, ln1_w, ln1_b)
        hx = _shift(h)
        xk = h * tmk + hx * (1.0 - tmk)
        xv = h * tmv + hx * (1.0 - tmv)
        xr = h * tmr + hx * (1.0 - tmr)
        k = jnp.einsum('btc,dc->btd', xk, att_kw)
        v = jnp.einsum('btc,dc->btd', xv, att_vw)
        sr = jax.nn.sigmoid(jnp.einsum('btc,dc->btd', xr, att_rw))
        rwkv = sr * _wkv(time_decay, time_first, k, v)
        x = x + jnp.einsum('btd,cd->btc', rwkv, att_ow)
        h = _ln(x, ln2_w, ln2_b)
        hx = _shift(h)
        xk = h * f_tmk + hx * (1.0 - f_tmk)
        xr = h * f_tmr + hx * (1.0 - f_tmr)
        kk = jnp.square(jax.nn.relu(jnp.einsum('btc,fc->btf', xk, f_kw)))
        kv = jnp.einsum('btf,cf->btc', kk, f_vw)
        x = x + jax.nn.sigmoid(jnp.einsum('btc,dc->btd', xr, f_rw)) * kv
        return x

    def _L0_ffn_ref(hidden_states, gate_w, shared_gate, shared_up, shared_down, r_gate, r_up, r_down):
        import jax, jax.numpy as jnp
        import numpy as np
        B, S, H, F, E = (1, 256, 128, 256, 8)

        def _swiglu(x, wg, wu, wd):
            return jax.nn.silu(x @ wg.T) * (x @ wu.T) @ wd.T
        b, s, h = hidden_states.shape
        x = hidden_states.reshape(-1, h)
        shared_out = _swiglu(x, shared_gate, shared_up, shared_down)
        logits = x @ gate_w.T
        top_id = jnp.argmax(logits, axis=-1)
        score = jax.nn.sigmoid(jnp.max(logits, axis=-1))
        xs = x * score[:, None]

        def body(acc, ws):
            wg, wu, wd, e = ws
            xe = jnp.where((top_id == e)[:, None], xs, 0.0)
            return (acc + _swiglu(xe, wg, wu, wd), None)
        acc0 = jnp.zeros_like(x)
        routed_out, _ = jax.lax.scan(body, acc0, (r_gate, r_up, r_down, jnp.arange(E)))
        return (shared_out + routed_out).reshape(b, s, h)
    x = L0_attn_x
    xn = _layernorm(x, axis=-1)
    s = _L0_attn_ref(xn, L0_attn_ln1_w, L0_attn_ln1_b, L0_attn_ln2_w, L0_attn_ln2_b, L0_attn_time_decay, L0_attn_time_first, L0_attn_tmk, L0_attn_tmv, L0_attn_tmr, L0_attn_att_kw, L0_attn_att_vw, L0_attn_att_rw, L0_attn_att_ow, L0_attn_f_tmk, L0_attn_f_tmr, L0_attn_f_kw, L0_attn_f_rw, L0_attn_f_vw)
    g = _silu(_L0_ffn_ref(xn, L0_ffn_gate_w, L0_ffn_shared_gate, L0_ffn_shared_up, L0_ffn_shared_down, L0_ffn_r_gate, L0_ffn_r_up, L0_ffn_r_down))
    x = x + s * g
    return x

_drawn_inputs = setup_inputs


def setup_inputs(seed=0):
    import zlib

    import numpy as np

    out = dict(_drawn_inputs(seed))
    spreads = {'L0_attn_ln1_w': (1.0, 0.6),
     'L0_attn_ln1_b': (0.0, 0.8),
     'L0_attn_ln2_w': (1.0, 0.6),
     'L0_attn_ln2_b': (0.0, 0.8)}
    factors = {'L0_attn_time_decay': 8.0,
     'L0_attn_time_first': 8.0,
     'L0_attn_tmk': 8.0,
     'L0_attn_tmv': 8.0,
     'L0_attn_tmr': 8.0,
     'L0_attn_att_kw': 8.0,
     'L0_attn_att_vw': 8.0,
     'L0_attn_att_rw': 8.0,
     'L0_attn_att_ow': 8.0,
     'L0_attn_f_tmk': 8.0,
     'L0_attn_f_tmr': 8.0,
     'L0_attn_f_kw': 8.0,
     'L0_attn_f_rw': 8.0,
     'L0_attn_f_vw': 8.0}
    for name, (base, spread) in spreads.items():
        noise = np.random.default_rng([zlib.crc32(name.encode()), seed]).standard_normal(out[name].shape)
        drawn = base * np.exp(spread * noise) if base else spread * noise
        out[name] = jnp.asarray(drawn.astype(out[name].dtype))
    for name, factor in factors.items():
        out[name] = (out[name] * factor).astype(out[name].dtype)
    return out
```

```python
import concourse.bass as bass
from concourse import mybir
from contextlib import ExitStack

BATCH, SEQ, CH = 32, 256, 128
TOKENS = BATCH * SEQ
P = 128
CHUNK = 512
BPC = CHUNK // SEQ
TPC = CHUNK // P
CHUNKS = TOKENS // CHUNK
TILES = TOKENS // P
FFN = 512
FQ = FFN // P
EXPERTS = 8
EF = 256
EQ = EF // P
XTILES = TILES + EXPERTS - 1
SCATTER_STEPS = 4
CPS = CHUNKS // SCATTER_STEPS
XSLOTS = 6
XROW = CH + 4
NOWHERE = 1048576.0
EPS = 1e-5
NEG = -1e38
(V_G1, V_B1, V_G2, V_B2, V_DECAY, V_FIRST, V_TMK, V_TMV, V_TMR, V_FTMK, V_FTMR, V_W) = range(12)
NVEC = 11
K_ID, K_TRI, K_ONE, K_E8, K_CAP, K_TILE, K_TOK = 0, 128, 256, 384, 392, 456, 536
NCST = K_TOK + TILES


def program(nc, x, vecs, cst, att_w, f_kw, f_vw, gate_w, sh_up, sh_dn, ex_up, ex_dn, out):
    f32, i32 = mybir.dt.float32, mybir.dt.int32
    ALU, ACT, AX = mybir.AluOpType, mybir.ActivationFunctionType, mybir.AxisListType
    ds = bass.ds

    xs_dram = nc.dram_tensor("tokens_by_expert", [XTILES * P, XROW], f32, kind="Internal").ap()
    routed_dram = nc.dram_tensor("routed_out", [TOKENS, CH], f32, kind="Internal").ap()

    ctx = ExitStack()
    with ctx:
        def sb(name, width, dt=f32):
            return ctx.enter_context(nc.sbuf_tensor(name, [P, width], dt))

        def sem(name):
            return ctx.enter_context(nc.semaphore(name))

        def bank(name):
            return ctx.enter_context(nc.psum_tensor(name, [P, CHUNK], f32))

        XN = sb("xn", TOKENS)
        XT = sb("xt", TOKENS)
        VEC = sb("vectors", 12)
        CST = sb("consts", NCST)
        ATT = sb("att", 5 * CH)
        FKW = sb("fkw", FFN)
        FVW = sb("fvw", FQ * CH)
        GW = sb("gw", EXPERTS)
        SUP = sb("sup", 2 * EF)
        SDN = sb("sdn", EQ * CH)
        EUP = sb("eup", EXPERTS * 2 * EF)
        EDN = sb("edn", EXPERTS * EQ * CH)
        R2 = sb("r2", TILES)
        POS = sb("pos", TILES, i32)
        SC = sb("score", TILES)
        ET = sb("expert_of_tile", 80, i32)
        NH = sb("minus_half", TPC)

        XI = [sb(f"xi{u}", CHUNK) for u in range(2)]
        ZC = [sb(f"zc{u}", CHUNK) for u in range(2)]
        BS = [sb(f"bs{u}", TPC * 6) for u in range(2)]
        MV = [sb(f"mv{u}", TPC * 2) for u in range(2)]
        SM = [sb(f"sm{u}", 5 * TPC) for u in range(2)]

        MX = sb("mx", TILES)
        RT = sb("rt", 8 * EXPERTS)
        POSF = sb("posf", TILES)

        XSS = [sb(f"xss{u}", TPC * XROW) for u in range(2)]
        PIX = [sb(f"pix{u}", TPC, i32) for u in range(2)]

        Z1 = sb("z1", CHUNK)
        H1 = sb("h1", BPC * (SEQ + 1))
        D1 = sb("d1", CHUNK)
        XK, XV, XR = sb("xk", CHUNK), sb("xv", CHUNK), sb("xr", CHUNK)
        PP = sb("pp", BPC * (SEQ + 1))
        AA = sb("aa", BPC * (SEQ + 1))
        BB = sb("bb", BPC * (SEQ + 1))
        E1, E2 = sb("e1", CHUNK), sb("e2", CHUNK)
        DD = sb("dd", CHUNK)
        M1, M2 = sb("m1", CHUNK), sb("m2", CHUNK)
        EV = sb("ev", CHUNK)
        N1, N2, NUM = sb("n1", CHUNK), sb("n2", CHUNK), sb("num", CHUNK)
        Q1, DEN, LQ = sb("q1", CHUNK), sb("den", CHUNK), sb("lq", CHUNK)
        TR = sb("tr", CHUNK)
        RW = sb("rw", CHUNK)

        X2 = sb("x2", CHUNK)
        BS2, MV2, SM2 = sb("bs2", TPC * 6), sb("mv2", TPC * 2), sb("sm2", 2 * TPC)
        ZA, Z2 = sb("za", CHUNK), sb("z2", CHUNK)
        H2 = sb("h2", BPC * (SEQ + 1))
        D2, XK2, XR2 = sb("d2", CHUNK), sb("xk2", CHUNK), sb("xr2", CHUNK)
        TF = sb("tf", CHUNK)
        RK = sb("rk", 2 * CHUNK)
        KK = sb("kk", FQ * CHUNK)
        CAND, OH, CUM = (KK[:, k * TILES * EXPERTS:(k + 1) * TILES * EXPERTS] for k in range(3))
        UU = ZA

        TG, PS, HS = sb("tg", CHUNK), sb("ps", CHUNK), sb("hs", EQ * CHUNK)
        NX = 3
        XS = [sb(f"xs{u}", XROW) for u in range(NX)]
        TX, PX, HX = sb("tx", EF), sb("px", EF), sb("hx", EF)
        XH = [sb(f"xh{u}", P + EF) for u in range(2)]
        YX = [sb(f"yx{u}", CH) for u in range(NX)]
        YI = [sb(f"yi{u}", 1, i32) for u in range(NX)]

        XTS = [XK[:, :], XV[:, :]]
        FY = [D1[:, :], D2[:, :]]
        FT = [XK[:, :], XK2[:, :]]
        FW = [XV[:, :], XR2[:, :]]
        FV = [XR[:, :], EV[:, :]]
        FO = [N1[:, :], N2[:, :]]

        BK, BV = bank("bank_k"), bank("bank_v")
        FA, FB = bank("bank_fa"), bank("bank_fb")
        BT = bank("bank_transposed")
        BO = bank("bank_out")
        BG = bank("bank_gate_up")
        BX = bank("bank_expert")
        YX_ = BX[:, P + EF:P + EF + CH]

        s_w = sem("weights_loaded")
        s_fill = sem("xs_dram_filled")
        s_pad = sem("pad_row_made")
        s_init = sem("constants_made")
        s_half = sem("weights_halved")
        s_xi = [sem(f"x_loaded{u}") for u in range(2)]
        s_bn = sem("x_partial_stats")
        s_mv = sem("x_stats")
        s_sm = sem("x_small_chain")
        s_r2 = sem("r2_made")
        s_settled = sem("settled")
        s_w0 = sem("decay_exp")
        s_w1 = sem("decay_negated")
        s_oh = sem("routing_side_chain")
        s_zc = sem("x_centred")
        s_xn = sem("xn_made")
        s_xnt = sem("xn_transposed")
        s_xt = sem("xt_made")
        s_xts = sem("xt_staged")
        s_xns = sem("xn_staged")
        s_lg = sem("logits_made")
        s_rt = sem("routing_chain")
        s_rm = sem("routing_prefix_made")
        s_sc = sem("scores_made")
        s_xss = sem("scatter_rows_made")
        s_sct = [sem(f"rows_scattered{u}") for u in range(2)]

        s_z1, s_z1t, s_h1, s_d1, s_mix = sem("z1"), sem("z1_transposed"), sem("h1"), sem("d1"), sem("mixed")
        s_k, s_v, s_r = sem("k"), sem("v"), sem("r")
        s_pp, s_a, s_b, s_d = sem("running_max"), sem("a"), sem("b"), sem("d")
        s_tr, s_e1, s_e2, s_m, s_g = sem("tanh_r"), sem("e1"), sem("e2"), sem("relu_d"), sem("exp_d")
        s_ev, s_aa, s_bb, s_n2 = sem("ev"), sem("aa"), sem("bb"), sem("n2")
        s_n1, s_q1, s_num, s_den = sem("n1"), sem("q1"), sem("num"), sem("den")
        s_lq, s_iq, s_tn, s_rw = sem("ln_den"), sem("inv_den"), sem("tn"), sem("rwkv")

        s_att, s_x2, s_bn2, s_mv2 = sem("att_out"), sem("x2"), sem("x2_partial_stats"), sem("x2_stats")
        s_sm2, s_za, s_z2, s_z2t = sem("x2_small_chain"), sem("x2_centred"), sem("z2"), sem("z2_transposed")
        s_h2, s_d2, s_mix2 = sem("h2"), sem("d2"), sem("mixed2")
        s_fr, s_tf, s_fk, s_rk, s_kk = sem("fr"), sem("tanh_fr"), sem("fk"), sem("relu_fk"), sem("kk")
        s_kv, s_u, s_s = sem("kv"), sem("u"), sem("s")

        s_sg, s_tg, s_ps, s_su, s_hs = sem("sh_gate"), sem("sh_tanh"), sem("sh_gated"), sem("sh_up"), sem("sh_h")
        s_sd, s_sh = sem("sh_down"), sem("sh_out")

        s_xs = [sem(f"xs_loaded{u}") for u in range(NX)]
        s_xht, s_xh = sem("x_and_h_transposed"), sem("xh_copied")
        s_gu, s_tx, s_px, s_hx = sem("gate_up"), sem("x_tanh"), sem("x_gated"), sem("x_h")
        s_y_, s_y = sem("y_psum"), sem("y")
        s_yi = sem("y_rows")
        s_yo = [sem(f"y_scattered{u}") for u in range(NX)]

        s_fx = [sem(f"final_loaded{u}") for u in range(2)]
        s_fy, s_ft, s_fw, s_fv, s_fo = (sem("final_y"), sem("final_tanh"), sem("final_silu"),
                                        sem("final_gated"), sem("final_out"))
        s_out = [sem(f"out_stored{u}") for u in range(2)]

        ident = CST[:, K_ID:K_ID + P]

        def vec(n):
            return VEC[:, n:n + 1]

        def tiles(ap):
            return ap.rearrange("p (j c) -> p j c", j=TPC)

        def batches(ap):
            return ap.rearrange("p (b t) -> p b t", b=BPC)

        def now(t):
            return t[:, :].rearrange("p (b t) -> p b t", b=BPC)[:, :, 1:SEQ + 1]

        def before(t):
            return t[:, :].rearrange("p (b t) -> p b t", b=BPC)[:, :, 0:SEQ]

        def per_tile(ap):
            return ap.unsqueeze(2).to_broadcast([P, TPC, CH])

        def chunk(t, c, w=CHUNK):
            return t[:, ds(c * w, w)]

        def stats(t):
            v = t[:, :].rearrange("p (j s) -> p s j", s=2)
            return v[:, 0, :], v[:, 1, :]

        def slot(i, s):
            return XSLOTS * (i - SCATTER_STEPS) + s + 1

        def is_int(v):
            return isinstance(v, int)

        block = ctx.enter_context(nc.Block())

        def settle(eng):
            eng.sem_inc(s_settled, 1)

        def drive(eng, step, before_experts):
            step(0, True)
            step(1, True)
            with eng.Fori(2, SCATTER_STEPS) as i:
                step(i, True)
            before_experts()
            step(SCATTER_STEPS, False)
            with eng.Fori(SCATTER_STEPS + 1, CHUNKS - 1) as i:
                step(i, False)
            step(CHUNKS - 1, False)
            step(CHUNKS, False)

        def has(i, part):
            if not is_int(i):
                return True
            return {"T": i < CHUNKS, "P": i + 1 < CHUNKS, "C": i > 0}[part]

        def tile_of(i, s):
            return slot(i, s) if is_int(i) else (i, s)

        def num(n, d=0):
            return n + d if is_int(n) else slot(n[0], n[1]) + d

        def exists(n, d=0):
            return not is_int(n) or 0 <= n + d < XTILES

        def place(n, d=0):
            return (n + d) % NX if is_int(n) else (n[1] + 1 + d) % NX

        def parity(n, d=0):
            return (n + d) % 2 if is_int(n) else (n[1] + 1 + d) % 2

        def laps(n, d=0):
            if is_int(n):
                return (n + d) // NX + 1
            return (n[0] - SCATTER_STEPS) * (XSLOTS // NX) + (n[1] + 1 + d) // NX + 1

        @block.sync
        def _(sp):
            W = [(VEC[:, 0:NVEC], vecs), (CST[:, :], cst), (GW[:, :], gate_w), (ATT[:, :], att_w),
                 (SUP[:, :], sh_up), (SDN[:, :], sh_dn), (FKW[:, :], f_kw), (FVW[:, :], f_vw),
                 (EUP[:, :], ex_up), (EDN[:, :], ex_dn)]

            def load_x(c, u):
                sp.dma_start(tiles(XI[u][:, :]), x[ds(c * CHUNK, CHUNK), :].rearrange("(j p) c -> p j c", p=P))\
                  .then_inc(s_xi[u], 16)

            load_x(0, 0)
            load_x(1, 1)
            for dst, src in W[0:3]:
                sp.dma_start(dst, src).then_inc(s_w, 16)
            sp.wait_ge(s_pad, 2)
            sp.dma_start(xs_dram.rearrange("(n p) c -> p n c", p=P),
                         XSS[0][:, 0:XROW].unsqueeze(1).to_broadcast([P, XTILES, XROW])).then_inc(s_fill, 16)
            with sp.Fori(1, CHUNKS // 2) as h:
                for u in range(2):
                    sp.wait_ge(s_zc, 2 * h + u - 1)
                    load_x(2 * h + u, u)
            for dst, src in W[3:]:
                sp.dma_start(dst, src).then_inc(s_w, 16)

            def load_xs(n, d=0):
                u = place(n, d)
                if not is_int(n) or n + d >= NX:
                    sp.wait_ge(s_xht, num(n, d) - NX + 1)
                    sp.wait_ge(s_yi, num(n, d) - NX + 1)
                sp.dma_start(XS[u][:, :], xs_dram[ds(num(n, d) * P, P), :]).then_inc(s_xs[u], 16)

            def step(i, scatter):
                if scatter:
                    return
                for s in range(XSLOTS):
                    n = tile_of(i, s)
                    if exists(n, 2):
                        load_xs(n, 2)

            for u in range(2):
                sp.wait_ge(s_sct[u], 16 * TPC * CHUNKS // 2)
            for n in range(3):
                load_xs(n)
            step(SCATTER_STEPS, False)
            with sp.Fori(SCATTER_STEPS + 1, CHUNKS - 1) as i:
                step(i, False)
            step(CHUNKS - 1, False)

            for u in range(NX):
                sp.wait_ge(s_yo[u], 16 * ((XTILES - 1 - u) // NX + 1))

            def load_final(c, u):
                sp.dma_start(tiles(XI[u][:, :]), x[ds(c * CHUNK, CHUNK), :].rearrange("(j p) c -> p j c", p=P))\
                  .then_inc(s_fx[u], 16)
                sp.dma_start(tiles(ZC[u][:, :]),
                             routed_dram[ds(c * CHUNK, CHUNK), :].rearrange("(j p) c -> p j c", p=P))\
                  .then_inc(s_fx[u], 16)

            def store(c, u):
                sp.wait_ge(s_fo, c + 1)
                sp.dma_start(out[ds(c * CHUNK, CHUNK), :].rearrange("(j p) c -> p j c", p=P), tiles(FO[u]))\
                  .then_inc(s_out[u], 16)

            load_final(0, 0)
            load_final(1, 1)
            with sp.Fori(1, CHUNKS // 2) as h:
                for u in range(2):
                    store(2 * h + u - 2, u)
                    load_final(2 * h + u, u)
            for u in range(2):
                store(CHUNKS - 2 + u, u)
            for u in range(2):
                sp.wait_ge(s_out[u], 16 * (CHUNKS // 2))

        @block.tensor
        def _(pe):
            pe.wait_ge(s_w, 16 * 3)

            def first(c, u, h):
                pe.wait_ge(s_xns, c + 1)
                if h is not None:
                    pe.wait_ge(s_xt, c - 1)
                b = (BT, BO)[u]
                for j in range(TPC):
                    last = nc.tensor.transpose(b[:, j * P:(j + 1) * P], ZC[u][:, j * P:(j + 1) * P], ident)
                last.then_inc(s_xnt, 1)

            def logits(c, u):
                pe.wait_ge(s_xts, c + 1)
                for j in range(TPC):
                    last = nc.tensor.matmul(BG[:, ds(c * (TPC * EXPERTS) + j * EXPERTS, EXPERTS)],
                                            XTS[u][:, j * P:(j + 1) * P], GW[:, :], start=True, stop=True)
                last.then_inc(s_lg, 1)

            first(0, 0, None)
            first(1, 1, None)
            with pe.Fori(1, CHUNKS // 2) as h:
                logits(2 * h - 2, 0)
                first(2 * h, 0, h)
                logits(2 * h - 1, 1)
                first(2 * h + 1, 1, h)
            logits(CHUNKS - 2, 0)
            logits(CHUNKS - 1, 1)

            pe.wait_ge(s_rt, 13)
            nc.tensor.matmul(BX[:, 0:EXPERTS], CST[:, K_TRI:K_TRI + P], RT[:, 0:EXPERTS], start=True, stop=True)
            nc.tensor.matmul(BX[:, EXPERTS:2 * EXPERTS], CST[:, K_ONE:K_ONE + P], RT[:, 0:EXPERTS],
                             start=True, stop=True).then_inc(s_rm, 1)

            pe.wait_ge(s_w, 16 * 10)
            pe.wait_ge(s_half, 3)

            def z1_transpose(c):
                pe.wait_ge(s_z1, c + 1)
                if not is_int(c):
                    pe.wait_ge(s_h2, c - 2)
                elif c > 2:
                    pe.wait_ge(s_h2, c - 2)
                elif c == 0:
                    pe.wait_ge(s_xt, CHUNKS)
                else:
                    pe.wait_ge(s_h1, c)
                for j in range(TPC):
                    last = nc.tensor.transpose(BT[:, j * P:(j + 1) * P], Z1[:, j * P:(j + 1) * P], ident)
                last.then_inc(s_z1t, 1)

            def key_value_receptance(c):
                pe.wait_ge(s_mix, 3 * c + 3)
                if not is_int(c) or c > 0:
                    pe.wait_ge(s_d, c)
                    pe.wait_ge(s_n2, c)
                    if not is_int(c) or c > 1:
                        pe.wait_ge(s_rk, 4 * c - 5)
                    else:
                        pe.wait_ge(s_hs, 2 * c)
                nc.tensor.matmul(BK[:, :], ATT[:, 0:CH], XK[:, :], start=True, stop=True).then_inc(s_k, 1)
                nc.tensor.matmul(BV[:, :], ATT[:, CH:2 * CH], XV[:, :], start=True, stop=True).then_inc(s_v, 1)
                nc.tensor.matmul(FA[:, :], ATT[:, 2 * CH:3 * CH], XR[:, :], start=True, stop=True).then_inc(s_r, 1)

            def attention_out(c):
                pe.wait_ge(s_rw, c + 1)
                if is_int(c) and c == 0:
                    pe.wait_ge(s_sh, 1)
                else:
                    pe.wait_ge(s_u, c)
                for j in range(TPC):
                    last = nc.tensor.matmul(BO[:, j * CH:(j + 1) * CH], RW[:, j * P:(j + 1) * P],
                                            ATT[:, 3 * CH:4 * CH], start=True, stop=True)
                last.then_inc(s_att, 1)

            def shared_gate_up(c, q):
                if q == 0:
                    if not is_int(c) or c > 1:
                        pe.wait_ge(s_rk, 4 * c - 4)
                    elif c == 1:
                        pe.wait_ge(s_ps, 2)
                else:
                    pe.wait_ge(s_ps, 2 * c + 1)
                rhs = chunk(XT, c)
                nc.tensor.matmul(FB[:, :], SUP[:, q * P:(q + 1) * P], rhs, start=True, stop=True).then_inc(s_sg, 1)
                if q == 0:
                    pe.wait_ge(s_tr, c + 1)
                else:
                    pe.wait_ge(s_hs, 2 * c + 1)
                nc.tensor.matmul(FA[:, :], SUP[:, EF + q * P:EF + (q + 1) * P], rhs, start=True, stop=True)\
                  .then_inc(s_su, 1)

            def shared_down(c):
                pe.wait_ge(s_hs, 2 * c + 2)
                if is_int(c) and c == 0:
                    pe.wait_ge(s_xt, CHUNKS)
                else:
                    pe.wait_ge(s_x2, c)
                for j in range(TPC):
                    for q in range(EQ):
                        last = nc.tensor.matmul(BO[:, j * CH:(j + 1) * CH],
                                                HS[:, q * CHUNK + j * P:q * CHUNK + (j + 1) * P],
                                                SDN[:, q * CH:(q + 1) * CH], start=(q == 0), stop=(q == EQ - 1))
                last.then_inc(s_sd, 1)

            def z2_transpose(c):
                pe.wait_ge(s_z2, c + 1)
                if not is_int(c):
                    pe.wait_ge(s_h1, c + 3)
                else:
                    pe.wait_ge(s_h1, min(c + 3, CHUNKS))
                for j in range(TPC):
                    last = nc.tensor.transpose(BT[:, j * P:(j + 1) * P], Z2[:, j * P:(j + 1) * P], ident)
                last.then_inc(s_z2t, 1)

            def ffn_receptance_key(c):
                pe.wait_ge(s_mix2, 2 * c + 2)
                pe.wait_ge(s_ps, 2 * c + 4 if not is_int(c) else min(2 * c + 4, 2 * CHUNKS))
                for j in range(TPC):
                    last = nc.tensor.matmul(FB[:, j * CH:(j + 1) * CH], XR2[:, j * P:(j + 1) * P],
                                            ATT[:, 4 * CH:5 * CH], start=True, stop=True)
                last.then_inc(s_fr, 1)
                pe.wait_ge(s_hs, 2 * c + 4 if not is_int(c) else min(2 * c + 4, 2 * CHUNKS))
                for q in range(FQ):
                    if q == 1:
                        pe.wait_ge(s_tf, c + 1)
                    if q >= 2:
                        pe.wait_ge(s_rk, 4 * c + q - 1)
                    nc.tensor.matmul((FA, FB)[q % 2][:, :], FKW[:, q * P:(q + 1) * P], XK2[:, :],
                                     start=True, stop=True).then_inc(s_fk, 1)

            def ffn_value(c):
                pe.wait_ge(s_kk, 4 * c + 4)
                pe.wait_ge(s_sh, c + 2 if not is_int(c) else min(c + 2, CHUNKS))
                if is_int(c) and c == CHUNKS - 1:
                    pe.wait_ge(s_x2, CHUNKS)
                for j in range(TPC):
                    for q in range(FQ):
                        last = nc.tensor.matmul(BO[:, j * CH:(j + 1) * CH],
                                                KK[:, q * CHUNK + j * P:q * CHUNK + (j + 1) * P],
                                                FVW[:, q * CH:(q + 1) * CH], start=(q == 0), stop=(q == FQ - 1))
                last.then_inc(s_kv, 1)

            def expert_slot(n):
                if exists(n) and (not is_int(n) or n >= 0):
                    e_up = nc.tensor.value_load(ET[0:1, ds(num(n), 1)], min_val=0, max_val=EXPERTS - 1)
                if exists(n, -1):
                    e_dn = nc.tensor.value_load(ET[0:1, ds(num(n, -1), 1)], min_val=0, max_val=EXPERTS - 1)
                    pe.wait_ge(s_hx, num(n))
                    if not is_int(n) or n > 1:
                        pe.wait_ge(s_y, num(n, -1))
                    for q in range(EQ):
                        last = nc.tensor.transpose(BX[:, P + q * P:P + (q + 1) * P], HX[:, q * P:(q + 1) * P], ident)
                if exists(n, 1):
                    u = place(n, 1)
                    pe.wait_ge(s_xs[u], 16 * laps(n, 1))
                    if is_int(n) and n == 0:
                        pe.wait_ge(s_xh, 1)
                    last = nc.tensor.transpose(BX[:, 0:P], XS[u][:, 0:CH], ident)
                last.then_inc(s_xht, 1)
                if is_int(n) and n < 0:
                    return
                if exists(n):
                    pe.wait_ge(s_xh, num(n, 1))
                    nc.tensor.matmul(BG[:, :], XH[parity(n, 1)][:, 0:P], EUP[:, ds(e_up * (2 * EF), 2 * EF)],
                                     start=True, stop=True).then_inc(s_gu, 1)
                if exists(n, -1):
                    pe.wait_ge(s_xh, num(n, 2))
                    for q in range(EQ):
                        last = nc.tensor.matmul(YX_, XH[parity(n)][:, P + q * P:P + (q + 1) * P],
                                                EDN[:, ds(e_dn * (EQ * CH) + q * CH, CH)],
                                                start=(q == 0), stop=(q == EQ - 1))
                    last.then_inc(s_y_, 1)

            def step(i, scatter):
                def experts(s):
                    if not scatter and exists(tile_of(i, s), -1) and has(i, "T"):
                        expert_slot(tile_of(i, s))

                if has(i, "T"):
                    key_value_receptance(i)
                if has(i, "C"):
                    attention_out(i - 1)
                experts(0)
                if has(i, "T"):
                    shared_gate_up(i, 0)
                if has(i, "P"):
                    z1_transpose(i + 1)
                experts(1)
                if has(i, "T"):
                    shared_gate_up(i, 1)
                if has(i, "C"):
                    z2_transpose(i - 1)
                experts(2)
                if has(i, "T"):
                    shared_down(i)
                experts(3)
                if has(i, "C"):
                    ffn_receptance_key(i - 1)
                experts(4)
                if has(i, "C"):
                    ffn_value(i - 1)
                experts(5)

            def before_experts():
                pe.wait_ge(s_rt, 27)
                expert_slot(-1)
                expert_slot(0)

            z1_transpose(0)
            drive(pe, step, before_experts)

        @block.scalar
        def _(act):
            act.wait_ge(s_w, 16 * 3)
            nc.scalar.activation(vec(V_W), vec(V_DECAY), ACT.Exp).then_inc(s_w0, 1)

            def first(c, u, h):
                act.wait_ge(s_xnt, c + 1)
                if not is_int(h):
                    act.wait_ge(s_lg, c - 1)
                nc.scalar.activation(XTS[u], (BT, BO)[u][:, :], ACT.Copy).then_inc(s_xts, 1)
                nc.scalar.activation(chunk(XT, c), (BT, BO)[u][:, :], ACT.Copy).then_inc(s_xt, 1)

            first(0, 0, 0)
            first(1, 1, 0)
            with act.Fori(1, CHUNKS // 2) as h:
                for u in range(2):
                    first(2 * h + u, u, h)
            act.wait_ge(s_rt, 1)
            nc.scalar.activation(SC[:, :], MX[:, :], ACT.Sigmoid).then_inc(s_sc, 1)
            act.wait_ge(s_w, 16 * 10)
            for w in (SDN[:, :], EDN[:, :], ATT[:, 3 * CH:4 * CH]):
                nc.scalar.activation(w, w, ACT.Copy, scale=0.5).then_inc(s_half, 1)

            def make_h1(c):
                act.wait_ge(s_z1t, c + 1)
                if not is_int(c) or c > 0:
                    act.wait_ge(s_mix, 3 * c)
                nc.scalar.activation(now(H1), batches(BT[:, :]), ACT.Identity, bias=vec(V_B1),
                                     scale=vec(V_G1)).then_inc(s_h1, 1)

            def make_h2(c):
                act.wait_ge(s_z2t, c + 1)
                if not is_int(c) or c > 0:
                    act.wait_ge(s_mix2, 2 * c)
                nc.scalar.activation(now(H2), batches(BT[:, :]), ACT.Identity, bias=vec(V_B2),
                                     scale=vec(V_G2)).then_inc(s_h2, 1)

            def wkv_exponentials(c):
                act.wait_ge(s_a, c + 1)
                nc.scalar.activation(E1[:, :], E1[:, :], ACT.Exp).then_inc(s_e1, 1)
                act.wait_ge(s_b, c + 1)
                nc.scalar.activation(E2[:, :], E2[:, :], ACT.Exp).then_inc(s_e2, 1)
                act.wait_ge(s_r, c + 1)
                if not is_int(c) or c > 0:
                    act.wait_ge(s_tn, c)
                nc.scalar.activation(TR[:, :], FA[:, :], ACT.Tanh, scale=0.5).then_inc(s_tr, 1)
                act.wait_ge(s_d, c + 1)
                if not is_int(c) or c > 0:
                    act.wait_ge(s_n1, c)
                    act.wait_ge(s_den, c)
                nc.scalar.activation(M1[:, :], DD[:, :], ACT.Relu, scale=-1.0).then_inc(s_m, 1)
                nc.scalar.activation(M2[:, :], DD[:, :], ACT.Relu).then_inc(s_m, 1)
                act.wait_ge(s_m, 2 * c + 1)
                nc.scalar.activation(M1[:, :], M1[:, :], ACT.Exp, scale=-1.0).then_inc(s_g, 1)
                act.wait_ge(s_m, 2 * c + 2)
                nc.scalar.activation(M2[:, :], M2[:, :], ACT.Exp, scale=-1.0).then_inc(s_g, 1)

            def inverse_of_den(c):
                act.wait_ge(s_den, c + 1)
                if not is_int(c) or c > 0:
                    act.wait_ge(s_rw, c)
                nc.scalar.activation(LQ[:, :], DEN[:, :], ACT.Ln).then_inc(s_lq, 1)
                act.wait_ge(s_lq, c + 1)
                nc.scalar.activation(LQ[:, :], LQ[:, :], ACT.Exp, scale=-1.0).then_inc(s_iq, 1)

            def shared_tanh(c, q):
                act.wait_ge(s_sg, 2 * c + q + 1)
                if not (is_int(c) and c == 0 and q == 0):
                    act.wait_ge(s_ps, 2 * c + q)
                nc.scalar.activation(TG[:, :], FB[:, :], ACT.Tanh, scale=0.5).then_inc(s_tg, 1)

            def ffn_activations(c):
                act.wait_ge(s_fr, c + 1)
                if not is_int(c) or c > 0:
                    act.wait_ge(s_u, c)
                nc.scalar.activation(TF[:, :], FB[:, :], ACT.Tanh, scale=0.5).then_inc(s_tf, 1)
                for q in range(FQ):
                    act.wait_ge(s_fk, 4 * c + q + 1)
                    if not (is_int(c) and c == 0 and q < 2):
                        act.wait_ge(s_kk, 4 * c + q - 1)
                    nc.scalar.activation(RK[:, (q % 2) * CHUNK:(q % 2 + 1) * CHUNK], (FA, FB)[q % 2][:, :],
                                         ACT.Relu).then_inc(s_rk, 1)

            def expert_slot(n):
                act.wait_ge(s_xht, num(n, 2))
                if not is_int(n) or n > 1:
                    act.wait_ge(s_y_, num(n, -1))
                a = 0 if exists(n, 1) else P
                b = P + EF if exists(n, -1) else P
                nc.scalar.activation(XH[parity(n)][:, a:b], BX[:, a:b], ACT.Copy).then_inc(s_xh, 1)
                if is_int(n) and n < 0:
                    return
                if exists(n):
                    act.wait_ge(s_gu, num(n, 1))
                    if not is_int(n) or n > 0:
                        act.wait_ge(s_px, num(n))
                    nc.scalar.activation(TX[:, :], BG[:, 0:EF], ACT.Tanh, scale=0.5).then_inc(s_tx, 1)

            def step(i, scatter):
                def experts(s):
                    if not scatter and exists(tile_of(i, s), -1) and has(i, "T"):
                        expert_slot(tile_of(i, s))

                if has(i, "T"):
                    wkv_exponentials(i)
                experts(0)
                if has(i, "T"):
                    shared_tanh(i, 0)
                if has(i, "P"):
                    make_h1(i + 1)
                experts(1)
                if has(i, "T"):
                    shared_tanh(i, 1)
                if has(i, "C"):
                    make_h2(i - 1)
                experts(2)
                if has(i, "T"):
                    inverse_of_den(i)
                experts(3)
                if has(i, "C"):
                    ffn_activations(i - 1)
                experts(4)
                experts(5)

            def before_experts():
                expert_slot(-1)
                expert_slot(0)

            make_h1(0)
            drive(act, step, before_experts)

            with act.Fori(0, CHUNKS // 2) as h:
                for u in range(2):
                    c = 2 * h + u
                    act.wait_ge(s_fy, c + 1)
                    nc.scalar.activation(FT[u], FY[u], ACT.Tanh, scale=0.5).then_inc(s_ft, 1)

        @block.gpsimd
        def _(pool):
            nc.gpsimd.memset(XSS[0][:, :], 0.0).then_inc(s_pad, 1)
            pool.wait_ge(s_pad, 1)
            nc.gpsimd.memset(XSS[0][:, CH:CH + 1], NOWHERE).then_inc(s_pad, 1)
            nc.gpsimd.memset(XSS[1][:, :], 0.0).then_inc(s_init, 1)
            nc.gpsimd.memset(NH[:, :], -0.5).then_inc(s_init, 1)
            nc.gpsimd.memset(PP[:, :], NEG).then_inc(s_init, 1)
            for t in (H1, H2, AA, BB):
                last = nc.gpsimd.memset(t[:, :], 0.0)
            last.then_inc(s_init, 1)
            pool.wait_ge(s_init, 4)
            pool.wait_ge(s_fill, 16)
            nc.gpsimd.memset(XSS[0][:, CH:CH + 1], 0.0).then_inc(s_init, 1)

            def rsqrt_chain(sm, var, chain, n0, width=TPC):
                settle(pool)
                nc.gpsimd.tensor_scalar(sm[:, 0:TPC], var, EPS, None, ALU.add).then_inc(chain, 1)
                pool.wait_ge(chain, n0 + 1)
                nc.gpsimd.tensor_tensor(sm[:, TPC:2 * TPC], sm[:, 0:TPC], NH[:, :], ALU.pow).then_inc(chain, 1)

            def first(c, u, h):
                mean, var = stats(MV[u])
                pool.wait_ge(s_mv, TPC * (c + 1))
                pool.wait_ge(s_xi[u], 16 * (h + 1))
                rsqrt_chain(SM[u], var, s_sm, 5 * c)
                if not is_int(h):
                    pool.wait_ge(s_xnt, c - 1)
                nc.gpsimd.tensor_tensor(tiles(ZC[u][:, :]), tiles(XI[u][:, :]), per_tile(mean), ALU.subtract)\
                  .then_inc(s_zc, 1)
                pool.wait_ge(s_sm, 5 * c + 2)
                pool.wait_ge(s_zc, c + 1)
                r = SM[u][:, TPC:2 * TPC]
                nc.gpsimd.tensor_tensor(tiles(ZC[u][:, :]), tiles(ZC[u][:, :]), per_tile(r), ALU.mult)\
                  .then_inc(s_xns, 1)
                pool.wait_ge(s_xns, c + 1)
                nc.gpsimd.tensor_copy(chunk(XN, c), ZC[u][:, :]).then_inc(s_xn, 1)
                a, b, v = (SM[u][:, k * TPC:(k + 1) * TPC] for k in (2, 3, 4))
                nc.gpsimd.tensor_tensor(a, r, r, ALU.mult).then_inc(s_sm, 1)
                pool.wait_ge(s_sm, 5 * c + 3)
                nc.gpsimd.tensor_tensor(b, a, var, ALU.mult).then_inc(s_sm, 1)
                pool.wait_ge(s_sm, 5 * c + 4)
                settle(pool)
                nc.gpsimd.tensor_scalar(v, b, EPS, None, ALU.add).then_inc(s_sm, 1)
                pool.wait_ge(s_sm, 5 * c + 5)
                nc.gpsimd.tensor_tensor(R2[:, ds(c * TPC, TPC)], v, NH[:, :], ALU.pow).then_inc(s_r2, 1)

            first(0, 0, 0)
            first(1, 1, 0)
            with pool.Fori(1, CHUNKS // 2) as h:
                for u in range(2):
                    first(2 * h + u, u, h)

            def make_z1(c):
                pool.wait_ge(s_r2, CHUNKS)
                if not is_int(c) or c > 0:
                    pool.wait_ge(s_z1t, c)
                nc.gpsimd.tensor_tensor(tiles(Z1[:, :]), tiles(chunk(XN, c)), per_tile(chunk(R2, c, TPC)),
                                        ALU.mult).then_inc(s_z1, 1)

            def make_d1(c):
                pool.wait_ge(s_h1, c + 1)
                if not is_int(c) or c > 0:
                    pool.wait_ge(s_mix, 3 * c)
                nc.gpsimd.tensor_tensor(batches(D1[:, :]), now(H1), before(H1), ALU.subtract).then_inc(s_d1, 1)

            def make_d2(c):
                pool.wait_ge(s_h2, c + 1)
                if not is_int(c) or c > 0:
                    pool.wait_ge(s_mix2, 2 * c)
                nc.gpsimd.tensor_tensor(batches(D2[:, :]), now(H2), before(H2), ALU.subtract).then_inc(s_d2, 1)

            def make_z2(c):
                mean, var = stats(MV2)
                pool.wait_ge(s_mv2, TPC * (c + 1))
                rsqrt_chain(SM2, var, s_sm2, 2 * c)
                nc.gpsimd.tensor_tensor(tiles(ZA[:, :]), tiles(X2[:, :]), per_tile(mean), ALU.subtract)\
                  .then_inc(s_za, 1)
                pool.wait_ge(s_sm2, 2 * c + 2)
                pool.wait_ge(s_za, c + 1)
                if not is_int(c) or c > 0:
                    pool.wait_ge(s_z2t, c)
                nc.gpsimd.tensor_tensor(tiles(Z2[:, :]), tiles(ZA[:, :]), per_tile(SM2[:, TPC:2 * TPC]), ALU.mult)\
                  .then_inc(s_z2, 1)

            def wkv_sums(c):
                pool.wait_ge(s_g, 2 * c + 2)
                pool.wait_ge(s_bb, 2 * c + 2)
                if not is_int(c) or c > 0:
                    pool.wait_ge(s_lq, c)
                    pool.wait_ge(s_tn, c)
                nc.gpsimd.tensor_tensor(batches(Q1[:, :]), batches(M1[:, :]), before(BB), ALU.mult).then_inc(s_q1, 1)
                pool.wait_ge(s_q1, c + 1)
                nc.gpsimd.tensor_tensor(DEN[:, :], Q1[:, :], M2[:, :], ALU.add).then_inc(s_den, 1)
                pool.wait_ge(s_aa, 2 * c + 2)
                nc.gpsimd.tensor_tensor(batches(N1[:, :]), batches(M1[:, :]), before(AA), ALU.mult).then_inc(s_n1, 1)
                pool.wait_ge(s_n1, c + 1)
                pool.wait_ge(s_n2, c + 1)
                nc.gpsimd.tensor_tensor(NUM[:, :], N1[:, :], N2[:, :], ALU.add).then_inc(s_num, 1)

            def make_rw(c):
                pool.wait_ge(s_tn, c + 1)
                pool.wait_ge(s_iq, c + 1)
                if not is_int(c) or c > 0:
                    pool.wait_ge(s_att, c)
                nc.gpsimd.tensor_tensor(RW[:, :], NUM[:, :], LQ[:, :], ALU.mult).then_inc(s_rw, 1)

            def make_kk(c):
                for q in range(FQ):
                    pool.wait_ge(s_rk, 4 * c + q + 1)
                    if q == 0 and (not is_int(c) or c > 0):
                        pool.wait_ge(s_kv, c)
                    r = RK[:, (q % 2) * CHUNK:(q % 2 + 1) * CHUNK]
                    nc.gpsimd.tensor_tensor(KK[:, q * CHUNK:(q + 1) * CHUNK], r, r, ALU.mult).then_inc(s_kk, 1)

            def scatter_rows(i):
                for q in range(CPS):
                    u, c = q % 2, i * CPS + q
                    if q >= 2 or not is_int(i) or i > 0:
                        pool.wait_ge(s_sct[u], 16 * TPC * (i * (CPS // 2) + q // 2))
                    rows = XSS[u][:, :].rearrange("p (j c) -> p j c", j=TPC)
                    nc.gpsimd.tensor_tensor(rows[:, :, 0:CH], tiles(chunk(XN, c)), per_tile(chunk(SC, c, TPC)),
                                            ALU.mult).then_inc(s_xss, 1)
                    nc.gpsimd.tensor_copy(rows[:, :, CH], CST[:, ds(K_TOK + c * TPC, TPC)]).then_inc(s_xss, 1)
                    nc.gpsimd.tensor_copy(PIX[u][:, :], chunk(POS, c, TPC)).then_inc(s_xss, 1)
                    pool.wait_ge(s_xss, 3 * c + 3)
                    settle(pool)
                    for j in range(TPC):
                        nc.gpsimd.indirect_dma_start(
                            xs_dram, bass.IndirectOffsetOnAxis(ap=PIX[u][:, j:j + 1], axis=0),
                            XSS[u][:, j * XROW:(j + 1) * XROW], None).then_inc(s_sct[u], 16)

            def expert_slot(n):
                if exists(n, -1):
                    u = place(n, -1)
                    pool.wait_ge(s_xs[u], 16 * laps(n, -1))
                    if not is_int(n) or n > NX:
                        pool.wait_ge(s_yo[u], 16 * (laps(n, -1) - 1))
                    settle(pool)
                    nc.gpsimd.tensor_copy(YI[u][:, :], XS[u][:, CH:CH + 1]).then_inc(s_yi, 1)
                    pool.wait_ge(s_yi, num(n))
                    pool.wait_ge(s_y, num(n))
                    settle(pool)
                    nc.gpsimd.indirect_dma_start(
                        routed_dram, bass.IndirectOffsetOnAxis(ap=YI[u][:, 0:1], axis=0), YX[u][:, :], None,
                        bounds_check=TOKENS - 1, oob_is_err=False).then_inc(s_yo[u], 16)

            def step(i, scatter):
                def experts(s):
                    if not scatter and exists(tile_of(i, s), -1) and has(i, "T"):
                        expert_slot(tile_of(i, s))

                if has(i, "P"):
                    make_z1(i + 1)
                if has(i, "C"):
                    make_z2(i - 1)
                if has(i, "T"):
                    wkv_sums(i)
                experts(0)
                if has(i, "P"):
                    make_d1(i + 1)
                experts(1)
                if has(i, "C"):
                    make_d2(i - 1)
                experts(2)
                if has(i, "T"):
                    make_rw(i)
                experts(3)
                if has(i, "C"):
                    make_kk(i - 1)
                experts(4)
                experts(5)
                if scatter:
                    scatter_rows(i)

            make_z1(0)
            make_d1(0)
            pool.wait_ge(s_rt, 27)
            pool.wait_ge(s_sc, 1)
            drive(pool, step, lambda: None)

            def final(c, u, h):
                pool.wait_ge(s_fv, c + 1)
                if not is_int(h):
                    pool.wait_ge(s_out[u], 16 * h)
                nc.gpsimd.tensor_tensor(FO[u], FV[u], XI[u][:, :], ALU.add).then_inc(s_fo, 1)

            for u in range(2):
                final(u, u, 0)
            with pool.Fori(1, CHUNKS // 2) as h:
                for u in range(2):
                    final(2 * h + u, u, h)

        @block.vector
        def _(dve):
            def first(c, u, h):
                dve.wait_ge(s_xi[u], 16 * (h + 1))
                for j in range(TPC):
                    nc.vector.bn_stats(BS[u][:, j * 6:(j + 1) * 6], XI[u][:, j * P:(j + 1) * P]).then_inc(s_bn, 1)
                if not is_int(h):
                    dve.wait_ge(s_r2, c - 1)
                dve.wait_ge(s_bn, TPC * c + TPC)
                settle(dve)
                for j in range(TPC):
                    nc.vector.bn_aggr(MV[u][:, j * 2:(j + 1) * 2], BS[u][:, j * 6:(j + 1) * 6]).then_inc(s_mv, 1)

            first(0, 0, 0)
            first(1, 1, 0)
            with dve.Fori(1, CHUNKS // 2) as h:
                for u in range(2):
                    first(2 * h + u, u, h)

            done = [0]

            def link(ins):
                done[0] += 1
                ins.then_inc(s_rt, 1)
                dve.wait_ge(s_rt, done[0])

            J, E = TILES, EXPERTS
            lg = BG[:, :].rearrange("p (j e) -> p j e", e=E)
            cand = CAND[:, :].rearrange("p (j e) -> p j e", e=E)
            oh_je = OH[:, :].rearrange("p (e j) -> p j e", e=E)
            oh = OH[:, :].rearrange("p (e j) -> p e j", e=E)
            cum = CUM[:, :].rearrange("p (e j) -> p e j", e=E)
            rt = [RT[:, k * E:(k + 1) * E] for k in range(8)]
            tot, before_me, counts, tiles_of, upto, base = rt[0], rt[1], rt[2], rt[3], rt[4], rt[5]
            dve.wait_ge(s_lg, CHUNKS)
            dve.wait_ge(s_w, 16 * 3)
            link(nc.vector.tensor_reduce(MX[:, :], lg, AX.X, ALU.max))
            link(nc.vector.tensor_tensor(cand, lg, MX[:, :].unsqueeze(2).to_broadcast([P, J, E]), ALU.is_equal))
            link(nc.vector.tensor_tensor(cand, cand, CST[:, K_E8:K_E8 + E].unsqueeze(1).to_broadcast([P, J, E]),
                                         ALU.mult))
            link(nc.vector.tensor_reduce(POSF[:, :], cand, AX.X, ALU.max))
            nc.vector.tensor_tensor(oh_je, cand, POSF[:, :].unsqueeze(2).to_broadcast([P, J, E]), ALU.is_equal)\
              .then_inc(s_oh, 1)
            dve.wait_ge(s_oh, 1)
            for e in range(E):
                link(nc.vector.tensor_tensor_scan(cum[:, e, :], CST[:, K_ONE:K_ONE + J], oh[:, e, :], 0.0,
                                                  ALU.mult, ALU.add))
            link(nc.vector.tensor_copy(tot, cum[:, :, J - 1]))
            dve.wait_ge(s_rm, 1)
            link(nc.vector.tensor_copy(before_me, BX[:, 0:E]))
            link(nc.vector.tensor_copy(counts, BX[:, E:2 * E]))
            cmp = CAND[:, :].rearrange("p (e k) -> p e k", e=E)
            link(nc.vector.tensor_tensor(cmp, counts.unsqueeze(2).to_broadcast([P, E, J]),
                                         CST[:, K_CAP:K_CAP + J].unsqueeze(1).to_broadcast([P, E, J]), ALU.is_gt))
            link(nc.vector.tensor_reduce(tiles_of, cmp, AX.X, ALU.add))
            link(nc.vector.tensor_tensor_scan(upto, CST[:, K_ONE:K_ONE + E], tiles_of, 0.0, ALU.mult, ALU.add))
            link(nc.vector.tensor_tensor(base, upto, tiles_of, ALU.subtract))
            link(nc.vector.tensor_scalar(base, base, float(P), -1.0, ALU.mult, ALU.add))
            link(nc.vector.tensor_tensor(base, base, before_me, ALU.add))
            link(nc.vector.tensor_tensor(cum, cum, base.unsqueeze(2).to_broadcast([P, E, J]), ALU.add))
            link(nc.vector.tensor_tensor(cum, cum, oh, ALU.mult))
            link(nc.vector.tensor_reduce(POSF[:, :], CUM[:, :].rearrange("p (e j) -> p j e", e=E), AX.X, ALU.add))
            link(nc.vector.tensor_copy(POS[:, :], POSF[:, :]))
            X = 72
            last = CAND[0:1, 0:X * (E - 1)].rearrange("p (n e) -> p n e", e=E - 1)
            link(nc.vector.tensor_tensor(last, CST[0:1, K_TILE:K_TILE + X].unsqueeze(2).to_broadcast([1, X, E - 1]),
                                         upto[0:1, 0:E - 1].unsqueeze(1).to_broadcast([1, X, E - 1]), ALU.is_ge))
            nc.vector.tensor_reduce(MX[0:1, 0:1] if X == 1 else CUM[0:1, 0:X], last, AX.X, ALU.add).then_inc(s_oh, 1)
            dve.wait_ge(s_oh, 2)
            link(nc.vector.tensor_copy(ET[0:1, 0:X], CUM[0:1, 0:X]))

            dve.wait_ge(s_w0, 1)
            nc.vector.tensor_scalar(vec(V_W), vec(V_W), -1.0, None, ALU.mult).then_inc(s_w1, 1)
            dve.wait_ge(s_w1, 1)
            dve.wait_ge(s_init, 4)

            def time_mixes(c):
                dve.wait_ge(s_d1, c + 1)
                if not is_int(c) or c > 0:
                    dve.wait_ge(s_r, c)
                for dst, m in ((XK, V_TMK), (XV, V_TMV), (XR, V_TMR)):
                    nc.vector.scalar_tensor_tensor(batches(dst[:, :]), batches(D1[:, :]), vec(m), before(H1),
                                                   ALU.mult, ALU.add).then_inc(s_mix, 1)

            def running_max(c):
                dve.wait_ge(s_k, c + 1)
                for b in range(BPC):
                    o = b * (SEQ + 1) + 1
                    nc.vector.tensor_tensor_scan(PP[:, o:o + SEQ], vec(V_W).to_broadcast([P, SEQ]),
                                                 BK[:, b * SEQ:(b + 1) * SEQ], NEG, ALU.add, ALU.max)\
                      .then_inc(s_pp, 1)
                dve.wait_ge(s_pp, 2 * c + 2)
                if not is_int(c) or c > 0:
                    dve.wait_ge(s_bb, 2 * c)
                nc.vector.scalar_tensor_tensor(batches(E1[:, :]), before(PP), vec(V_W), now(PP),
                                               ALU.add, ALU.subtract).then_inc(s_a, 1)
                nc.vector.tensor_tensor(batches(E2[:, :]), batches(BK[:, :]), now(PP), ALU.subtract).then_inc(s_b, 1)
                if not is_int(c) or c > 0:
                    dve.wait_ge(s_m, 2 * c)
                nc.vector.scalar_tensor_tensor(batches(DD[:, :]), before(PP), vec(V_FIRST), batches(BK[:, :]),
                                               ALU.subtract, ALU.subtract).then_inc(s_d, 1)

            def wkv_states(c):
                dve.wait_ge(s_e2, c + 1)
                dve.wait_ge(s_v, c + 1)
                nc.vector.tensor_tensor(EV[:, :], E2[:, :], BV[:, :], ALU.mult).then_inc(s_ev, 1)
                dve.wait_ge(s_e1, c + 1)
                if not is_int(c) or c > 0:
                    dve.wait_ge(s_n1, c)
                for t, src, done_ in ((BB, E2, s_bb), (AA, EV, s_aa)):
                    if t is AA:
                        dve.wait_ge(s_ev, c + 1)
                    for b in range(BPC):
                        o = b * (SEQ + 1) + 1
                        nc.vector.tensor_tensor_scan(t[:, o:o + SEQ], E1[:, b * SEQ:(b + 1) * SEQ],
                                                     src[:, b * SEQ:(b + 1) * SEQ], 0.0, ALU.mult, ALU.add)\
                          .then_inc(done_, 1)
                dve.wait_ge(s_g, 2 * c + 2)
                if not is_int(c) or c > 0:
                    dve.wait_ge(s_num, c)
                nc.vector.tensor_tensor(N2[:, :], M2[:, :], BV[:, :], ALU.mult).then_inc(s_n2, 1)

            def make_tn(c):
                dve.wait_ge(s_num, c + 1)
                dve.wait_ge(s_tr, c + 1)
                nc.vector.scalar_tensor_tensor(NUM[:, :], TR[:, :], 1.0, NUM[:, :], ALU.add, ALU.mult)\
                  .then_inc(s_tn, 1)

            def make_x2(c):
                dve.wait_ge(s_att, c + 1)
                if not is_int(c) or c > 0:
                    dve.wait_ge(s_s, c)
                    dve.wait_ge(s_za, c)
                nc.vector.tensor_tensor(X2[:, :], BO[:, :], chunk(XN, c), ALU.add).then_inc(s_x2, 1)
                dve.wait_ge(s_x2, c + 1)
                for j in range(TPC):
                    nc.vector.bn_stats(BS2[:, j * 6:(j + 1) * 6], X2[:, j * P:(j + 1) * P]).then_inc(s_bn2, 1)
                dve.wait_ge(s_bn2, TPC * c + TPC)
                settle(dve)
                for j in range(TPC):
                    nc.vector.bn_aggr(MV2[:, j * 2:(j + 1) * 2], BS2[:, j * 6:(j + 1) * 6]).then_inc(s_mv2, 1)

            def channel_mixes(c):
                dve.wait_ge(s_d2, c + 1)
                if not is_int(c) or c > 0:
                    dve.wait_ge(s_fk, 4 * c)
                for dst, m in ((XR2, V_FTMR), (XK2, V_FTMK)):
                    nc.vector.scalar_tensor_tensor(batches(dst[:, :]), batches(D2[:, :]), vec(m), before(H2),
                                                   ALU.mult, ALU.add).then_inc(s_mix2, 1)

            def make_s(c):
                dve.wait_ge(s_kv, c + 1)
                dve.wait_ge(s_tf, c + 1)
                nc.vector.scalar_tensor_tensor(UU[:, :], TF[:, :], 1.0, BO[:, :], ALU.add, ALU.mult).then_inc(s_u, 1)
                dve.wait_ge(s_u, c + 1)
                dve.wait_ge(s_xss, 3 * c + 3)
                nc.vector.scalar_tensor_tensor(chunk(XN, c), UU[:, :], 0.5, X2[:, :], ALU.mult, ALU.add)\
                  .then_inc(s_s, 1)

            def shared_gated(c, q):
                dve.wait_ge(s_tg, 2 * c + q + 1)
                if not (is_int(c) and c == 0 and q == 0):
                    dve.wait_ge(s_hs, 2 * c + q)
                nc.vector.scalar_tensor_tensor(PS[:, :], TG[:, :], 1.0, FB[:, :], ALU.add, ALU.mult)\
                  .then_inc(s_ps, 1)
                dve.wait_ge(s_ps, 2 * c + q + 1)
                dve.wait_ge(s_su, 2 * c + q + 1)
                if q == 0 and (not is_int(c) or c > 0):
                    dve.wait_ge(s_sd, c)
                nc.vector.tensor_tensor(HS[:, q * CHUNK:(q + 1) * CHUNK], PS[:, :], FA[:, :], ALU.mult)\
                  .then_inc(s_hs, 1)

            def shared_out(c):
                dve.wait_ge(s_sd, c + 1)
                nc.vector.tensor_copy(chunk(XT, c), BO[:, :]).then_inc(s_sh, 1)

            def expert_slot(n):
                if exists(n):
                    dve.wait_ge(s_tx, num(n, 1))
                    nc.vector.scalar_tensor_tensor(PX[:, :], TX[:, :], 1.0, BG[:, 0:EF], ALU.add, ALU.mult)\
                      .then_inc(s_px, 1)
                    dve.wait_ge(s_px, num(n, 1))
                    if not is_int(n) or n > 0:
                        dve.wait_ge(s_xht, num(n, 2))
                    nc.vector.tensor_tensor(HX[:, :], PX[:, :], BG[:, EF:2 * EF], ALU.mult).then_inc(s_hx, 1)
                if exists(n, -1):
                    u = place(n, -1)
                    dve.wait_ge(s_y_, num(n))
                    if not is_int(n) or n > NX:
                        dve.wait_ge(s_yo[u], 16 * (laps(n, -1) - 1))
                    nc.vector.tensor_copy(YX[u][:, :], YX_).then_inc(s_y, 1)

            def step(i, scatter):
                def experts(s):
                    if not scatter and exists(tile_of(i, s), -1) and has(i, "T"):
                        expert_slot(tile_of(i, s))

                if has(i, "T"):
                    running_max(i)
                if has(i, "C"):
                    make_x2(i - 1)
                if has(i, "T"):
                    wkv_states(i)
                experts(0)
                if has(i, "T"):
                    shared_gated(i, 0)
                experts(1)
                if has(i, "P"):
                    time_mixes(i + 1)
                if has(i, "T"):
                    shared_gated(i, 1)
                experts(2)
                if has(i, "T"):
                    make_tn(i)
                    shared_out(i)
                if has(i, "C"):
                    channel_mixes(i - 1)
                experts(3)
                experts(4)
                if has(i, "C"):
                    make_s(i - 1)
                experts(5)

            time_mixes(0)
            drive(dve, step, lambda: expert_slot(0))

            dve.wait_ge(s_s, CHUNKS)
            dve.wait_ge(s_sh, CHUNKS)

            def final(c, u, h):
                dve.wait_ge(s_fx[u], 32 * (h + 1))
                nc.vector.tensor_tensor(FY[u], ZC[u][:, :], chunk(XT, c), ALU.add).then_inc(s_fy, 1)

            def final2(c, u, h):
                dve.wait_ge(s_ft, c + 1)
                nc.vector.scalar_tensor_tensor(FW[u], FT[u], 1.0, FY[u], ALU.add, ALU.mult).then_inc(s_fw, 1)
                dve.wait_ge(s_fw, c + 1)
                if not is_int(h):
                    dve.wait_ge(s_fo, c - 1)
                nc.vector.scalar_tensor_tensor(FV[u], FW[u], 0.5, chunk(XN, c), ALU.mult, ALU.mult)\
                  .then_inc(s_fv, 1)

            for u in range(2):
                final(u, u, 0)
            for u in range(2):
                final2(u, u, 0)
            with dve.Fori(1, CHUNKS // 2) as h:
                for u in range(2):
                    final(2 * h + u, u, h)
                for u in range(2):
                    final2(2 * h + u, u, h)


def constants():
    import numpy as np
    c = np.zeros((P, NCST), np.float32)
    p = np.arange(P)
    c[:, K_ID:K_ID + P] = np.eye(P)
    c[:, K_TRI:K_TRI + P] = p[:, None] < p[None, :]
    c[:, K_ONE:K_ONE + P] = 1.0
    c[:, K_E8:K_E8 + EXPERTS] = EXPERTS - np.arange(EXPERTS)
    c[:, K_CAP:K_CAP + TILES] = P * np.arange(TILES)
    c[:, K_TILE:K_TILE + 80] = np.arange(80)
    c[:, K_TOK:K_TOK + TILES] = P * np.arange(TILES)[None, :] + p[:, None]
    return c


def kernel(**inputs):
    import numpy as np
    import concourse.bacc as bacc
    from concourse.bass_utils import run_bass_kernel_spmd

    a = {k[3:]: np.asarray(v) for k, v in inputs.items()}
    vecs = np.stack([a["attn_" + k] for k in (
        "ln1_w", "ln1_b", "ln2_w", "ln2_b", "time_decay", "time_first", "tmk", "tmv", "tmr", "f_tmk", "f_tmr")], 1)
    att = np.concatenate([a["attn_" + k].T for k in ("att_kw", "att_vw", "att_rw", "att_ow", "f_rw")], 1)
    arrays = {
        "x": a["attn_x"].reshape(TOKENS, CH),
        "vecs": vecs,
        "cst": constants(),
        "att_w": att,
        "f_kw": a["attn_f_kw"].T,
        "f_vw": a["attn_f_vw"].T.reshape(FQ, P, CH).transpose(1, 0, 2).reshape(P, FQ * CH),
        "gate_w": a["ffn_gate_w"].T,
        "sh_up": np.concatenate([a["ffn_shared_gate"].T, a["ffn_shared_up"].T], 1),
        "sh_dn": a["ffn_shared_down"].T.reshape(EQ, P, CH).transpose(1, 0, 2).reshape(P, EQ * CH),
        "ex_up": np.concatenate([a["ffn_r_gate"].transpose(2, 0, 1), a["ffn_r_up"].transpose(2, 0, 1)], 2)
        .reshape(P, EXPERTS * 2 * EF),
        "ex_dn": a["ffn_r_down"].transpose(2, 0, 1).reshape(EQ, P, EXPERTS, CH).transpose(1, 2, 0, 3)
        .reshape(P, EXPERTS * EQ * CH),
    }
    arrays = {k: np.ascontiguousarray(v) for k, v in arrays.items()}
    nc = bacc.Bacc("TRN2", target_bir_lowering=False, num_devices=1)
    args = {k: nc.dram_tensor(k, v.shape, mybir.dt.from_np(v.dtype), kind="ExternalInput").ap()
            for k, v in arrays.items()}
    args["out"] = nc.dram_tensor("out", (TOKENS, CH), mybir.dt.float32, kind="ExternalOutput").ap()
    program(nc, **args)
    r = run_bass_kernel_spmd(nc, [arrays], core_ids=[0])
    return r.results[0]["out"].reshape(BATCH, SEQ, CH)
```

```python
import concourse.bass as bass
from concourse import mybir
from contextlib import ExitStack

BATCH, SEQ, CH = 32, 256, 128
TOKENS = BATCH * SEQ
P = 128
CHUNK = 512
BPC = CHUNK // SEQ
TPC = CHUNK // P
CHUNKS = TOKENS // CHUNK
TILES = TOKENS // P
FFN = 512
FQ = FFN // P
EXPERTS = 8
EF = 256
EQ = EF // P
XTILES = TILES + EXPERTS - 1
SCATTER_STEPS = 4
CPS = CHUNKS // SCATTER_STEPS
XSLOTS = 6
XROW = CH + 4
NOWHERE = 1048576.0
EPS = 1e-5
NEG = -1e38
(V_G1, V_B1, V_G2, V_B2, V_DECAY, V_FIRST, V_TMK, V_TMV, V_TMR, V_FTMK, V_FTMR, V_W) = range(12)
NVEC = 11
K_ID, K_TRI, K_ONE, K_E8, K_CAP, K_TILE, K_TOK = 0, 128, 256, 384, 392, 456, 536
NCST = K_TOK + TILES


def program(nc, x, vecs, cst, att_w, f_kw, f_vw, gate_w, sh_up, sh_dn, ex_up, ex_dn, out):
    f32, i32 = mybir.dt.float32, mybir.dt.int32
    ALU, ACT, AX = mybir.AluOpType, mybir.ActivationFunctionType, mybir.AxisListType
    ds = bass.ds

    xs_dram = nc.dram_tensor("tokens_by_expert", [XTILES * P, XROW], f32, kind="Internal").ap()
    routed_dram = nc.dram_tensor("routed_out", [TOKENS, CH], f32, kind="Internal").ap()

    ctx = ExitStack()
    with ctx:
        def sb(name, width, dt=f32):
            return ctx.enter_context(nc.sbuf_tensor(name, [P, width], dt))

        def sem(name):
            return ctx.enter_context(nc.semaphore(name))

        def bank(name):
            return ctx.enter_context(nc.psum_tensor(name, [P, CHUNK], f32))

        XN = sb("xn", TOKENS)
        XT = sb("xt", TOKENS)
        VEC = sb("vectors", 12)
        CST = sb("consts", NCST)
        ATT = sb("att", 5 * CH)
        FKW = sb("fkw", FFN)
        FVW = sb("fvw", FQ * CH)
        GW = sb("gw", EXPERTS)
        SUP = sb("sup", 2 * EF)
        SDN = sb("sdn", EQ * CH)
        EUP = sb("eup", EXPERTS * 2 * EF)
        EDN = sb("edn", EXPERTS * EQ * CH)
        R2 = sb("r2", TILES)
        POS = sb("pos", TILES, i32)
        SC = sb("score", TILES)
        ET = sb("expert_of_tile", 80, i32)
        NH = sb("minus_half", TILES)

        XI = [sb(f"xi{u}", CHUNK) for u in range(2)]
        ZC = [sb(f"zc{u}", CHUNK) for u in range(2)]
        BS = [sb(f"bs{u}", TPC * 6) for u in range(2)]
        MV = [sb(f"mv{u}", TPC * 2) for u in range(2)]
        SM = [sb(f"sm{u}", 3 * TPC) for u in range(2)]
        V2 = sb("v2", TILES)

        MX = sb("mx", TILES)
        RT = sb("rt", 8 * EXPERTS)
        POSF = sb("posf", TILES)

        XSS = [sb(f"xss{u}", TPC * XROW) for u in range(2)]
        PIX = [sb(f"pix{u}", TPC, i32) for u in range(2)]

        Z1 = sb("z1", CHUNK)
        H1 = sb("h1", BPC * (SEQ + 1))
        D1 = sb("d1", CHUNK)
        XK, XV, XR = sb("xk", CHUNK), sb("xv", CHUNK), sb("xr", CHUNK)
        PP = sb("pp", BPC * (SEQ + 1))
        AA = sb("aa", BPC * (SEQ + 1))
        BB = sb("bb", BPC * (SEQ + 1))
        E1, E2 = sb("e1", CHUNK), sb("e2", CHUNK)
        DD = sb("dd", CHUNK)
        M1, M2 = sb("m1", CHUNK), sb("m2", CHUNK)
        EV = sb("ev", CHUNK)
        N1, N2, NUM = sb("n1", CHUNK), sb("n2", CHUNK), sb("num", CHUNK)
        Q1, DEN, LQ = sb("q1", CHUNK), sb("den", CHUNK), sb("lq", CHUNK)
        TR = sb("tr", CHUNK)
        RW = sb("rw", CHUNK)

        X2 = sb("x2", CHUNK)
        BS2, MV2, SM2 = sb("bs2", TPC * 6), sb("mv2", TPC * 2), sb("sm2", 2 * TPC)
        Z2 = sb("z2", CHUNK)
        H2 = sb("h2", BPC * (SEQ + 1))
        D2, XK2, XR2 = sb("d2", CHUNK), sb("xk2", CHUNK), sb("xr2", CHUNK)
        TF = sb("tf", CHUNK)
        RK = sb("rk", 2 * CHUNK)
        KK = sb("kk", FQ * CHUNK)
        CAND, OH, CUM = (KK[:, k * TILES * EXPERTS:(k + 1) * TILES * EXPERTS] for k in range(3))
        UU = sb("uu", CHUNK)

        TG, PS, HS = sb("tg", CHUNK), sb("ps", CHUNK), sb("hs", EQ * CHUNK)
        NX = 3
        XS = [sb(f"xs{u}", XROW) for u in range(NX)]
        TX, PX, HX = sb("tx", EF), sb("px", EF), sb("hx", EF)
        XH = [sb(f"xh{u}", P + EF) for u in range(2)]
        YX = [sb(f"yx{u}", CH) for u in range(NX)]
        YI = [sb(f"yi{u}", 1, i32) for u in range(NX)]

        XTS = [XK[:, :], XV[:, :]]
        XR4 = [XI[0], XI[1], E1, E2]
        RR4 = [ZC[0], ZC[1], M1, M2]
        FO4 = [N1, N2, NUM, Q1]
        FY = [D1[:, :], D2[:, :]]
        FT = [XK[:, :], XK2[:, :]]
        FW = [XV[:, :], XR2[:, :]]
        FV = [XR[:, :], EV[:, :]]

        BK, BV = bank("bank_k"), bank("bank_v")
        FA, FB = bank("bank_fa"), bank("bank_fb")
        BT = bank("bank_transposed")
        BO = bank("bank_out")
        BG = bank("bank_gate_up")
        BX = bank("bank_expert")
        YX_ = BX[:, P + EF:P + EF + CH]

        s_w = sem("vectors_constants_router_loaded")
        s_wa = sem("attention_and_shared_weights_loaded")
        s_we = sem("expert_weights_loaded")
        s_fill = sem("xs_dram_filled")
        s_pad = sem("pad_row_made")
        s_init = sem("constants_made")
        s_half = sem("weights_halved")
        s_halfe = sem("expert_weights_halved")
        s_xi = [sem(f"x_loaded{u}") for u in range(4)]
        s_bn = sem("x_partial_stats")
        s_mv = sem("x_stats")
        s_sm = sem("x_small_chain")
        s_r2 = sem("r2_made")
        s_settled = sem("settled")
        s_w0 = sem("decay_exp")
        s_w1 = sem("decay_negated")
        s_oh = sem("routing_side_chain")
        s_rs = sem("x_rstd")
        s_v2 = sem("xn_variance")
        s_xn = sem("xn_made")
        s_xnt = sem("xn_transposed")
        s_xt = sem("xt_made")
        s_xts = sem("xt_staged")
        s_xns = sem("xn_staged")
        s_lg = sem("logits_made")
        s_rt = sem("routing_chain")
        s_rm = sem("routing_prefix_made")
        s_sc = sem("scores_made")
        s_xss = sem("scatter_rows_made")
        s_sct = [sem(f"rows_scattered{u}") for u in range(2)]

        s_z1, s_z1t, s_h1, s_d1, s_mix = sem("z1"), sem("z1_transposed"), sem("h1"), sem("d1"), sem("mixed")
        s_k, s_v, s_r = sem("k"), sem("v"), sem("r")
        s_pp, s_a, s_b, s_d = sem("running_max"), sem("a"), sem("b"), sem("d")
        s_tr, s_e1, s_e2, s_m, s_g = sem("tanh_r"), sem("e1"), sem("e2"), sem("relu_d"), sem("exp_d")
        s_ev, s_aa, s_bb, s_n2 = sem("ev"), sem("aa"), sem("bb"), sem("n2")
        s_n1, s_q1, s_num, s_den = sem("n1"), sem("q1"), sem("num"), sem("den")
        s_lq, s_iq, s_tn, s_rw = sem("ln_den"), sem("inv_den"), sem("tn"), sem("rwkv")

        s_att, s_x2, s_bn2, s_mv2 = sem("att_out"), sem("x2"), sem("x2_partial_stats"), sem("x2_stats")
        s_sm2, s_rs2, s_z2, s_z2t = sem("x2_small_chain"), sem("x2_rstd"), sem("z2"), sem("z2_transposed")
        s_h2, s_d2, s_mix2 = sem("h2"), sem("d2"), sem("mixed2")
        s_fr, s_tf, s_fk, s_rk, s_kk = sem("fr"), sem("tanh_fr"), sem("fk"), sem("relu_fk"), sem("kk")
        s_kv, s_u, s_s = sem("kv"), sem("u"), sem("s")

        s_sg, s_tg, s_ps, s_su, s_hs = sem("sh_gate"), sem("sh_tanh"), sem("sh_gated"), sem("sh_up"), sem("sh_h")
        s_sd, s_sh = sem("sh_down"), sem("sh_out")

        s_xs = [sem(f"xs_loaded{u}") for u in range(NX)]
        s_xht, s_xh = sem("x_and_h_transposed"), sem("xh_copied")
        s_gu, s_tx, s_px, s_hx = sem("gate_up"), sem("x_tanh"), sem("x_gated"), sem("x_h")
        s_y_, s_y = sem("y_psum"), sem("y")
        s_yi = sem("y_rows")
        s_yo = [sem(f"y_scattered{u}") for u in range(NX)]

        s_fx = [sem(f"final_loaded{u}") for u in range(4)]
        s_fy, s_ft, s_fw, s_fv, s_fo = (sem("final_y"), sem("final_tanh"), sem("final_silu"),
                                        sem("final_gated"), sem("final_out"))
        s_out = [sem(f"out_stored{u}") for u in range(4)]

        ident = CST[:, K_ID:K_ID + P]

        def vec(n):
            return VEC[:, n:n + 1]

        def tiles(ap):
            return ap.rearrange("p (j c) -> p j c", j=TPC)

        def batches(ap):
            return ap.rearrange("p (b t) -> p b t", b=BPC)

        def now(t):
            return t[:, :].rearrange("p (b t) -> p b t", b=BPC)[:, :, 1:SEQ + 1]

        def before(t):
            return t[:, :].rearrange("p (b t) -> p b t", b=BPC)[:, :, 0:SEQ]

        def per_tile(ap):
            return ap.unsqueeze(2).to_broadcast([P, TPC, CH])

        def chunk(t, c, w=CHUNK):
            return t[:, ds(c * w, w)]

        def stats(t):
            v = t[:, :].rearrange("p (j s) -> p s j", s=2)
            return v[:, 0, :], v[:, 1, :]

        def slot(i, s):
            return XSLOTS * (i - SCATTER_STEPS) + s + 1

        def is_int(v):
            return isinstance(v, int)

        block = ctx.enter_context(nc.Block())

        def settle(eng):
            eng.sem_inc(s_settled, 1)

        def drive(eng, step, before_experts):
            step(0, True)
            step(1, True)
            with eng.Fori(2, SCATTER_STEPS) as i:
                step(i, True)
            before_experts()
            step(SCATTER_STEPS, False)
            with eng.Fori(SCATTER_STEPS + 1, CHUNKS - 1) as i:
                step(i, False)
            step(CHUNKS - 1, False)
            step(CHUNKS, False)

        def has(i, part):
            if not is_int(i):
                return True
            return {"T": i < CHUNKS, "P": i + 1 < CHUNKS, "C": i > 0}[part]

        def tile_of(i, s):
            return slot(i, s) if is_int(i) else (i, s)

        def num(n, d=0):
            return n + d if is_int(n) else slot(n[0], n[1]) + d

        def exists(n, d=0):
            return not is_int(n) or 0 <= n + d < XTILES

        def place(n, d=0):
            return (n + d) % NX if is_int(n) else (n[1] + 1 + d) % NX

        def parity(n, d=0):
            return (n + d) % 2 if is_int(n) else (n[1] + 1 + d) % 2

        def laps(n, d=0):
            if is_int(n):
                return (n + d) // NX + 1
            return (n[0] - SCATTER_STEPS) * (XSLOTS // NX) + (n[1] + 1 + d) // NX + 1

        @block.sync
        def _(sp):
            def load_x(c, u):
                sp.dma_start(tiles(XR4[u][:, :]), x[ds(c * CHUNK, CHUNK), :].rearrange("(j p) c -> p j c", p=P))\
                  .then_inc(s_xi[u], 16)

            for u in range(4):
                load_x(u, u)
            with sp.Fori(1, CHUNKS // 4) as h:
                for u in range(4):
                    sp.wait_ge(s_xns, 4 * h + u - 3)
                    load_x(4 * h + u, u)
            sp.wait_ge(s_pad, 2)
            sp.dma_start(xs_dram.rearrange("(n p) c -> p n c", p=P),
                         XSS[0][:, 0:XROW].unsqueeze(1).to_broadcast([P, XTILES, XROW])).then_inc(s_fill, 16)

            def load_xs(n, d=0):
                u = place(n, d)
                if not is_int(n) or n + d >= NX:
                    sp.wait_ge(s_xht, num(n, d) - NX + 1)
                    sp.wait_ge(s_yi, num(n, d) - NX + 1)
                sp.dma_start(XS[u][:, :], xs_dram[ds(num(n, d) * P, P), :]).then_inc(s_xs[u], 16)

            def step(i, scatter):
                if scatter:
                    return
                for s in range(XSLOTS):
                    n = tile_of(i, s)
                    if exists(n, 2):
                        load_xs(n, 2)

            for u in range(2):
                sp.wait_ge(s_sct[u], 16 * TPC * CHUNKS // 2)
            for n in range(3):
                load_xs(n)
            step(SCATTER_STEPS, False)
            with sp.Fori(SCATTER_STEPS + 1, CHUNKS - 1) as i:
                step(i, False)
            step(CHUNKS - 1, False)

            def load_final_x(c, u):
                sp.dma_start(tiles(XR4[u][:, :]), x[ds(c * CHUNK, CHUNK), :].rearrange("(j p) c -> p j c", p=P))\
                  .then_inc(s_fx[u], 16)

            def load_final_routed(c, u):
                sp.dma_start(tiles(RR4[u][:, :]),
                             routed_dram[ds(c * CHUNK, CHUNK), :].rearrange("(j p) c -> p j c", p=P))\
                  .then_inc(s_fx[u], 16)

            def store(c, u):
                sp.wait_ge(s_fo, c + 1)
                sp.dma_start(out[ds(c * CHUNK, CHUNK), :].rearrange("(j p) c -> p j c", p=P),
                             tiles(FO4[u][:, :])).then_inc(s_out[u], 16)

            sp.wait_ge(s_rw, CHUNKS)
            for u in range(4):
                load_final_x(u, u)
            for u in range(NX):
                sp.wait_ge(s_yo[u], 16 * ((XTILES - 1 - u) // NX + 1))
            for u in range(4):
                load_final_routed(u, u)
            with sp.Fori(1, CHUNKS // 4) as h:
                for u in range(4):
                    store(4 * h + u - 4, u)
                    load_final_x(4 * h + u, u)
                    load_final_routed(4 * h + u, u)
            for u in range(4):
                store(CHUNKS - 4 + u, u)
            for u in range(4):
                sp.wait_ge(s_out[u], 16 * (CHUNKS // 4))

        @block.tensor
        def _(pe):
            pe.wait_ge(s_w, 16 * 3)

            def first(c, u, h):
                pe.wait_ge(s_xns, c + 1)
                if h is not None:
                    pe.wait_ge(s_xt, c - 1)
                b = (BT, BO)[u]
                for j in range(TPC):
                    last = nc.tensor.transpose(b[:, j * P:(j + 1) * P], ZC[u][:, j * P:(j + 1) * P], ident)
                last.then_inc(s_xnt, 1)

            def logits(c, u):
                pe.wait_ge(s_xts, c + 1)
                for j in range(TPC):
                    last = nc.tensor.matmul(BG[:, ds(c * (TPC * EXPERTS) + j * EXPERTS, EXPERTS)],
                                            XTS[u][:, j * P:(j + 1) * P], GW[:, :], start=True, stop=True)
                last.then_inc(s_lg, 1)

            first(0, 0, None)
            first(1, 1, None)
            with pe.Fori(1, CHUNKS // 2) as h:
                logits(2 * h - 2, 0)
                first(2 * h, 0, h)
                logits(2 * h - 1, 1)
                first(2 * h + 1, 1, h)
            logits(CHUNKS - 2, 0)
            logits(CHUNKS - 1, 1)

            def routing_prefix():
                pe.wait_ge(s_rt, 13)
                nc.tensor.matmul(BX[:, 0:EXPERTS], CST[:, K_TRI:K_TRI + P], RT[:, 0:EXPERTS], start=True, stop=True)
                nc.tensor.matmul(BX[:, EXPERTS:2 * EXPERTS], CST[:, K_ONE:K_ONE + P], RT[:, 0:EXPERTS],
                                 start=True, stop=True).then_inc(s_rm, 1)

            pe.wait_ge(s_wa, 16 * 5)
            pe.wait_ge(s_half, 2)

            def z1_transpose(c):
                pe.wait_ge(s_z1, c + 1)
                if not is_int(c):
                    pe.wait_ge(s_h2, c - 2)
                elif c > 2:
                    pe.wait_ge(s_h2, c - 2)
                elif c == 0:
                    pe.wait_ge(s_xt, CHUNKS)
                else:
                    pe.wait_ge(s_h1, c)
                for j in range(TPC):
                    last = nc.tensor.transpose(BT[:, j * P:(j + 1) * P], Z1[:, j * P:(j + 1) * P], ident)
                last.then_inc(s_z1t, 1)

            def key_value_receptance(c, shared):
                pe.wait_ge(s_mix, 3 * c + 3)
                if not is_int(c) or c > 0:
                    pe.wait_ge(s_d, c)
                    pe.wait_ge(s_n2, c)
                    if shared or is_int(c) and c == SCATTER_STEPS:
                        pe.wait_ge(s_hs, 2 * CPS * c)
                    else:
                        pe.wait_ge(s_rk, 4 * c - 5)
                nc.tensor.matmul(BK[:, :], ATT[:, 0:CH], XK[:, :], start=True, stop=True).then_inc(s_k, 1)
                nc.tensor.matmul(BV[:, :], ATT[:, CH:2 * CH], XV[:, :], start=True, stop=True).then_inc(s_v, 1)
                nc.tensor.matmul(FA[:, :], ATT[:, 2 * CH:3 * CH], XR[:, :], start=True, stop=True).then_inc(s_r, 1)

            def attention_out(c, shared):
                pe.wait_ge(s_rw, c + 1)
                if shared or is_int(c) and c + 1 == SCATTER_STEPS:
                    pe.wait_ge(s_sh, CPS * (c + 1))
                else:
                    pe.wait_ge(s_u, c)
                for j in range(TPC):
                    last = nc.tensor.matmul(BO[:, j * CH:(j + 1) * CH], RW[:, j * P:(j + 1) * P],
                                            ATT[:, 3 * CH:4 * CH], start=True, stop=True)
                last.then_inc(s_att, 1)

            def shared_gate_up(i, m, q):
                c = CPS * i + m
                behind_ffn = m == 2 and q == 0 and has(i, "C")
                if behind_ffn:
                    pe.wait_ge(s_rk, 4 * i)
                elif not (is_int(c) and c == 0 and q == 0):
                    pe.wait_ge(s_ps, 2 * c + q)
                rhs = chunk(XT, c)
                nc.tensor.matmul(FB[:, :], SUP[:, q * P:(q + 1) * P], rhs, start=True, stop=True).then_inc(s_sg, 1)
                if m == 0 and q == 0:
                    pe.wait_ge(s_tr, i + 1)
                elif not behind_ffn:
                    pe.wait_ge(s_hs, 2 * c + q)
                nc.tensor.matmul(FA[:, :], SUP[:, EF + q * P:EF + (q + 1) * P], rhs, start=True, stop=True)\
                  .then_inc(s_su, 1)

            def shared_down(i, m):
                c = CPS * i + m
                pe.wait_ge(s_hs, 2 * c + 2)
                if m == 0 and has(i, "C"):
                    pe.wait_ge(s_x2, i)
                elif m == 2 and has(i, "C"):
                    pe.wait_ge(s_u, i)
                elif is_int(c) and c == 0:
                    pe.wait_ge(s_xt, CHUNKS)
                else:
                    pe.wait_ge(s_sh, c)
                for j in range(TPC):
                    for q in range(EQ):
                        last = nc.tensor.matmul(BO[:, j * CH:(j + 1) * CH],
                                                HS[:, q * CHUNK + j * P:q * CHUNK + (j + 1) * P],
                                                SDN[:, q * CH:(q + 1) * CH], start=(q == 0), stop=(q == EQ - 1))
                last.then_inc(s_sd, 1)

            def z2_transpose(c):
                pe.wait_ge(s_z2, TPC * c + TPC)
                if not is_int(c):
                    pe.wait_ge(s_h1, c + 3)
                else:
                    pe.wait_ge(s_h1, min(c + 3, CHUNKS))
                for j in range(TPC):
                    last = nc.tensor.transpose(BT[:, j * P:(j + 1) * P], Z2[:, j * P:(j + 1) * P], ident)
                last.then_inc(s_z2t, 1)

            def ffn_receptance(c, shared):
                pe.wait_ge(s_mix2, 2 * c + 2)
                if shared:
                    pe.wait_ge(s_ps, 2 * CPS * (c + 1) + 4)
                elif is_int(c) and c + 1 == SCATTER_STEPS:
                    pe.wait_ge(s_ps, 2 * CHUNKS)
                else:
                    pe.wait_ge(s_rk, 4 * c)
                for j in range(TPC):
                    last = nc.tensor.matmul(FB[:, j * CH:(j + 1) * CH], XR2[:, j * P:(j + 1) * P],
                                            ATT[:, 4 * CH:5 * CH], start=True, stop=True)
                last.then_inc(s_fr, 1)

            def ffn_key(c, q, shared):
                if q == 0 and shared:
                    pe.wait_ge(s_hs, 2 * CPS * (c + 1) + 4)
                elif q == 0:
                    pe.wait_ge(s_tr, c + 2 if not is_int(c) else min(c + 2, CHUNKS))
                    if is_int(c) and c == CHUNKS - 1:
                        pe.wait_ge(s_rk, 4 * c - 1)
                elif q == 1:
                    pe.wait_ge(s_tf, c + 1)
                else:
                    pe.wait_ge(s_rk, 4 * c + q - 1)
                nc.tensor.matmul((FA, FB)[q % 2][:, :], FKW[:, q * P:(q + 1) * P], XK2[:, :],
                                 start=True, stop=True).then_inc(s_fk, 1)

            def ffn_value(c, shared):
                pe.wait_ge(s_kk, 4 * c + 4)
                if shared:
                    pe.wait_ge(s_sh, CPS * (c + 1) + 2)
                else:
                    pe.wait_ge(s_x2, c + 1)
                for j in range(TPC):
                    for q in range(FQ):
                        last = nc.tensor.matmul(BO[:, j * CH:(j + 1) * CH],
                                                KK[:, q * CHUNK + j * P:q * CHUNK + (j + 1) * P],
                                                FVW[:, q * CH:(q + 1) * CH], start=(q == 0), stop=(q == FQ - 1))
                last.then_inc(s_kv, 1)

            def expert_slot(n):
                if exists(n) and (not is_int(n) or n >= 0):
                    e_up = nc.tensor.value_load(ET[0:1, ds(num(n), 1)], min_val=0, max_val=EXPERTS - 1)
                if exists(n, -1):
                    e_dn = nc.tensor.value_load(ET[0:1, ds(num(n, -1), 1)], min_val=0, max_val=EXPERTS - 1)
                    pe.wait_ge(s_hx, num(n))
                    if not is_int(n) or n > 1:
                        pe.wait_ge(s_y, num(n, -1))
                    for q in range(EQ):
                        last = nc.tensor.transpose(BX[:, P + q * P:P + (q + 1) * P], HX[:, q * P:(q + 1) * P], ident)
                if exists(n, 1):
                    u = place(n, 1)
                    pe.wait_ge(s_xs[u], 16 * laps(n, 1))
                    if is_int(n) and n == 0:
                        pe.wait_ge(s_xh, 1)
                    last = nc.tensor.transpose(BX[:, 0:P], XS[u][:, 0:CH], ident)
                last.then_inc(s_xht, 1)
                if is_int(n) and n < 0:
                    return
                if exists(n):
                    pe.wait_ge(s_xh, num(n, 1))
                    nc.tensor.matmul(BG[:, :], XH[parity(n, 1)][:, 0:P], EUP[:, ds(e_up * (2 * EF), 2 * EF)],
                                     start=True, stop=True).then_inc(s_gu, 1)
                if exists(n, -1):
                    pe.wait_ge(s_xh, num(n, 2))
                    for q in range(EQ):
                        last = nc.tensor.matmul(YX_, XH[parity(n)][:, P + q * P:P + (q + 1) * P],
                                                EDN[:, ds(e_dn * (EQ * CH) + q * CH, CH)],
                                                start=(q == 0), stop=(q == EQ - 1))
                    last.then_inc(s_y_, 1)

            def step_one(i):
                key_value_receptance(i, True)
                if has(i, "C"):
                    attention_out(i - 1, True)
                shared_gate_up(i, 0, 0)
                z1_transpose(i + 1)
                shared_gate_up(i, 0, 1)
                if is_int(i) and i == 0:
                    routing_prefix()
                shared_down(i, 0)
                if has(i, "C"):
                    z2_transpose(i - 1)
                shared_gate_up(i, 1, 0)
                shared_gate_up(i, 1, 1)
                if has(i, "C"):
                    ffn_receptance(i - 1, True)
                    for q in range(FQ):
                        ffn_key(i - 1, q, True)
                shared_down(i, 1)
                shared_gate_up(i, 2, 0)
                shared_gate_up(i, 2, 1)
                if has(i, "C"):
                    ffn_value(i - 1, True)
                shared_down(i, 2)
                shared_gate_up(i, 3, 0)
                shared_gate_up(i, 3, 1)
                shared_down(i, 3)

            def step_two(i):
                def experts(s):
                    if exists(tile_of(i, s), -1) and has(i, "T"):
                        expert_slot(tile_of(i, s))

                if has(i, "T"):
                    key_value_receptance(i, False)
                attention_out(i - 1, False)
                experts(0)
                if has(i, "P"):
                    z1_transpose(i + 1)
                experts(1)
                z2_transpose(i - 1)
                experts(2)
                experts(3)
                ffn_receptance(i - 1, False)
                ffn_key(i - 1, 0, False)
                ffn_key(i - 1, 1, False)
                experts(4)
                ffn_key(i - 1, 2, False)
                ffn_key(i - 1, 3, False)
                experts(5)
                ffn_value(i - 1, False)

            def step(i, scatter):
                (step_one if scatter else step_two)(i)

            def before_experts():
                pe.wait_ge(s_rt, 27)
                pe.wait_ge(s_we, 16 * 2)
                pe.wait_ge(s_halfe, 1)
                expert_slot(-1)
                expert_slot(0)

            z1_transpose(0)
            drive(pe, step, before_experts)

        @block.scalar
        def _(act):
            for dst, src, s in ((VEC[:, 0:NVEC], vecs, s_w), (CST[:, :], cst, s_w), (GW[:, :], gate_w, s_w),
                                (ATT[:, :], att_w, s_wa), (SUP[:, :], sh_up, s_wa), (SDN[:, :], sh_dn, s_wa),
                                (FKW[:, :], f_kw, s_wa), (FVW[:, :], f_vw, s_wa),
                                (EUP[:, :], ex_up, s_we), (EDN[:, :], ex_dn, s_we)):
                act.dma_start(dst, src).then_inc(s, 16)
            act.wait_ge(s_w, 16 * 3)
            nc.scalar.activation(vec(V_W), vec(V_DECAY), ACT.Exp).then_inc(s_w0, 1)

            def first(c, u, h):
                act.wait_ge(s_xns, c + 1)
                nc.scalar.activation(chunk(XN, c), ZC[u][:, :], ACT.Copy).then_inc(s_xn, 1)
                act.wait_ge(s_xnt, c + 1)
                if not is_int(h):
                    act.wait_ge(s_lg, c - 1)
                nc.scalar.activation(XTS[u], (BT, BO)[u][:, :], ACT.Copy).then_inc(s_xts, 1)
                nc.scalar.activation(chunk(XT, c), (BT, BO)[u][:, :], ACT.Copy).then_inc(s_xt, 1)

            first(0, 0, 0)
            first(1, 1, 0)
            with act.Fori(1, CHUNKS // 2) as h:
                for u in range(2):
                    first(2 * h + u, u, h)
            act.wait_ge(s_wa, 16 * 5)
            for w in (SDN[:, :], ATT[:, 3 * CH:4 * CH]):
                nc.scalar.activation(w, w, ACT.Copy, scale=0.5).then_inc(s_half, 1)

            def scores():
                act.wait_ge(s_rt, 1)
                nc.scalar.activation(SC[:, :], MX[:, :], ACT.Sigmoid).then_inc(s_sc, 1)

            def make_h1(c):
                act.wait_ge(s_z1t, c + 1)
                if not is_int(c) or c > 0:
                    act.wait_ge(s_mix, 3 * c)
                nc.scalar.activation(now(H1), batches(BT[:, :]), ACT.Identity, bias=vec(V_B1),
                                     scale=vec(V_G1)).then_inc(s_h1, 1)

            def make_h2(c):
                act.wait_ge(s_z2t, c + 1)
                if not is_int(c) or c > 0:
                    act.wait_ge(s_mix2, 2 * c)
                nc.scalar.activation(now(H2), batches(BT[:, :]), ACT.Identity, bias=vec(V_B2),
                                     scale=vec(V_G2)).then_inc(s_h2, 1)

            def wkv_exponentials(c):
                act.wait_ge(s_a, c + 1)
                nc.scalar.activation(E1[:, :], E1[:, :], ACT.Exp).then_inc(s_e1, 1)
                act.wait_ge(s_b, c + 1)
                nc.scalar.activation(E2[:, :], E2[:, :], ACT.Exp).then_inc(s_e2, 1)
                act.wait_ge(s_r, c + 1)
                if not is_int(c) or c > 0:
                    act.wait_ge(s_tn, c)
                nc.scalar.activation(TR[:, :], FA[:, :], ACT.Tanh, scale=0.5).then_inc(s_tr, 1)
                act.wait_ge(s_d, c + 1)
                if not is_int(c) or c > 0:
                    act.wait_ge(s_n1, c)
                    act.wait_ge(s_den, c)
                nc.scalar.activation(M1[:, :], DD[:, :], ACT.Relu, scale=-1.0).then_inc(s_m, 1)
                nc.scalar.activation(M2[:, :], DD[:, :], ACT.Relu).then_inc(s_m, 1)
                act.wait_ge(s_m, 2 * c + 1)
                nc.scalar.activation(M1[:, :], M1[:, :], ACT.Exp, scale=-1.0).then_inc(s_g, 1)
                act.wait_ge(s_m, 2 * c + 2)
                nc.scalar.activation(M2[:, :], M2[:, :], ACT.Exp, scale=-1.0).then_inc(s_g, 1)

            def inverse_of_den(c):
                act.wait_ge(s_den, c + 1)
                if not is_int(c) or c > 0:
                    act.wait_ge(s_rw, c)
                nc.scalar.activation(LQ[:, :], DEN[:, :], ACT.Ln).then_inc(s_lq, 1)
                act.wait_ge(s_lq, c + 1)
                nc.scalar.activation(LQ[:, :], LQ[:, :], ACT.Exp, scale=-1.0).then_inc(s_iq, 1)

            def shared_tanh(c, q):
                act.wait_ge(s_sg, 2 * c + q + 1)
                if not (is_int(c) and c == 0 and q == 0):
                    act.wait_ge(s_ps, 2 * c + q)
                nc.scalar.activation(TG[:, :], FB[:, :], ACT.Tanh, scale=0.5).then_inc(s_tg, 1)

            def ffn_tanh(c):
                act.wait_ge(s_fr, c + 1)
                if not is_int(c) or c > 0:
                    act.wait_ge(s_u, c)
                nc.scalar.activation(TF[:, :], FB[:, :], ACT.Tanh, scale=0.5).then_inc(s_tf, 1)

            def ffn_squares(c, q):
                act.wait_ge(s_fk, 4 * c + q + 1)
                if not (is_int(c) and c == 0 and q < 2):
                    act.wait_ge(s_kk, 4 * c + q - 1)
                rk = RK[:, (q % 2) * CHUNK:(q % 2 + 1) * CHUNK]
                nc.scalar.activation(rk, (FA, FB)[q % 2][:, :], ACT.Relu).then_inc(s_rk, 1)
                act.wait_ge(s_rk, 4 * c + q + 1)
                if q == 0 and (not is_int(c) or c > 0):
                    act.wait_ge(s_kv, c)
                nc.scalar.activation(KK[:, q * CHUNK:(q + 1) * CHUNK], rk, ACT.Square).then_inc(s_kk, 1)

            def shared_out(c):
                act.wait_ge(s_sd, c + 1)
                nc.scalar.activation(chunk(XT, c), BO[:, :], ACT.Copy).then_inc(s_sh, 1)

            def expert_slot(n):
                act.wait_ge(s_xht, num(n, 2))
                if not is_int(n) or n > 1:
                    act.wait_ge(s_y_, num(n, -1))
                a = 0 if exists(n, 1) else P
                b = P + EF if exists(n, -1) else P
                nc.scalar.activation(XH[parity(n)][:, a:b], BX[:, a:b], ACT.Copy).then_inc(s_xh, 1)
                if is_int(n) and n < 0:
                    return
                if exists(n):
                    act.wait_ge(s_gu, num(n, 1))
                    if not is_int(n) or n > 0:
                        act.wait_ge(s_px, num(n))
                    nc.scalar.activation(TX[:, :], BG[:, 0:EF], ACT.Tanh, scale=0.5).then_inc(s_tx, 1)

            def step_one(i):
                wkv_exponentials(i)
                shared_tanh(CPS * i, 0)
                make_h1(i + 1)
                shared_tanh(CPS * i, 1)
                if is_int(i) and i == 0:
                    scores()
                shared_out(CPS * i)
                if has(i, "C"):
                    make_h2(i - 1)
                shared_tanh(CPS * i + 1, 0)
                shared_tanh(CPS * i + 1, 1)
                if has(i, "C"):
                    ffn_tanh(i - 1)
                    for q in range(FQ):
                        ffn_squares(i - 1, q)
                shared_out(CPS * i + 1)
                for m in (2, 3):
                    shared_tanh(CPS * i + m, 0)
                    shared_tanh(CPS * i + m, 1)
                    shared_out(CPS * i + m)
                inverse_of_den(i)

            def step_two(i):
                def experts(s):
                    if exists(tile_of(i, s), -1) and has(i, "T"):
                        expert_slot(tile_of(i, s))

                if has(i, "T"):
                    wkv_exponentials(i)
                experts(0)
                if has(i, "P"):
                    make_h1(i + 1)
                experts(1)
                make_h2(i - 1)
                experts(2)
                experts(3)
                ffn_tanh(i - 1)
                ffn_squares(i - 1, 0)
                ffn_squares(i - 1, 1)
                experts(4)
                ffn_squares(i - 1, 2)
                ffn_squares(i - 1, 3)
                experts(5)
                if has(i, "T"):
                    inverse_of_den(i)

            def step(i, scatter):
                (step_one if scatter else step_two)(i)

            def before_experts():
                act.wait_ge(s_we, 16 * 2)
                nc.scalar.activation(EDN[:, :], EDN[:, :], ACT.Copy, scale=0.5).then_inc(s_halfe, 1)
                expert_slot(-1)
                expert_slot(0)

            make_h1(0)
            drive(act, step, before_experts)

            with act.Fori(0, CHUNKS // 2) as h:
                for u in range(2):
                    c = 2 * h + u
                    act.wait_ge(s_fy, c + 1)
                    nc.scalar.activation(FT[u], FY[u], ACT.Tanh, scale=0.5).then_inc(s_ft, 1)

        @block.gpsimd
        def _(pool):
            nc.gpsimd.memset(XSS[0][:, :], 0.0).then_inc(s_pad, 1)
            pool.wait_ge(s_pad, 1)
            nc.gpsimd.memset(XSS[0][:, CH:CH + 1], NOWHERE).then_inc(s_pad, 1)
            nc.gpsimd.memset(XSS[1][:, :], 0.0).then_inc(s_init, 1)
            nc.gpsimd.memset(NH[:, :], -0.5).then_inc(s_init, 1)
            nc.gpsimd.memset(PP[:, :], NEG).then_inc(s_init, 1)
            for t in (H1, H2, AA, BB):
                last = nc.gpsimd.memset(t[:, :], 0.0)
            last.then_inc(s_init, 1)
            pool.wait_ge(s_init, 4)

            def first(c, u):
                mean, var = stats(MV[u])
                pool.wait_ge(s_mv, TPC * (c + 1))
                settle(pool)
                nc.gpsimd.tensor_scalar(SM[u][:, 0:TPC], var, EPS, None, ALU.add).then_inc(s_sm, 1)
                pool.wait_ge(s_sm, c + 1)
                nc.gpsimd.tensor_tensor(SM[u][:, TPC:2 * TPC], SM[u][:, 0:TPC], NH[:, 0:TPC], ALU.pow)\
                  .then_inc(s_rs, 1)

            with pool.Fori(0, CHUNKS // 2) as h:
                for u in range(2):
                    first(2 * h + u, u)
            pool.wait_ge(s_v2, 2 * CHUNKS)
            nc.gpsimd.tensor_scalar(V2[:, :], V2[:, :], EPS, None, ALU.add).then_inc(s_v2, 1)
            pool.wait_ge(s_v2, 2 * CHUNKS + 1)
            nc.gpsimd.tensor_tensor(R2[:, :], V2[:, :], NH[:, :], ALU.pow).then_inc(s_r2, 1)

            def make_z1(c):
                pool.wait_ge(s_r2, 1)
                if is_int(c) and c == 0:
                    pool.wait_ge(s_xn, CHUNKS)
                if not is_int(c) or c > 0:
                    pool.wait_ge(s_z1t, c)
                nc.gpsimd.tensor_tensor(tiles(Z1[:, :]), tiles(chunk(XN, c)), per_tile(chunk(R2, c, TPC)),
                                        ALU.mult).then_inc(s_z1, 1)

            def make_d1(c):
                pool.wait_ge(s_h1, c + 1)
                if not is_int(c) or c > 0:
                    pool.wait_ge(s_mix, 3 * c)
                nc.gpsimd.tensor_tensor(batches(D1[:, :]), now(H1), before(H1), ALU.subtract).then_inc(s_d1, 1)

            def make_d2(c):
                pool.wait_ge(s_h2, c + 1)
                if not is_int(c) or c > 0:
                    pool.wait_ge(s_mix2, 2 * c)
                nc.gpsimd.tensor_tensor(batches(D2[:, :]), now(H2), before(H2), ALU.subtract).then_inc(s_d2, 1)

            def rstd_of_x2(c):
                mean, var = stats(MV2)
                pool.wait_ge(s_mv2, TPC * (c + 1))
                settle(pool)
                nc.gpsimd.tensor_scalar(SM2[:, 0:TPC], var, EPS, None, ALU.add).then_inc(s_sm2, 1)
                pool.wait_ge(s_sm2, c + 1)
                nc.gpsimd.tensor_tensor(SM2[:, TPC:2 * TPC], SM2[:, 0:TPC], NH[:, 0:TPC], ALU.pow)\
                  .then_inc(s_rs2, 1)

            def wkv_den(c):
                pool.wait_ge(s_g, 2 * c + 2)
                pool.wait_ge(s_bb, 2 * c + 2)
                if not is_int(c) or c > 0:
                    pool.wait_ge(s_lq, c)
                nc.gpsimd.tensor_tensor(batches(Q1[:, :]), batches(M1[:, :]), before(BB), ALU.mult).then_inc(s_q1, 1)
                pool.wait_ge(s_q1, c + 1)
                nc.gpsimd.tensor_tensor(DEN[:, :], Q1[:, :], M2[:, :], ALU.add).then_inc(s_den, 1)

            def wkv_num(c):
                pool.wait_ge(s_aa, 2 * c + 2)
                nc.gpsimd.tensor_tensor(batches(N1[:, :]), batches(M1[:, :]), before(AA), ALU.mult).then_inc(s_n1, 1)
                pool.wait_ge(s_n1, c + 1)
                pool.wait_ge(s_n2, c + 1)
                nc.gpsimd.tensor_tensor(NUM[:, :], N1[:, :], N2[:, :], ALU.add).then_inc(s_num, 1)

            def make_rw(c):
                pool.wait_ge(s_tn, c + 1)
                pool.wait_ge(s_iq, c + 1)
                if not is_int(c) or c > 0:
                    pool.wait_ge(s_att, c)
                nc.gpsimd.tensor_tensor(RW[:, :], NUM[:, :], LQ[:, :], ALU.mult).then_inc(s_rw, 1)

            def scatter_rows(i, q):
                u, c = q % 2, i * CPS + q
                pool.wait_ge(s_xss, 3 * c + 3)
                settle(pool)
                for j in range(TPC):
                    nc.gpsimd.indirect_dma_start(
                        xs_dram, bass.IndirectOffsetOnAxis(ap=PIX[u][:, j:j + 1], axis=0),
                        XSS[u][:, j * XROW:(j + 1) * XROW], None).then_inc(s_sct[u], 16)

            def expert_slot(n):
                if exists(n, -1):
                    u = place(n, -1)
                    pool.wait_ge(s_xs[u], 16 * laps(n, -1))
                    if not is_int(n) or n > NX:
                        pool.wait_ge(s_yo[u], 16 * (laps(n, -1) - 1))
                    settle(pool)
                    nc.gpsimd.tensor_copy(YI[u][:, :], XS[u][:, CH:CH + 1]).then_inc(s_yi, 1)
                    pool.wait_ge(s_yi, num(n))
                    pool.wait_ge(s_y, num(n))
                    settle(pool)
                    nc.gpsimd.indirect_dma_start(
                        routed_dram, bass.IndirectOffsetOnAxis(ap=YI[u][:, 0:1], axis=0), YX[u][:, :], None,
                        bounds_check=TOKENS - 1, oob_is_err=False).then_inc(s_yo[u], 16)

            def step_one(i):
                make_z1(i + 1)
                if has(i, "C"):
                    rstd_of_x2(i - 1)
                wkv_den(i)
                if has(i, "C"):
                    make_d2(i - 1)
                wkv_num(i)
                scatter_rows(i, 0)
                make_d1(i + 1)
                for q in range(1, CPS):
                    scatter_rows(i, q)
                make_rw(i)

            def step_two(i):
                def experts(s):
                    if exists(tile_of(i, s), -1) and has(i, "T"):
                        expert_slot(tile_of(i, s))

                if has(i, "P"):
                    make_z1(i + 1)
                rstd_of_x2(i - 1)
                if has(i, "T"):
                    wkv_den(i)
                experts(0)
                make_d2(i - 1)
                experts(1)
                if has(i, "T"):
                    wkv_num(i)
                experts(2)
                if has(i, "P"):
                    make_d1(i + 1)
                experts(3)
                experts(4)
                experts(5)
                if has(i, "T"):
                    make_rw(i)

            def step(i, scatter):
                (step_one if scatter else step_two)(i)

            make_z1(0)
            pool.wait_ge(s_fill, 16)
            nc.gpsimd.memset(XSS[0][:, CH:CH + 1], 0.0).then_inc(s_init, 1)
            make_d1(0)
            drive(pool, step, lambda: None)

            def final(c, u, h):
                pool.wait_ge(s_fv, c + 1)
                if not is_int(h):
                    pool.wait_ge(s_out[u], 16 * h)
                nc.gpsimd.tensor_tensor(FO4[u][:, :], FV[u % 2], XR4[u][:, :], ALU.add).then_inc(s_fo, 1)

            for u in range(4):
                final(u, u, 0)
            with pool.Fori(1, CHUNKS // 4) as h:
                for u in range(4):
                    final(4 * h + u, u, h)

        @block.vector
        def _(dve):
            def first_stats(c, w, h):
                u = w % 2
                dve.wait_ge(s_xi[w], 16 * (h + 1))
                for j in range(TPC):
                    nc.vector.bn_stats(BS[u][:, j * 6:(j + 1) * 6], XR4[w][:, j * P:(j + 1) * P]).then_inc(s_bn, 1)
                dve.wait_ge(s_bn, TPC * c + TPC)
                settle(dve)
                for j in range(TPC):
                    nc.vector.bn_aggr(MV[u][:, j * 2:(j + 1) * 2], BS[u][:, j * 6:(j + 1) * 6]).then_inc(s_mv, 1)

            def first_xn(c, w, h):
                u = w % 2
                mean, var = stats(MV[u])
                r = SM[u][:, TPC:2 * TPC]
                dve.wait_ge(s_rs, c + 1)
                if not (is_int(h) and c < 2):
                    dve.wait_ge(s_xnt, c - 1)
                    dve.wait_ge(s_xn, c - 1)
                for j in range(TPC):
                    last = nc.vector.tensor_scalar(ZC[u][:, j * P:(j + 1) * P], XR4[w][:, j * P:(j + 1) * P],
                                                   mean[:, j:j + 1], r[:, j:j + 1], ALU.subtract, ALU.mult)
                last.then_inc(s_xns, 1)
                a = SM[u][:, 2 * TPC:3 * TPC]
                nc.vector.tensor_tensor(a, r, var, ALU.mult).then_inc(s_v2, 1)
                dve.wait_ge(s_v2, 2 * c + 1)
                nc.vector.tensor_tensor(chunk(V2, c, TPC), a, r, ALU.mult).then_inc(s_v2, 1)

            for w in range(2):
                first_stats(w, w, 0)
            for w in range(2):
                first_xn(w, w, 0)
                first_stats(w + 2, w + 2, 0)
            with dve.Fori(1, CHUNKS // 4) as h:
                for w in range(4):
                    v = (w + 2) % 4
                    first_xn(4 * h + w - 2, v, h if w >= 2 else h - 1)
                    first_stats(4 * h + w, w, h)
            for w in (2, 3):
                first_xn(CHUNKS - 4 + w, w, CHUNKS // 4 - 1)

            def routing():
                done = [0]

                def link(ins):
                    done[0] += 1
                    ins.then_inc(s_rt, 1)
                    dve.wait_ge(s_rt, done[0])

                J, E = TILES, EXPERTS
                lg = BG[:, :].rearrange("p (j e) -> p j e", e=E)
                cand = CAND[:, :].rearrange("p (j e) -> p j e", e=E)
                oh_je = OH[:, :].rearrange("p (e j) -> p j e", e=E)
                oh = OH[:, :].rearrange("p (e j) -> p e j", e=E)
                cum = CUM[:, :].rearrange("p (e j) -> p e j", e=E)
                rt = [RT[:, k * E:(k + 1) * E] for k in range(8)]
                tot, before_me, counts, tiles_of, upto, base = rt[0], rt[1], rt[2], rt[3], rt[4], rt[5]
                dve.wait_ge(s_lg, CHUNKS)
                link(nc.vector.tensor_reduce(MX[:, :], lg, AX.X, ALU.max))
                link(nc.vector.tensor_tensor(cand, lg, MX[:, :].unsqueeze(2).to_broadcast([P, J, E]), ALU.is_equal))
                link(nc.vector.tensor_tensor(cand, cand, CST[:, K_E8:K_E8 + E].unsqueeze(1).to_broadcast([P, J, E]),
                                             ALU.mult))
                link(nc.vector.tensor_reduce(POSF[:, :], cand, AX.X, ALU.max))
                nc.vector.tensor_tensor(oh_je, cand, POSF[:, :].unsqueeze(2).to_broadcast([P, J, E]), ALU.is_equal)\
                  .then_inc(s_oh, 1)
                dve.wait_ge(s_oh, 1)
                for e in range(E):
                    link(nc.vector.tensor_tensor_scan(cum[:, e, :], CST[:, K_ONE:K_ONE + J], oh[:, e, :], 0.0,
                                                      ALU.mult, ALU.add))
                link(nc.vector.tensor_copy(tot, cum[:, :, J - 1]))
                dve.wait_ge(s_rm, 1)
                link(nc.vector.tensor_copy(before_me, BX[:, 0:E]))
                link(nc.vector.tensor_copy(counts, BX[:, E:2 * E]))
                cmp = CAND[:, :].rearrange("p (e k) -> p e k", e=E)
                link(nc.vector.tensor_tensor(cmp, counts.unsqueeze(2).to_broadcast([P, E, J]),
                                             CST[:, K_CAP:K_CAP + J].unsqueeze(1).to_broadcast([P, E, J]), ALU.is_gt))
                link(nc.vector.tensor_reduce(tiles_of, cmp, AX.X, ALU.add))
                link(nc.vector.tensor_tensor_scan(upto, CST[:, K_ONE:K_ONE + E], tiles_of, 0.0, ALU.mult, ALU.add))
                link(nc.vector.tensor_tensor(base, upto, tiles_of, ALU.subtract))
                link(nc.vector.tensor_scalar(base, base, float(P), -1.0, ALU.mult, ALU.add))
                link(nc.vector.tensor_tensor(base, base, before_me, ALU.add))
                link(nc.vector.tensor_tensor(cum, cum, base.unsqueeze(2).to_broadcast([P, E, J]), ALU.add))
                link(nc.vector.tensor_tensor(cum, cum, oh, ALU.mult))
                link(nc.vector.tensor_reduce(POSF[:, :], CUM[:, :].rearrange("p (e j) -> p j e", e=E), AX.X, ALU.add))
                link(nc.vector.tensor_copy(POS[:, :], POSF[:, :]))
                X = 72
                last = CAND[0:1, 0:X * (E - 1)].rearrange("p (n e) -> p n e", e=E - 1)
                link(nc.vector.tensor_tensor(last, CST[0:1, K_TILE:K_TILE + X].unsqueeze(2).to_broadcast([1, X, E - 1]),
                                             upto[0:1, 0:E - 1].unsqueeze(1).to_broadcast([1, X, E - 1]), ALU.is_ge))
                nc.vector.tensor_reduce(MX[0:1, 0:1] if X == 1 else CUM[0:1, 0:X], last, AX.X, ALU.add).then_inc(s_oh, 1)
                dve.wait_ge(s_oh, 2)
                link(nc.vector.tensor_copy(ET[0:1, 0:X], CUM[0:1, 0:X]))

            dve.wait_ge(s_w, 16 * 3)
            dve.wait_ge(s_w0, 1)
            nc.vector.tensor_scalar(vec(V_W), vec(V_W), -1.0, None, ALU.mult).then_inc(s_w1, 1)
            dve.wait_ge(s_w1, 1)
            dve.wait_ge(s_init, 4)

            def time_mixes(c):
                dve.wait_ge(s_d1, c + 1)
                if not is_int(c) or c > 0:
                    dve.wait_ge(s_r, c)
                for dst, m in ((XK, V_TMK), (XV, V_TMV), (XR, V_TMR)):
                    nc.vector.scalar_tensor_tensor(batches(dst[:, :]), batches(D1[:, :]), vec(m), before(H1),
                                                   ALU.mult, ALU.add).then_inc(s_mix, 1)

            def running_max(c):
                dve.wait_ge(s_k, c + 1)
                for b in range(BPC):
                    o = b * (SEQ + 1) + 1
                    nc.vector.tensor_tensor_scan(PP[:, o:o + SEQ], vec(V_W).to_broadcast([P, SEQ]),
                                                 BK[:, b * SEQ:(b + 1) * SEQ], NEG, ALU.add, ALU.max)\
                      .then_inc(s_pp, 1)
                dve.wait_ge(s_pp, 2 * c + 2)
                if not is_int(c) or c > 0:
                    dve.wait_ge(s_bb, 2 * c)
                nc.vector.scalar_tensor_tensor(batches(E1[:, :]), before(PP), vec(V_W), now(PP),
                                               ALU.add, ALU.subtract).then_inc(s_a, 1)
                nc.vector.tensor_tensor(batches(E2[:, :]), batches(BK[:, :]), now(PP), ALU.subtract).then_inc(s_b, 1)
                if not is_int(c) or c > 0:
                    dve.wait_ge(s_m, 2 * c)
                nc.vector.scalar_tensor_tensor(batches(DD[:, :]), before(PP), vec(V_FIRST), batches(BK[:, :]),
                                               ALU.subtract, ALU.subtract).then_inc(s_d, 1)

            def wkv_states(c):
                dve.wait_ge(s_e2, c + 1)
                dve.wait_ge(s_v, c + 1)
                nc.vector.tensor_tensor(EV[:, :], E2[:, :], BV[:, :], ALU.mult).then_inc(s_ev, 1)
                dve.wait_ge(s_e1, c + 1)
                if not is_int(c) or c > 0:
                    dve.wait_ge(s_n1, c)
                for t, src, done_ in ((BB, E2, s_bb), (AA, EV, s_aa)):
                    if t is AA:
                        dve.wait_ge(s_ev, c + 1)
                    for b in range(BPC):
                        o = b * (SEQ + 1) + 1
                        nc.vector.tensor_tensor_scan(t[:, o:o + SEQ], E1[:, b * SEQ:(b + 1) * SEQ],
                                                     src[:, b * SEQ:(b + 1) * SEQ], 0.0, ALU.mult, ALU.add)\
                          .then_inc(done_, 1)
                dve.wait_ge(s_g, 2 * c + 2)
                if not is_int(c) or c > 0:
                    dve.wait_ge(s_num, c)
                nc.vector.tensor_tensor(N2[:, :], M2[:, :], BV[:, :], ALU.mult).then_inc(s_n2, 1)

            def make_tn(c):
                dve.wait_ge(s_num, c + 1)
                dve.wait_ge(s_tr, c + 1)
                nc.vector.scalar_tensor_tensor(NUM[:, :], TR[:, :], 1.0, NUM[:, :], ALU.add, ALU.mult)\
                  .then_inc(s_tn, 1)

            def make_x2(c):
                dve.wait_ge(s_att, c + 1)
                if not is_int(c) or c > 0:
                    dve.wait_ge(s_s, c)
                    dve.wait_ge(s_z2, TPC * c)
                nc.vector.tensor_tensor(X2[:, :], BO[:, :], chunk(XN, c), ALU.add).then_inc(s_x2, 1)
                dve.wait_ge(s_x2, c + 1)
                for j in range(TPC):
                    nc.vector.bn_stats(BS2[:, j * 6:(j + 1) * 6], X2[:, j * P:(j + 1) * P]).then_inc(s_bn2, 1)
                dve.wait_ge(s_bn2, TPC * c + TPC)
                settle(dve)
                for j in range(TPC):
                    nc.vector.bn_aggr(MV2[:, j * 2:(j + 1) * 2], BS2[:, j * 6:(j + 1) * 6]).then_inc(s_mv2, 1)

            def make_z2(c):
                mean, var = stats(MV2)
                dve.wait_ge(s_rs2, c + 1)
                if not is_int(c) or c > 0:
                    dve.wait_ge(s_z2t, c)
                for j in range(TPC):
                    nc.vector.tensor_scalar(Z2[:, j * P:(j + 1) * P], X2[:, j * P:(j + 1) * P], mean[:, j:j + 1],
                                            SM2[:, TPC + j:TPC + j + 1], ALU.subtract, ALU.mult).then_inc(s_z2, 1)

            def rows_to_scatter(i, q):
                u, c = q % 2, i * CPS + q
                if is_int(i) and i == 0 and q == 0:
                    dve.wait_ge(s_sc, 1)
                    dve.wait_ge(s_init, 5)
                if q >= 2 or not is_int(i) or i > 0:
                    dve.wait_ge(s_sct[u], 16 * TPC * (i * (CPS // 2) + q // 2))
                rows = XSS[u][:, :].rearrange("p (j c) -> p j c", j=TPC)
                nc.vector.tensor_tensor(rows[:, :, 0:CH], tiles(chunk(XN, c)), per_tile(chunk(SC, c, TPC)),
                                        ALU.mult).then_inc(s_xss, 1)
                nc.vector.tensor_copy(rows[:, :, CH], CST[:, ds(K_TOK + c * TPC, TPC)]).then_inc(s_xss, 1)
                nc.vector.tensor_copy(PIX[u][:, :], chunk(POS, c, TPC)).then_inc(s_xss, 1)

            def channel_mixes(c):
                dve.wait_ge(s_d2, c + 1)
                if not is_int(c) or c > 0:
                    dve.wait_ge(s_fk, 4 * c)
                for dst, m in ((XR2, V_FTMR), (XK2, V_FTMK)):
                    nc.vector.scalar_tensor_tensor(batches(dst[:, :]), batches(D2[:, :]), vec(m), before(H2),
                                                   ALU.mult, ALU.add).then_inc(s_mix2, 1)

            def make_s(c):
                dve.wait_ge(s_kv, c + 1)
                dve.wait_ge(s_tf, c + 1)
                nc.vector.scalar_tensor_tensor(UU[:, :], TF[:, :], 1.0, BO[:, :], ALU.add, ALU.mult).then_inc(s_u, 1)
                dve.wait_ge(s_u, c + 1)
                nc.vector.scalar_tensor_tensor(chunk(XN, c), UU[:, :], 0.5, X2[:, :], ALU.mult, ALU.add)\
                  .then_inc(s_s, 1)

            def shared_gated(c, q):
                dve.wait_ge(s_tg, 2 * c + q + 1)
                if not (is_int(c) and c == 0 and q == 0):
                    dve.wait_ge(s_hs, 2 * c + q)
                nc.vector.scalar_tensor_tensor(PS[:, :], TG[:, :], 1.0, FB[:, :], ALU.add, ALU.mult)\
                  .then_inc(s_ps, 1)
                dve.wait_ge(s_ps, 2 * c + q + 1)
                dve.wait_ge(s_su, 2 * c + q + 1)
                if q == 0 and (not is_int(c) or c > 0):
                    dve.wait_ge(s_sd, c)
                nc.vector.tensor_tensor(HS[:, q * CHUNK:(q + 1) * CHUNK], PS[:, :], FA[:, :], ALU.mult)\
                  .then_inc(s_hs, 1)

            def expert_slot(n):
                if exists(n):
                    dve.wait_ge(s_tx, num(n, 1))
                    nc.vector.scalar_tensor_tensor(PX[:, :], TX[:, :], 1.0, BG[:, 0:EF], ALU.add, ALU.mult)\
                      .then_inc(s_px, 1)
                    dve.wait_ge(s_px, num(n, 1))
                    if not is_int(n) or n > 0:
                        dve.wait_ge(s_xht, num(n, 2))
                    nc.vector.tensor_tensor(HX[:, :], PX[:, :], BG[:, EF:2 * EF], ALU.mult).then_inc(s_hx, 1)
                if exists(n, -1):
                    u = place(n, -1)
                    dve.wait_ge(s_y_, num(n))
                    if not is_int(n) or n > NX:
                        dve.wait_ge(s_yo[u], 16 * (laps(n, -1) - 1))
                    nc.vector.tensor_copy(YX[u][:, :], YX_).then_inc(s_y, 1)

            def step_one(i):
                running_max(i)
                if has(i, "C"):
                    make_x2(i - 1)
                shared_gated(CPS * i, 0)
                wkv_states(i)
                shared_gated(CPS * i, 1)
                if is_int(i) and i == 0:
                    routing()
                if has(i, "C"):
                    make_z2(i - 1)
                rows_to_scatter(i, 0)
                shared_gated(CPS * i + 1, 0)
                rows_to_scatter(i, 1)
                shared_gated(CPS * i + 1, 1)
                make_tn(i)
                if has(i, "C"):
                    channel_mixes(i - 1)
                shared_gated(CPS * i + 2, 0)
                rows_to_scatter(i, 2)
                shared_gated(CPS * i + 2, 1)
                if has(i, "C"):
                    make_s(i - 1)
                shared_gated(CPS * i + 3, 0)
                rows_to_scatter(i, 3)
                shared_gated(CPS * i + 3, 1)
                time_mixes(i + 1)

            def step_two(i):
                def experts(s):
                    if exists(tile_of(i, s), -1) and has(i, "T"):
                        expert_slot(tile_of(i, s))

                if has(i, "T"):
                    running_max(i)
                make_x2(i - 1)
                if has(i, "T"):
                    wkv_states(i)
                experts(0)
                make_z2(i - 1)
                experts(1)
                experts(2)
                experts(3)
                channel_mixes(i - 1)
                if has(i, "T"):
                    make_tn(i)
                experts(4)
                if has(i, "P"):
                    time_mixes(i + 1)
                experts(5)
                make_s(i - 1)

            def step(i, scatter):
                (step_one if scatter else step_two)(i)

            time_mixes(0)
            drive(dve, step, lambda: expert_slot(0))

            dve.wait_ge(s_s, CHUNKS)
            dve.wait_ge(s_sh, CHUNKS)

            def final(c, w, h):
                dve.wait_ge(s_fx[w], 32 * (h + 1))
                nc.vector.tensor_tensor(FY[w % 2], RR4[w][:, :], chunk(XT, c), ALU.add).then_inc(s_fy, 1)

            def final2(c, w, h):
                u = w % 2
                dve.wait_ge(s_ft, c + 1)
                nc.vector.scalar_tensor_tensor(FW[u], FT[u], 1.0, FY[u], ALU.add, ALU.mult).then_inc(s_fw, 1)
                dve.wait_ge(s_fw, c + 1)
                if not (is_int(h) and w < 2):
                    dve.wait_ge(s_fo, c - 1)
                nc.vector.scalar_tensor_tensor(FV[u], FW[u], 0.5, chunk(XN, c), ALU.mult, ALU.mult)\
                  .then_inc(s_fv, 1)

            def final_four(h):
                for w in range(4):
                    final(4 * h + w, w, h)
                    if w > 0:
                        final2(4 * h + w - 1, w - 1, h)
                final2(4 * h + 3, 3, h)

            final_four(0)
            with dve.Fori(1, CHUNKS // 4) as h:
                final_four(h)


def constants():
    import numpy as np
    c = np.zeros((P, NCST), np.float32)
    p = np.arange(P)
    c[:, K_ID:K_ID + P] = np.eye(P)
    c[:, K_TRI:K_TRI + P] = p[:, None] < p[None, :]
    c[:, K_ONE:K_ONE + P] = 1.0
    c[:, K_E8:K_E8 + EXPERTS] = EXPERTS - np.arange(EXPERTS)
    c[:, K_CAP:K_CAP + TILES] = P * np.arange(TILES)
    c[:, K_TILE:K_TILE + 80] = np.arange(80)
    c[:, K_TOK:K_TOK + TILES] = P * np.arange(TILES)[None, :] + p[:, None]
    return c


def kernel(**inputs):
    import numpy as np
    import concourse.bacc as bacc
    from concourse.bass_utils import run_bass_kernel_spmd

    a = {k[3:]: np.asarray(v) for k, v in inputs.items()}
    vecs = np.stack([a["attn_" + k] for k in (
        "ln1_w", "ln1_b", "ln2_w", "ln2_b", "time_decay", "time_first", "tmk", "tmv", "tmr", "f_tmk", "f_tmr")], 1)
    att = np.concatenate([a["attn_" + k].T for k in ("att_kw", "att_vw", "att_rw", "att_ow", "f_rw")], 1)
    arrays = {
        "x": a["attn_x"].reshape(TOKENS, CH),
        "vecs": vecs,
        "cst": constants(),
        "att_w": att,
        "f_kw": a["attn_f_kw"].T,
        "f_vw": a["attn_f_vw"].T.reshape(FQ, P, CH).transpose(1, 0, 2).reshape(P, FQ * CH),
        "gate_w": a["ffn_gate_w"].T,
        "sh_up": np.concatenate([a["ffn_shared_gate"].T, a["ffn_shared_up"].T], 1),
        "sh_dn": a["ffn_shared_down"].T.reshape(EQ, P, CH).transpose(1, 0, 2).reshape(P, EQ * CH),
        "ex_up": np.concatenate([a["ffn_r_gate"].transpose(2, 0, 1), a["ffn_r_up"].transpose(2, 0, 1)], 2)
        .reshape(P, EXPERTS * 2 * EF),
        "ex_dn": a["ffn_r_down"].transpose(2, 0, 1).reshape(EQ, P, EXPERTS, CH).transpose(1, 2, 0, 3)
        .reshape(P, EXPERTS * EQ * CH),
    }
    arrays = {k: np.ascontiguousarray(v) for k, v in arrays.items()}
    nc = bacc.Bacc("TRN2", target_bir_lowering=False, num_devices=1)
    args = {k: nc.dram_tensor(k, v.shape, mybir.dt.from_np(v.dtype), kind="ExternalInput").ap()
            for k, v in arrays.items()}
    args["out"] = nc.dram_tensor("out", (TOKENS, CH), mybir.dt.float32, kind="ExternalOutput").ap()
    program(nc, **args)
    r = run_bass_kernel_spmd(nc, [arrays], core_ids=[0])
    return r.results[0]["out"].reshape(BATCH, SEQ, CH)
```

```python
import concourse.bass as bass
from concourse import mybir
from contextlib import ExitStack

BATCH, SEQ, CH = 32, 256, 128
TOKENS = BATCH * SEQ
P = 128
CHUNK = 512
BPC = CHUNK // SEQ
TPC = CHUNK // P
CHUNKS = TOKENS // CHUNK
TILES = TOKENS // P
FFN = 512
FQ = FFN // P
EXPERTS = 8
EF = 256
EQ = EF // P
XTILES = TILES + EXPERTS - 1
SCATTER_STEPS = 4
CPS = CHUNKS // SCATTER_STEPS
XSLOTS = 6
XROW = CH + 4
NOWHERE = 1048576.0
EPS = 1e-5
NEG = -1e38
(V_G1, V_B1, V_G2, V_B2, V_DECAY, V_FIRST, V_TMK, V_TMV, V_TMR, V_FTMK, V_FTMR, V_W) = range(12)
NVEC = 11
K_ID, K_TRI, K_ONE, K_E8, K_CAP, K_TILE, K_TOK = 0, 128, 256, 384, 392, 456, 536
NCST = K_TOK + TILES


def program(nc, x, vecs, cst, att_w, f_kw, f_vw, gate_w, sh_up, sh_dn, ex_up, ex_dn, out):
    f32, i32 = mybir.dt.float32, mybir.dt.int32
    ALU, ACT, AX = mybir.AluOpType, mybir.ActivationFunctionType, mybir.AxisListType
    ds = bass.ds

    xs_dram = nc.dram_tensor("tokens_by_expert", [XTILES * P, XROW], f32, kind="Internal").ap()
    routed_dram = nc.dram_tensor("routed_out", [TOKENS, CH], f32, kind="Internal").ap()

    ctx = ExitStack()
    with ctx:
        def sb(name, width, dt=f32):
            return ctx.enter_context(nc.sbuf_tensor(name, [P, width], dt))

        def sem(name):
            return ctx.enter_context(nc.semaphore(name))

        def bank(name):
            return ctx.enter_context(nc.psum_tensor(name, [P, CHUNK], f32))

        XN = sb("xn", TOKENS)
        XT = sb("xt", TOKENS)
        VEC = sb("vectors", 12)
        CST = sb("consts", NCST)
        ATT = sb("att", 5 * CH)
        FKW = sb("fkw", FFN)
        FVW = sb("fvw", FQ * CH)
        GW = sb("gw", EXPERTS)
        SUP = sb("sup", 2 * EF)
        SDN = sb("sdn", EQ * CH)
        EUP = sb("eup", EXPERTS * 2 * EF)
        EDN = sb("edn", EXPERTS * EQ * CH)
        R2 = sb("r2", TILES)
        POS = sb("pos", TILES, i32)
        SC = sb("score", TILES)
        ET = sb("expert_of_tile", 80, i32)
        NH = sb("minus_half", TILES)

        XI = [sb(f"xi{u}", CHUNK) for u in range(2)]
        ZC = [sb(f"zc{u}", CHUNK) for u in range(2)]
        BS = [sb(f"bs{u}", TPC * 6) for u in range(2)]
        MV = [sb(f"mv{u}", TPC * 2) for u in range(4)]
        SM = [sb(f"sm{u}", 3 * TPC) for u in range(4)]
        V2 = sb("v2", TILES)

        MX = sb("mx", TILES)
        RT = sb("rt", 8 * EXPERTS)
        POSF = sb("posf", TILES)

        XSS = [sb(f"xss{u}", TPC * XROW) for u in range(2)]
        PIX = [sb(f"pix{u}", TPC, i32) for u in range(2)]

        Z1 = sb("z1", CHUNK)
        H1 = sb("h1", BPC * (SEQ + 1))
        D1 = sb("d1", CHUNK)
        XK, XV, XR = sb("xk", CHUNK), sb("xv", CHUNK), sb("xr", CHUNK)
        PP = sb("pp", BPC * (SEQ + 1))
        AA = sb("aa", BPC * (SEQ + 1))
        BB = sb("bb", BPC * (SEQ + 1))
        E1, E2 = sb("e1", CHUNK), sb("e2", CHUNK)
        DD = sb("dd", CHUNK)
        M1, M2 = sb("m1", CHUNK), sb("m2", CHUNK)
        EV = sb("ev", CHUNK)
        N1, N2, NUM = sb("n1", CHUNK), sb("n2", CHUNK), sb("num", CHUNK)
        Q1, DEN, LQ = sb("q1", CHUNK), sb("den", CHUNK), sb("lq", CHUNK)
        TR = sb("tr", CHUNK)
        RW = sb("rw", CHUNK)

        X2 = sb("x2", CHUNK)
        BS2, MV2, SM2 = sb("x2_bs", TPC * 6), sb("x2_mv", TPC * 2), sb("x2_sm", 2 * TPC)
        Z2 = sb("z2", CHUNK)
        H2 = sb("h2", BPC * (SEQ + 1))
        D2, XK2, XR2 = sb("d2", CHUNK), sb("xk2", CHUNK), sb("xr2", CHUNK)
        TF = sb("tf", CHUNK)
        RK = sb("rk", 2 * CHUNK)
        KK = sb("kk", FQ * CHUNK)
        CAND, OH, CUM = (KK[:, k * TILES * EXPERTS:(k + 1) * TILES * EXPERTS] for k in range(3))
        UU = sb("uu", CHUNK)

        TG, PS, HS = sb("tg", CHUNK), sb("ps", CHUNK), sb("hs", EQ * CHUNK)
        NX = 6
        XS = [sb(f"xs{u}", XROW)[:, :] for u in range(3)] + [XSS[0][:, u * XROW:(u + 1) * XROW] for u in range(3)]
        TX, PX = sb("tx", EF), sb("px", EF)
        HX = [sb(f"hx{u}", EF) for u in range(2)]
        NXH = 3
        XH = [sb("xh0", P + EF + CH), sb("xh1", P + EF + CH), XSS[1]]
        YI = [sb(f"yi{u}", 1, i32) for u in range(NX)]

        XTS = [EV[:, :], NUM[:, :]]
        XR4 = [XI[0], XI[1], E1, E2]
        RR4 = [ZC[0], ZC[1], M1, M2]
        FO4 = [N1, N2, NUM, Q1]
        XF1, XF2 = EUP[:, :], EDN[:, :]
        FY = [D1[:, :], AA[:, 0:CHUNK]]
        FT = [XK[:, :], BB[:, 0:CHUNK]]
        FW = [XV[:, :], PP[:, 0:CHUNK]]
        FV = [XR[:, :], EV[:, :]]

        BK, BV = bank("bank_k"), bank("bank_v")
        FA, FB = bank("bank_fa"), bank("bank_fb")
        BT = bank("bank_transposed")
        BO = bank("bank_out")
        BG = bank("bank_gate_up")
        BX = bank("bank_expert")
        SHG, SHU = (FB, BT), (FA, BX)
        BGU = (BG, BT)

        s_w = sem("vectors_constants_router_loaded")
        s_wa = sem("attention_and_shared_weights_loaded")
        s_we = sem("expert_weights_loaded")
        s_fill = sem("xs_dram_filled")
        s_pad = sem("pad_row_made")
        s_init = sem("constants_made")
        s_half = sem("weights_halved")
        s_halfe = sem("expert_weights_halved")
        s_xi = [sem(f"x_loaded{u}") for u in range(4)]
        s_bn = sem("x_partial_stats")
        s_mv = sem("x_stats")
        s_sm = sem("x_small_chain")
        s_r2 = sem("r2_made")
        s_r2a = sem("r2_of_two_chunks_made")
        s_settled = sem("settled")
        s_w0 = sem("decay_exp")
        s_w1 = sem("decay_negated")
        s_oh = sem("routing_side_chain")
        s_rs = sem("x_rstd")
        s_v2 = sem("xn_variance")
        s_xn = sem("xn_made")
        s_xnt = sem("xn_transposed")
        s_xt = sem("xt_made")
        s_xts = sem("xt_staged")
        s_xns = sem("xn_staged")
        s_lg = sem("logits_made")
        s_rt = sem("routing_chain")
        s_rm = sem("routing_prefix_made")
        s_sc = sem("scores_made")
        s_xss = sem("scatter_rows_made")
        s_sct = [sem(f"rows_scattered{u}") for u in range(2)]

        s_z1, s_z1t, s_h1, s_d1, s_mix = sem("z1"), sem("z1_transposed"), sem("h1"), sem("d1"), sem("mixed")
        s_k, s_v, s_r = sem("k"), sem("v"), sem("r")
        s_pp, s_a, s_b, s_d = sem("running_max"), sem("a"), sem("b"), sem("d")
        s_tr, s_e1, s_e2, s_m, s_g = sem("tanh_r"), sem("e1"), sem("e2"), sem("relu_d"), sem("exp_d")
        s_ev, s_aa, s_bb, s_n2 = sem("ev"), sem("aa"), sem("bb"), sem("n2")
        s_n1, s_q1, s_num, s_den = sem("n1"), sem("q1"), sem("num"), sem("den")
        s_lq, s_iq, s_tn, s_rw = sem("ln_den"), sem("inv_den"), sem("tn"), sem("rwkv")

        s_att, s_x2, s_bn2, s_mv2 = sem("att_out"), sem("x2"), sem("x2_partial_stats"), sem("x2_stats")
        s_sm2, s_rs2, s_z2, s_z2t = sem("x2_small_chain"), sem("x2_rstd"), sem("z2"), sem("z2_transposed")
        s_h2, s_d2, s_mix2 = sem("h2"), sem("d2"), sem("mixed2")
        s_fr, s_tf, s_fk, s_rk, s_kk = sem("fr"), sem("tanh_fr"), sem("fk"), sem("relu_fk"), sem("kk")
        s_kv, s_u, s_s = sem("kv"), sem("u"), sem("s")

        s_sg, s_tg, s_ps, s_su, s_hs = sem("sh_gate"), sem("sh_tanh"), sem("sh_gated"), sem("sh_up"), sem("sh_h")
        s_sd, s_sh = sem("sh_down"), sem("sh_out")

        s_xs = [sem(f"xs_loaded{u}") for u in range(NX)]
        s_xht, s_xh = sem("x_and_h_transposed"), sem("xh_copied")
        s_gu, s_tx, s_px, s_hx = sem("gate_up"), sem("x_tanh"), sem("x_gated"), sem("x_h")
        s_yi = sem("y_rows")
        s_yo = [sem(f"y_scattered{u}") for u in range(NXH)]

        s_fx = [sem(f"final_loaded{u}") for u in range(4)]
        s_xf = sem("final_x_loaded")
        s_fy, s_ft, s_fw, s_fv, s_fo = (sem("final_y"), sem("final_tanh"), sem("final_silu"),
                                        sem("final_gated"), sem("final_out"))
        s_out = [sem(f"out_stored{u}") for u in range(4)]

        ident = CST[:, K_ID:K_ID + P]

        def vec(n):
            return VEC[:, n:n + 1]

        def tiles(ap):
            return ap.rearrange("p (j c) -> p j c", j=TPC)

        def batches(ap):
            return ap.rearrange("p (b t) -> p b t", b=BPC)

        def now(t):
            return t[:, :].rearrange("p (b t) -> p b t", b=BPC)[:, :, 1:SEQ + 1]

        def before(t):
            return t[:, :].rearrange("p (b t) -> p b t", b=BPC)[:, :, 0:SEQ]

        def per_tile(ap):
            return ap.unsqueeze(2).to_broadcast([P, TPC, CH])

        def chunk(t, c, w=CHUNK):
            return t[:, ds(c * w, w)]

        def stats(t):
            v = t[:, :].rearrange("p (j s) -> p s j", s=2)
            return v[:, 0, :], v[:, 1, :]

        def slot(i, s):
            return XSLOTS * (i - SCATTER_STEPS) + s + 1

        def is_int(v):
            return isinstance(v, int)

        block = ctx.enter_context(nc.Block())

        def settle(eng):
            eng.sem_inc(s_settled, 1)

        def drive(eng, step, before_experts):
            step(0, True)
            step(1, True)
            with eng.Fori(2, SCATTER_STEPS) as i:
                step(i, True)
            before_experts()
            step(SCATTER_STEPS, False)
            step(SCATTER_STEPS + 1, False)
            with eng.Fori(SCATTER_STEPS + 2, CHUNKS - 1) as i:
                step(i, False)
            step(CHUNKS - 1, False)
            step(CHUNKS, False)

        def has(i, part):
            if not is_int(i):
                return True
            return {"T": i < CHUNKS, "P": i + 1 < CHUNKS, "C": i > 0}[part]

        def tile_of(i, s):
            return slot(i, s) if is_int(i) else (i, s)

        def slots(expert_slot, i, s):
            n = tile_of(i, s)
            if exists(n, -3) or exists(n):
                expert_slot(n)

        def num(n, d=0):
            return n + d if is_int(n) else slot(n[0], n[1]) + d

        def exists(n, d=0):
            return not is_int(n) or 0 <= n + d < XTILES

        def place(n, d=0):
            return (n + d) % NX if is_int(n) else (n[1] + 1 + d) % NX

        def parity(n, d=0):
            return (n + d) % 2 if is_int(n) else (n[1] + 1 + d) % 2

        def third(n, d=0):
            return (n + d) % NXH if is_int(n) else (n[1] + 1 + d) % NXH

        def y_sent(n):
            laps = n // NXH if is_int(n) else (n[0] - SCATTER_STEPS) * (XSLOTS // NXH) + (n[1] + 1) // NXH
            return 16 * (laps - 1)

        def laps(n, d=0):
            if is_int(n):
                return (n + d) // NX + 1
            return (n[0] - SCATTER_STEPS) * (XSLOTS // NX) + (n[1] + 1 + d) // NX + 1

        @block.sync
        def _(sp):
            def load_x(c, u):
                sp.dma_start(tiles(XR4[u][:, :]), x[ds(c * CHUNK, CHUNK), :].rearrange("(j p) c -> p j c", p=P))\
                  .then_inc(s_xi[u], 16)

            for u in range(4):
                load_x(u, u)
            with sp.Fori(1, CHUNKS // 4) as h:
                for u in range(4):
                    sp.wait_ge(s_xns, 4 * h + u - 3)
                    load_x(4 * h + u, u)
            sp.wait_ge(s_pad, 2)
            sp.dma_start(xs_dram.rearrange("(n p) c -> p n c", p=P),
                         XSS[0][:, 0:XROW].unsqueeze(1).to_broadcast([P, XTILES, XROW])).then_inc(s_fill, 16)
            for dst, src in ((EUP[:, :], ex_up), (EDN[:, :], ex_dn)):
                sp.dma_start(dst, src).then_inc(s_we, 16)

            def load_xs(n, d=0):
                u = place(n, d)
                if not is_int(n) or n + d >= NX:
                    sp.wait_ge(s_xht, num(n, d) - NX + 1)
                    sp.wait_ge(s_yi, num(n, d) - NX + 1)
                sp.dma_start(XS[u], xs_dram[ds(num(n, d) * P, P), :]).then_inc(s_xs[u], 16)

            def step(i, scatter):
                if scatter:
                    return
                for s in range(XSLOTS):
                    n = tile_of(i, s)
                    if exists(n, 4):
                        load_xs(n, 4)

            for u in range(2):
                sp.wait_ge(s_sct[u], 16 * TPC * CHUNKS // 2)
            for n in range(5):
                load_xs(n)
            step(SCATTER_STEPS, False)
            step(SCATTER_STEPS + 1, False)
            with sp.Fori(SCATTER_STEPS + 2, CHUNKS - 1) as i:
                step(i, False)
            step(CHUNKS - 1, False)

            def load_final_x(c, u):
                sp.dma_start(tiles(XR4[u][:, :]), x[ds(c * CHUNK, CHUNK), :].rearrange("(j p) c -> p j c", p=P))\
                  .then_inc(s_fx[u], 16)

            def load_final_routed(c, u):
                sp.dma_start(tiles(RR4[u][:, :]),
                             routed_dram[ds(c * CHUNK, CHUNK), :].rearrange("(j p) c -> p j c", p=P))\
                  .then_inc(s_fx[u], 16)

            def store(c, u):
                sp.wait_ge(s_fo, c + 1)
                sp.dma_start(out[ds(c * CHUNK, CHUNK), :].rearrange("(j p) c -> p j c", p=P),
                             tiles(FO4[u][:, :])).then_inc(s_out[u], 16)

            sp.wait_ge(s_rw, CHUNKS)
            for u in range(4):
                load_final_x(u, u)
            sp.wait_ge(s_gu, XTILES)
            sp.dma_start(XF1.rearrange("p (t c) -> p t c", c=CH),
                         x[4 * CHUNK:12 * CHUNK, :].rearrange("(t p) c -> p t c", p=P)).then_inc(s_xf, 16)
            for u in range(NXH):
                sp.wait_ge(s_yo[u], 16 * ((XTILES - 1 - u) // NXH + 1))
            for u in range(4):
                load_final_routed(u, u)
            sp.wait_ge(s_xht, XTILES + 4)
            sp.dma_start(XF2.rearrange("p (t c) -> p t c", c=CH),
                         x[12 * CHUNK:16 * CHUNK, :].rearrange("(t p) c -> p t c", p=P)).then_inc(s_xf, 16)
            with sp.Fori(1, CHUNKS // 4) as h:
                for u in range(4):
                    sp.wait_ge(s_fy, 4 * h + u - 3)
                    load_final_routed(4 * h + u, u)
                    store(4 * h + u - 4, u)
            for u in range(4):
                store(CHUNKS - 4 + u, u)
            for u in range(4):
                sp.wait_ge(s_out[u], 16 * (CHUNKS // 4))

        @block.tensor
        def _(pe):
            pe.wait_ge(s_w, 16 * 3)

            def first(c, u, h):
                pe.wait_ge(s_xns, c + 1)
                if h is not None:
                    pe.wait_ge(s_xt, c - 1)
                b = (BT, BO)[u]
                for j in range(TPC):
                    last = nc.tensor.transpose(b[:, j * P:(j + 1) * P], ZC[u][:, j * P:(j + 1) * P], ident)
                last.then_inc(s_xnt, 1)

            def logits(c, u):
                pe.wait_ge(s_xts, c + 1)
                for j in range(TPC):
                    last = nc.tensor.matmul(BG[:, ds(c * (TPC * EXPERTS) + j * EXPERTS, EXPERTS)],
                                            XTS[u][:, j * P:(j + 1) * P], GW[:, :], start=True, stop=True)
                last.then_inc(s_lg, 1)

            first(0, 0, None)
            first(1, 1, None)
            with pe.Fori(1, CHUNKS // 2) as h:
                logits(2 * h - 2, 0)
                first(2 * h, 0, h)
                logits(2 * h - 1, 1)
                first(2 * h + 1, 1, h)

            def routing_prefix():
                pe.wait_ge(s_rt, 13)
                nc.tensor.matmul(BG[:, 0:EXPERTS], CST[:, K_TRI:K_TRI + P], RT[:, 0:EXPERTS], start=True, stop=True)
                nc.tensor.matmul(BG[:, EXPERTS:2 * EXPERTS], CST[:, K_ONE:K_ONE + P], RT[:, 0:EXPERTS],
                                 start=True, stop=True).then_inc(s_rm, 1)

            def z1_transpose(c):
                pe.wait_ge(s_z1, c + 1)
                if not is_int(c) or c > 0:
                    pe.wait_ge(s_d, c)
                for j in range(TPC):
                    last = nc.tensor.transpose(BK[:, j * P:(j + 1) * P], Z1[:, j * P:(j + 1) * P], ident)
                last.then_inc(s_z1t, 1)

            def key_value_receptance(c, shared):
                pe.wait_ge(s_mix, 3 * c + 1)
                if not is_int(c) or c > 0:
                    pe.wait_ge(s_n2, c)
                    if not is_int(c) or c > 1:
                        pe.wait_ge(s_h2, c - 1)
                    if shared:
                        pe.wait_ge(s_hs, 2 * CPS * c - 1)
                    else:
                        pe.wait_ge(s_rk, 4 * c - 5)
                nc.tensor.matmul(BK[:, :], ATT[:, 0:CH], XK[:, :], start=True, stop=True).then_inc(s_k, 1)
                pe.wait_ge(s_mix, 3 * c + 2)
                nc.tensor.matmul(BV[:, :], ATT[:, CH:2 * CH], XV[:, :], start=True, stop=True).then_inc(s_v, 1)
                pe.wait_ge(s_mix, 3 * c + 3)
                nc.tensor.matmul(FA[:, :], ATT[:, 2 * CH:3 * CH], XR[:, :], start=True, stop=True).then_inc(s_r, 1)

            def attention_out(c, shared):
                pe.wait_ge(s_rw, c + 1)
                if shared or is_int(c) and c + 1 == SCATTER_STEPS:
                    pe.wait_ge(s_sh, CPS * (c + 1))
                else:
                    pe.wait_ge(s_u, c)
                for j in range(TPC):
                    last = nc.tensor.matmul(BO[:, j * CH:(j + 1) * CH], RW[:, j * P:(j + 1) * P],
                                            ATT[:, 3 * CH:4 * CH], start=True, stop=True)
                last.then_inc(s_att, 1)

            def shared_gate_up(i, m, q):
                c = CPS * i + m
                behind_ffn = m == 3 and q == 0 and has(i, "C")
                if behind_ffn:
                    pe.wait_ge(s_rk, 4 * i)
                elif not is_int(c) or c > 0:
                    pe.wait_ge(s_ps, 2 * c + q - 1)
                elif q == 1:
                    pe.wait_ge(s_xt, CHUNKS)
                rhs = chunk(XT, c)
                nc.tensor.matmul(SHG[q][:, :], SUP[:, q * P:(q + 1) * P], rhs, start=True, stop=True)\
                  .then_inc(s_sg, 1)
                if m == 0 and q == 0:
                    pe.wait_ge(s_tr, i + 1)
                elif not behind_ffn and (not is_int(c) or c > 0):
                    pe.wait_ge(s_hs, 2 * c + q - 1)
                nc.tensor.matmul(SHU[q][:, :], SUP[:, EF + q * P:EF + (q + 1) * P], rhs, start=True, stop=True)\
                  .then_inc(s_su, 1)

            def shared_down(i, m):
                c = CPS * i + m
                pe.wait_ge(s_hs, 2 * c + 2)
                if m == 0 and has(i, "C"):
                    pe.wait_ge(s_x2, i)
                elif m == 3 and has(i, "C"):
                    pe.wait_ge(s_u, i)
                elif is_int(c) and c == 0:
                    pe.wait_ge(s_xt, CHUNKS)
                else:
                    pe.wait_ge(s_sh, c)
                for j in range(TPC):
                    for q in range(EQ):
                        last = nc.tensor.matmul(BO[:, j * CH:(j + 1) * CH],
                                                HS[:, q * CHUNK + j * P:q * CHUNK + (j + 1) * P],
                                                SDN[:, q * CH:(q + 1) * CH], start=(q == 0), stop=(q == EQ - 1))
                last.then_inc(s_sd, 1)

            def z2_transpose(c):
                pe.wait_ge(s_z2, TPC * c + TPC)
                pe.wait_ge(s_n2, c + 2 if not is_int(c) else min(c + 2, CHUNKS))
                if is_int(c) and c == CHUNKS - 1:
                    pe.wait_ge(s_h2, c)
                for j in range(TPC):
                    last = nc.tensor.transpose(BV[:, j * P:(j + 1) * P], Z2[:, j * P:(j + 1) * P], ident)
                last.then_inc(s_z2t, 1)

            def ffn_receptance(c, shared):
                pe.wait_ge(s_mix2, 2 * c + 1)
                if shared:
                    pe.wait_ge(s_ps, 2 * CPS * (c + 1) + 5)
                elif is_int(c) and c + 1 == SCATTER_STEPS:
                    pe.wait_ge(s_ps, 2 * CHUNKS)
                else:
                    pe.wait_ge(s_rk, 4 * c)
                for j in range(TPC):
                    last = nc.tensor.matmul(FB[:, j * CH:(j + 1) * CH], XR2[:, j * P:(j + 1) * P],
                                            ATT[:, 4 * CH:5 * CH], start=True, stop=True)
                last.then_inc(s_fr, 1)

            def ffn_key(c, q, shared):
                if q == 0:
                    pe.wait_ge(s_mix2, 2 * c + 2)
                if q == 0 and shared:
                    pe.wait_ge(s_hs, 2 * CPS * (c + 1) + 5)
                elif q == 0:
                    pe.wait_ge(s_tr, c + 2 if not is_int(c) else min(c + 2, CHUNKS))
                    if is_int(c) and c == CHUNKS - 1:
                        pe.wait_ge(s_rk, 4 * c - 1)
                elif q == 1:
                    pe.wait_ge(s_tf, c + 1)
                else:
                    pe.wait_ge(s_rk, 4 * c + q - 1)
                nc.tensor.matmul((FA, FB)[q % 2][:, :], FKW[:, q * P:(q + 1) * P], XK2[:, :],
                                 start=True, stop=True).then_inc(s_fk, 1)

            def ffn_value(c, shared):
                pe.wait_ge(s_kk, 4 * c + 4)
                if shared:
                    pe.wait_ge(s_sh, CPS * (c + 1) + 3)
                else:
                    pe.wait_ge(s_x2, c + 1)
                for j in range(TPC):
                    for q in range(FQ):
                        last = nc.tensor.matmul(BO[:, j * CH:(j + 1) * CH],
                                                KK[:, q * CHUNK + j * P:q * CHUNK + (j + 1) * P],
                                                FVW[:, q * CH:(q + 1) * CH], start=(q == 0), stop=(q == FQ - 1))
                last.then_inc(s_kv, 1)

            def expert_slot(n):
                if exists(n):
                    e_up = nc.tensor.value_load(ET[0:1, ds(num(n), 1)], min_val=0, max_val=EXPERTS - 1)
                if exists(n, -3):
                    e_dn = nc.tensor.value_load(ET[0:1, ds(num(n, -3), 1)], min_val=0, max_val=EXPERTS - 1)
                if not is_int(n) or n >= 0:
                    pe.wait_ge(s_xh, num(n, 1))
                xh = XH[third(n, -1)]
                if exists(n, -3):
                    for q in range(EQ):
                        last = nc.tensor.matmul(BX[:, P + EF:P + EF + CH], xh[:, P + q * P:P + (q + 1) * P],
                                                EDN[:, ds(e_dn * (EQ * CH) + q * CH, CH)],
                                                start=(q == 0), stop=(q == EQ - 1))
                if exists(n, -2):
                    pe.wait_ge(s_hx, num(n, -1))
                    h = HX[parity(n)]
                    for q in range(EQ):
                        last = nc.tensor.transpose(BX[:, P + q * P:P + (q + 1) * P], h[:, q * P:(q + 1) * P], ident)
                if exists(n, 1):
                    u = place(n, 1)
                    pe.wait_ge(s_xs[u], 16 * laps(n, 1))
                    last = nc.tensor.transpose(BX[:, 0:P], XS[u][:, 0:CH], ident)
                last.then_inc(s_xht, 1)
                if exists(n):
                    if is_int(n) and n == 1:
                        pe.wait_ge(s_ps, 2 * CHUNKS)
                    nc.tensor.matmul(BGU[parity(n)][:, :], xh[:, 0:P],
                                     EUP[:, ds(e_up * (2 * EF), 2 * EF)], start=True, stop=True).then_inc(s_gu, 1)

            def step_zero(i):
                shared_gate_up(i, 0, 0)
                z1_transpose(i + 1)
                shared_gate_up(i, 0, 1)
                shared_gate_up(i, 1, 0)
                shared_down(i, 0)
                shared_gate_up(i, 1, 1)
                shared_gate_up(i, 2, 0)
                shared_down(i, 1)
                shared_gate_up(i, 2, 1)
                shared_gate_up(i, 3, 0)
                shared_down(i, 2)
                shared_gate_up(i, 3, 1)
                key_value_receptance(i + 1, True)
                shared_down(i, 3)

            def step_one(i):
                C = has(i, "C")
                shared_gate_up(i, 0, 0)
                if C:
                    attention_out(i - 1, True)
                z1_transpose(i + 1)
                shared_gate_up(i, 0, 1)
                shared_gate_up(i, 1, 0)
                if C:
                    z2_transpose(i - 1)
                shared_gate_up(i, 1, 1)
                shared_down(i, 0)
                shared_gate_up(i, 2, 0)
                shared_down(i, 1)
                shared_gate_up(i, 2, 1)
                if C:
                    ffn_receptance(i - 1, True)
                    ffn_key(i - 1, 0, True)
                    ffn_key(i - 1, 1, True)
                shared_down(i, 2)
                if C:
                    ffn_key(i - 1, 2, True)
                    ffn_key(i - 1, 3, True)
                shared_gate_up(i, 3, 0)
                if C:
                    ffn_value(i - 1, True)
                shared_gate_up(i, 3, 1)
                key_value_receptance(i + 1, True)
                shared_down(i, 3)

            def step_two(i):
                attention_out(i - 1, False)
                slots(expert_slot, i, 0)
                if has(i, "P"):
                    z1_transpose(i + 1)
                slots(expert_slot, i, 1)
                slots(expert_slot, i, 2)
                z2_transpose(i - 1)
                slots(expert_slot, i, 3)
                ffn_receptance(i - 1, False)
                ffn_key(i - 1, 0, False)
                slots(expert_slot, i, 4)
                ffn_key(i - 1, 1, False)
                ffn_key(i - 1, 2, False)
                slots(expert_slot, i, 5)
                ffn_key(i - 1, 3, False)
                if has(i, "P"):
                    key_value_receptance(i + 1, False)
                ffn_value(i - 1, False)

            def step(i, scatter):
                (step_zero if is_int(i) and i == 0 else step_one if scatter else step_two)(i)

            def before_experts():
                pe.wait_ge(s_rt, 27)
                pe.wait_ge(s_hs, 2 * CHUNKS)
                pe.wait_ge(s_we, 16 * 2)
                pe.wait_ge(s_halfe, 1)
                expert_slot(-1)
                expert_slot(0)

            z1_transpose(0)
            logits(CHUNKS - 2, 0)
            logits(CHUNKS - 1, 1)
            pe.wait_ge(s_wa, 16 * 5)
            pe.wait_ge(s_half, 2)
            key_value_receptance(0, True)
            routing_prefix()
            drive(pe, step, before_experts)

        @block.scalar
        def _(act):
            for dst, src, s in ((VEC[:, 0:NVEC], vecs, s_w), (CST[:, :], cst, s_w), (GW[:, :], gate_w, s_w),
                                (ATT[:, :], att_w, s_wa), (SUP[:, :], sh_up, s_wa), (SDN[:, :], sh_dn, s_wa),
                                (FKW[:, :], f_kw, s_wa), (FVW[:, :], f_vw, s_wa)):
                act.dma_start(dst, src).then_inc(s, 16)
            act.wait_ge(s_w, 16 * 3)
            nc.scalar.activation(vec(V_W), vec(V_DECAY), ACT.Exp).then_inc(s_w0, 1)

            def first(c, u, h):
                act.wait_ge(s_xns, c + 1)
                nc.scalar.activation(chunk(XN, c), ZC[u][:, :], ACT.Copy).then_inc(s_xn, 1)
                act.wait_ge(s_xnt, c + 1)
                if not is_int(h):
                    act.wait_ge(s_lg, c - 1)
                nc.scalar.activation(XTS[u], (BT, BO)[u][:, :], ACT.Copy).then_inc(s_xts, 1)
                nc.scalar.activation(chunk(XT, c), (BT, BO)[u][:, :], ACT.Copy).then_inc(s_xt, 1)

            first(0, 0, 0)
            first(1, 1, 0)
            with act.Fori(1, CHUNKS // 2) as h:
                for u in range(2):
                    first(2 * h + u, u, h)
            act.wait_ge(s_wa, 16 * 5)
            for w in (SDN[:, :], ATT[:, 3 * CH:4 * CH]):
                nc.scalar.activation(w, w, ACT.Copy, scale=0.5).then_inc(s_half, 1)

            def scores():
                act.wait_ge(s_rt, 1)
                nc.scalar.activation(SC[:, :], MX[:, :], ACT.Sigmoid).then_inc(s_sc, 1)

            def make_h1(c):
                act.wait_ge(s_z1t, c + 1)
                if not is_int(c) or c > 0:
                    act.wait_ge(s_mix, 3 * c)
                nc.scalar.activation(now(H1), batches(BK[:, :]), ACT.Identity, bias=vec(V_B1),
                                     scale=vec(V_G1)).then_inc(s_h1, 1)

            def make_h2(c):
                act.wait_ge(s_z2t, c + 1)
                if not is_int(c) or c > 0:
                    act.wait_ge(s_mix2, 2 * c)
                nc.scalar.activation(now(H2), batches(BV[:, :]), ACT.Identity, bias=vec(V_B2),
                                     scale=vec(V_G2)).then_inc(s_h2, 1)

            def wkv_exponentials(c):
                act.wait_ge(s_r, c + 1)
                if not is_int(c) or c > 0:
                    act.wait_ge(s_tn, c)
                nc.scalar.activation(TR[:, :], FA[:, :], ACT.Tanh, scale=0.5).then_inc(s_tr, 1)
                act.wait_ge(s_a, c + 1)
                nc.scalar.activation(E1[:, :], E1[:, :], ACT.Exp).then_inc(s_e1, 1)
                act.wait_ge(s_b, c + 1)
                nc.scalar.activation(E2[:, :], E2[:, :], ACT.Exp).then_inc(s_e2, 1)
                act.wait_ge(s_d, c + 1)
                if not is_int(c) or c > 0:
                    act.wait_ge(s_n1, c)
                    act.wait_ge(s_den, c)
                nc.scalar.activation(M1[:, :], DD[:, :], ACT.Relu, scale=-1.0).then_inc(s_m, 1)
                nc.scalar.activation(M2[:, :], DD[:, :], ACT.Relu).then_inc(s_m, 1)
                act.wait_ge(s_m, 2 * c + 1)
                nc.scalar.activation(M1[:, :], M1[:, :], ACT.Exp, scale=-1.0).then_inc(s_g, 1)
                act.wait_ge(s_m, 2 * c + 2)
                nc.scalar.activation(M2[:, :], M2[:, :], ACT.Exp, scale=-1.0).then_inc(s_g, 1)

            def inverse_of_den(c):
                act.wait_ge(s_den, c + 1)
                if not is_int(c) or c > 0:
                    act.wait_ge(s_rw, c)
                nc.scalar.activation(LQ[:, :], DEN[:, :], ACT.Ln).then_inc(s_lq, 1)
                act.wait_ge(s_lq, c + 1)
                nc.scalar.activation(LQ[:, :], LQ[:, :], ACT.Exp, scale=-1.0).then_inc(s_iq, 1)

            def shared_tanh(c, q):
                act.wait_ge(s_sg, 2 * c + q + 1)
                if not (is_int(c) and c == 0 and q == 0):
                    act.wait_ge(s_ps, 2 * c + q)
                nc.scalar.activation(TG[:, :], SHG[q][:, :], ACT.Tanh, scale=0.5).then_inc(s_tg, 1)

            def ffn_tanh(c):
                act.wait_ge(s_fr, c + 1)
                if not is_int(c) or c > 0:
                    act.wait_ge(s_u, c)
                nc.scalar.activation(TF[:, :], FB[:, :], ACT.Tanh, scale=0.5).then_inc(s_tf, 1)

            def ffn_squares(c, q):
                act.wait_ge(s_fk, 4 * c + q + 1)
                if not (is_int(c) and c == 0 and q < 2):
                    act.wait_ge(s_kk, 4 * c + q - 1)
                rk = RK[:, (q % 2) * CHUNK:(q % 2 + 1) * CHUNK]
                nc.scalar.activation(rk, (FA, FB)[q % 2][:, :], ACT.Relu).then_inc(s_rk, 1)
                act.wait_ge(s_rk, 4 * c + q + 1)
                if q == 0 and (not is_int(c) or c > 0):
                    act.wait_ge(s_kv, c)
                nc.scalar.activation(KK[:, q * CHUNK:(q + 1) * CHUNK], rk, ACT.Square).then_inc(s_kk, 1)

            def shared_out(c):
                act.wait_ge(s_sd, c + 1)
                nc.scalar.activation(chunk(XT, c), BO[:, :], ACT.Copy).then_inc(s_sh, 1)

            def expert_slot(n):
                a = 0 if exists(n, 1) else P
                if not exists(n, -2) and not exists(n, 1):
                    a = P + EF
                b = P + EF + CH if exists(n, -3) else P + EF if exists(n, -2) else P
                act.wait_ge(s_xht, num(n, 2))
                if not is_int(n) or n >= 2 * NXH:
                    act.wait_ge(s_yo[third(n)], y_sent(n))
                nc.scalar.activation(XH[third(n)][:, a:b], BX[:, a:b], ACT.Copy).then_inc(s_xh, 1)
                if exists(n):
                    act.wait_ge(s_gu, num(n, 1))
                    if not is_int(n) or n > 0:
                        act.wait_ge(s_px, num(n))
                    nc.scalar.activation(TX[:, :], BGU[parity(n)][:, 0:EF], ACT.Tanh, scale=0.5).then_inc(s_tx, 1)

            def final_tanh(c, u):
                act.wait_ge(s_fy, c + 1)
                nc.scalar.activation(FT[u], FY[u], ACT.Tanh, scale=0.5).then_inc(s_ft, 1)

            def step_zero(i):
                shared_tanh(CPS * i + 0, 0)
                make_h1(i + 1)
                scores()
                shared_tanh(CPS * i + 0, 1)
                shared_tanh(CPS * i + 1, 0)
                shared_out(CPS * i + 0)
                shared_tanh(CPS * i + 1, 1)
                shared_tanh(CPS * i + 2, 0)
                shared_out(CPS * i + 1)
                shared_tanh(CPS * i + 2, 1)
                shared_out(CPS * i + 2)
                shared_tanh(CPS * i + 3, 0)
                inverse_of_den(i)
                shared_tanh(CPS * i + 3, 1)
                shared_out(CPS * i + 3)
                wkv_exponentials(i + 1)

            def step_one(i):
                C = has(i, "C")
                shared_tanh(CPS * i + 0, 0)
                make_h1(i + 1)
                shared_tanh(CPS * i + 0, 1)
                if C:
                    make_h2(i - 1)
                shared_tanh(CPS * i + 1, 0)
                shared_out(CPS * i + 0)
                shared_tanh(CPS * i + 1, 1)
                shared_tanh(CPS * i + 2, 0)
                inverse_of_den(i)
                shared_tanh(CPS * i + 2, 1)
                shared_out(CPS * i + 1)
                if C:
                    ffn_tanh(i - 1)
                    ffn_squares(i - 1, 0)
                    ffn_squares(i - 1, 1)
                shared_out(CPS * i + 2)
                if C:
                    ffn_squares(i - 1, 2)
                    ffn_squares(i - 1, 3)
                shared_tanh(CPS * i + 3, 0)
                shared_tanh(CPS * i + 3, 1)
                wkv_exponentials(i + 1)
                shared_out(CPS * i + 3)

            def step_two(i):
                slots(expert_slot, i, 0)
                if has(i, "P"):
                    make_h1(i + 1)
                slots(expert_slot, i, 1)
                slots(expert_slot, i, 2)
                make_h2(i - 1)
                slots(expert_slot, i, 3)
                ffn_tanh(i - 1)
                ffn_squares(i - 1, 0)
                if is_int(i) and i == CHUNKS:
                    final_tanh(0, 0)
                slots(expert_slot, i, 4)
                ffn_squares(i - 1, 1)
                if is_int(i) and i == CHUNKS:
                    final_tanh(1, 1)
                ffn_squares(i - 1, 2)
                if is_int(i) and i == CHUNKS:
                    final_tanh(2, 0)
                slots(expert_slot, i, 5)
                ffn_squares(i - 1, 3)
                if is_int(i) and i == CHUNKS:
                    final_tanh(3, 1)
                if has(i, "T"):
                    inverse_of_den(i)
                if has(i, "P"):
                    wkv_exponentials(i + 1)

            def step(i, scatter):
                (step_zero if is_int(i) and i == 0 else step_one if scatter else step_two)(i)

            def before_experts():
                act.wait_ge(s_we, 16 * 2)
                nc.scalar.activation(EDN[:, :], EDN[:, :], ACT.Copy, scale=0.5).then_inc(s_halfe, 1)
                expert_slot(-1)
                expert_slot(0)

            make_h1(0)
            act.wait_ge(s_v2, 2 * CHUNKS + 1)
            nc.scalar.activation(R2[:, 2 * TPC:], V2[:, 2 * TPC:], ACT.Ln).then_inc(s_r2, 1)
            act.wait_ge(s_r2, 1)
            nc.scalar.activation(R2[:, 2 * TPC:], R2[:, 2 * TPC:], ACT.Exp, scale=-0.5).then_inc(s_r2, 1)
            wkv_exponentials(0)
            drive(act, step, before_experts)

            with act.Fori(2, CHUNKS // 2) as h:
                for u in range(2):
                    final_tanh(2 * h + u, u)

        @block.gpsimd
        def _(pool):
            nc.gpsimd.memset(XSS[0][:, :], 0.0).then_inc(s_pad, 1)
            pool.wait_ge(s_pad, 1)
            nc.gpsimd.memset(XSS[0][:, CH:CH + 1], NOWHERE).then_inc(s_pad, 1)
            nc.gpsimd.memset(XSS[1][:, :], 0.0).then_inc(s_init, 1)
            nc.gpsimd.memset(NH[:, :], -0.5).then_inc(s_init, 1)
            nc.gpsimd.memset(PP[:, :], NEG).then_inc(s_init, 1)
            for t in (H1, H2, AA, BB):
                last = nc.gpsimd.memset(t[:, :], 0.0)
            last.then_inc(s_init, 1)
            pool.wait_ge(s_init, 4)

            def first(c, w):
                mean, var = stats(MV[w])
                a, r = SM[w][:, 2 * TPC:3 * TPC], SM[w][:, TPC:2 * TPC]
                pool.wait_ge(s_mv, TPC * (c + 1))
                settle(pool)
                nc.gpsimd.tensor_scalar(SM[w][:, 0:TPC], var, EPS, None, ALU.add).then_inc(s_sm, 1)
                pool.wait_ge(s_sm, c + 1)
                nc.gpsimd.tensor_tensor(r, SM[w][:, 0:TPC], NH[:, 0:TPC], ALU.pow).then_inc(s_rs, 1)
                pool.wait_ge(s_rs, c + 1)
                nc.gpsimd.tensor_tensor(a, r, var, ALU.mult).then_inc(s_v2, 1)
                pool.wait_ge(s_v2, 2 * c + 1)
                nc.gpsimd.tensor_tensor(chunk(V2, c, TPC), a, r, ALU.mult).then_inc(s_v2, 1)

            with pool.Fori(0, CHUNKS // 4) as h:
                for w in range(4):
                    first(4 * h + w, w)
            pool.wait_ge(s_v2, 2 * CHUNKS)
            nc.gpsimd.tensor_scalar(V2[:, :], V2[:, :], EPS, None, ALU.add).then_inc(s_v2, 1)
            pool.wait_ge(s_v2, 2 * CHUNKS + 1)
            nc.gpsimd.tensor_tensor(R2[:, 0:2 * TPC], V2[:, 0:2 * TPC], NH[:, 0:2 * TPC], ALU.pow).then_inc(s_r2a, 1)

            def make_z1(c):
                if not is_int(c) or c > 1:
                    pool.wait_ge(s_r2, 2)
                else:
                    pool.wait_ge(s_r2a, 1)
                if is_int(c) and c == 0:
                    pool.wait_ge(s_xn, 1)
                elif is_int(c) and c == 1:
                    pool.wait_ge(s_xn, CHUNKS)
                if not is_int(c) or c > 0:
                    pool.wait_ge(s_z1t, c)
                nc.gpsimd.tensor_tensor(tiles(Z1[:, :]), tiles(chunk(XN, c)), per_tile(chunk(R2, c, TPC)),
                                        ALU.mult).then_inc(s_z1, 1)

            def make_d1(c):
                pool.wait_ge(s_h1, c + 1)
                if not is_int(c) or c > 0:
                    pool.wait_ge(s_mix, 3 * c)
                nc.gpsimd.tensor_tensor(batches(D1[:, :]), now(H1), before(H1), ALU.subtract).then_inc(s_d1, 1)

            def rstd_of_x2(c):
                mean, var = stats(MV2)
                pool.wait_ge(s_mv2, TPC * (c + 1))
                settle(pool)
                nc.gpsimd.tensor_scalar(SM2[:, 0:TPC], var, EPS, None, ALU.add).then_inc(s_sm2, 1)
                pool.wait_ge(s_sm2, c + 1)
                nc.gpsimd.tensor_tensor(SM2[:, TPC:2 * TPC], SM2[:, 0:TPC], NH[:, 0:TPC], ALU.pow)\
                  .then_inc(s_rs2, 1)

            def wkv_den(c):
                pool.wait_ge(s_g, 2 * c + 2)
                pool.wait_ge(s_bb, 2 * c + 2)
                if not is_int(c) or c > 0:
                    pool.wait_ge(s_lq, c)
                nc.gpsimd.tensor_tensor(batches(Q1[:, :]), batches(M1[:, :]), before(BB), ALU.mult).then_inc(s_q1, 1)
                pool.wait_ge(s_q1, c + 1)
                nc.gpsimd.tensor_tensor(DEN[:, :], Q1[:, :], M2[:, :], ALU.add).then_inc(s_den, 1)

            def wkv_num(c):
                pool.wait_ge(s_aa, 2 * c + 2)
                nc.gpsimd.tensor_tensor(batches(N1[:, :]), batches(M1[:, :]), before(AA), ALU.mult).then_inc(s_n1, 1)
                pool.wait_ge(s_n1, c + 1)
                pool.wait_ge(s_n2, c + 1)
                nc.gpsimd.tensor_tensor(NUM[:, :], N1[:, :], N2[:, :], ALU.add).then_inc(s_num, 1)

            def make_rw(c):
                pool.wait_ge(s_tn, c + 1)
                pool.wait_ge(s_iq, c + 1)
                if not is_int(c) or c > 0:
                    pool.wait_ge(s_att, c)
                nc.gpsimd.tensor_tensor(RW[:, :], NUM[:, :], LQ[:, :], ALU.mult).then_inc(s_rw, 1)

            def scatter_rows(i, q):
                u, c = q % 2, i * CPS + q
                pool.wait_ge(s_xss, 3 * c + 3)
                settle(pool)
                for j in range(TPC):
                    nc.gpsimd.indirect_dma_start(
                        xs_dram, bass.IndirectOffsetOnAxis(ap=PIX[u][:, j:j + 1], axis=0),
                        XSS[u][:, j * XROW:(j + 1) * XROW], None).then_inc(s_sct[u], 16)

            def expert_slot(n):
                if exists(n):
                    u = place(n)
                    pool.wait_ge(s_xs[u], 16 * laps(n))
                    if not is_int(n) or n >= NX:
                        pool.wait_ge(s_yo[third(n)], y_sent(n))
                    settle(pool)
                    nc.gpsimd.tensor_copy(YI[u][:, :], XS[u][:, CH:CH + 1]).then_inc(s_yi, 1)
                if exists(n, -3):
                    u = place(n, -3)
                    pool.wait_ge(s_yi, num(n, -2))
                    pool.wait_ge(s_xh, num(n, 2))
                    settle(pool)
                    nc.gpsimd.indirect_dma_start(
                        routed_dram, bass.IndirectOffsetOnAxis(ap=YI[u][:, 0:1], axis=0),
                        XH[third(n)][:, P + EF:P + EF + CH], None,
                        bounds_check=TOKENS - 1, oob_is_err=False).then_inc(s_yo[third(n)], 16)

            def final(c, u, h, xc):
                pool.wait_ge(s_fv, c + 1)
                if not is_int(h) or h > 0:
                    pool.wait_ge(s_out[u], 16 * h)
                nc.gpsimd.tensor_tensor(FO4[u][:, :], FV[u % 2], xc, ALU.add).then_inc(s_fo, 1)

            def step_zero(i):
                make_z1(i + 1)
                wkv_den(i)
                wkv_num(i)
                make_d1(i + 1)
                scatter_rows(i, 0)
                scatter_rows(i, 1)
                make_rw(i)
                scatter_rows(i, 2)
                scatter_rows(i, 3)

            def step_one(i):
                C = has(i, "C")
                make_z1(i + 1)
                if C:
                    rstd_of_x2(i - 1)
                wkv_den(i)
                scatter_rows(i, 0)
                wkv_num(i)
                make_rw(i)
                scatter_rows(i, 1)
                make_d1(i + 1)
                scatter_rows(i, 2)
                scatter_rows(i, 3)

            def step_two(i):
                if has(i, "P"):
                    make_z1(i + 1)
                if has(i, "T"):
                    wkv_den(i)
                rstd_of_x2(i - 1)
                slots(expert_slot, i, 0)
                if has(i, "P"):
                    make_d1(i + 1)
                if has(i, "T"):
                    wkv_num(i)
                slots(expert_slot, i, 1)
                slots(expert_slot, i, 2)
                slots(expert_slot, i, 3)
                slots(expert_slot, i, 4)
                slots(expert_slot, i, 5)
                if has(i, "T"):
                    make_rw(i)
                if is_int(i) and i == CHUNKS:
                    for u in range(4):
                        final(u, u, 0, XR4[u][:, :])

            def step(i, scatter):
                (step_zero if is_int(i) and i == 0 else step_one if scatter else step_two)(i)

            make_z1(0)
            make_d1(0)
            pool.wait_ge(s_fill, 16)
            nc.gpsimd.memset(XSS[0][:, CH:CH + 1], 0.0).then_inc(s_init, 1)
            drive(pool, step, lambda: expert_slot(0))

            pool.wait_ge(s_xf, 16)
            with pool.Fori(1, 3) as h:
                for u in range(4):
                    final(4 * h + u, u, h, XF1[:, ds(h * (4 * CHUNK) + (u - 4) * CHUNK, CHUNK)])
            pool.wait_ge(s_xf, 32)
            for u in range(4):
                final(12 + u, u, 3, XF2[:, u * CHUNK:(u + 1) * CHUNK])

        @block.vector
        def _(dve):
            def first_stats(c, w, h):
                dve.wait_ge(s_xi[w], 16 * (h + 1))
                if not is_int(c) or c > 1:
                    dve.wait_ge(s_mv, TPC * (c - 1))
                for j in range(TPC):
                    nc.vector.bn_stats(BS[w % 2][:, j * 6:(j + 1) * 6], XR4[w][:, j * P:(j + 1) * P])\
                      .then_inc(s_bn, 1)

            def first_aggregate(c, w):
                dve.wait_ge(s_bn, TPC * c + TPC)
                if not is_int(c) or c > 3:
                    dve.wait_ge(s_v2, 2 * c - 6)
                    dve.wait_ge(s_xns, c - 3)
                settle(dve)
                for j in range(TPC):
                    nc.vector.bn_aggr(MV[w][:, j * 2:(j + 1) * 2], BS[w % 2][:, j * 6:(j + 1) * 6]).then_inc(s_mv, 1)

            def first_xn(c, w):
                mean, var = stats(MV[w])
                r = SM[w][:, TPC:2 * TPC]
                dve.wait_ge(s_rs, c + 1)
                if not is_int(c) or c > 1:
                    dve.wait_ge(s_xnt, c - 1)
                    dve.wait_ge(s_xn, c - 1)
                for j in range(TPC):
                    last = nc.vector.tensor_scalar(ZC[w % 2][:, j * P:(j + 1) * P], XR4[w][:, j * P:(j + 1) * P],
                                                   mean[:, j:j + 1], r[:, j:j + 1], ALU.subtract, ALU.mult)
                last.then_inc(s_xns, 1)

            for w in range(4):
                first_stats(w, w, 0)
                if w >= 2:
                    first_xn(w - 2, w - 2)
                first_aggregate(w, w)
            with dve.Fori(1, CHUNKS // 4) as h:
                for w in range(4):
                    first_stats(4 * h + w, w, h)
                    first_xn(4 * h + w - 2, (w + 2) % 4)
                    first_aggregate(4 * h + w, w)
            for w in (2, 3):
                first_xn(CHUNKS - 4 + w, w)

            done = [0]

            def link(ins):
                done[0] += 1
                ins.then_inc(s_rt, 1)
                dve.wait_ge(s_rt, done[0])

            J, E = TILES, EXPERTS
            lg = BG[:, :].rearrange("p (j e) -> p j e", e=E)
            cand = CAND[:, :].rearrange("p (j e) -> p j e", e=E)
            oh_je = OH[:, :].rearrange("p (e j) -> p j e", e=E)
            oh = OH[:, :].rearrange("p (e j) -> p e j", e=E)
            cum = CUM[:, :].rearrange("p (e j) -> p e j", e=E)
            rt = [RT[:, k * E:(k + 1) * E] for k in range(8)]
            tot, before_me, counts, tiles_of, upto, base = rt[0], rt[1], rt[2], rt[3], rt[4], rt[5]
            cmp = CAND[:, :].rearrange("p (e k) -> p e k", e=E)

            def routing_choice():
                dve.wait_ge(s_lg, CHUNKS)
                link(nc.vector.tensor_reduce(MX[:, :], lg, AX.X, ALU.max))
                link(nc.vector.tensor_tensor(cand, lg, MX[:, :].unsqueeze(2).to_broadcast([P, J, E]), ALU.is_equal))
                link(nc.vector.tensor_tensor(cand, cand, CST[:, K_E8:K_E8 + E].unsqueeze(1).to_broadcast([P, J, E]),
                                             ALU.mult))
                link(nc.vector.tensor_reduce(POSF[:, :], cand, AX.X, ALU.max))
                nc.vector.tensor_tensor(oh_je, cand, POSF[:, :].unsqueeze(2).to_broadcast([P, J, E]), ALU.is_equal)\
                  .then_inc(s_oh, 1)
                dve.wait_ge(s_oh, 1)

            def routing_counts():
                for e in range(E):
                    link(nc.vector.tensor_tensor_scan(cum[:, e, :], CST[:, K_ONE:K_ONE + J], oh[:, e, :], 0.0,
                                                      ALU.mult, ALU.add))
                link(nc.vector.tensor_copy(tot, cum[:, :, J - 1]))

            def routing_starts():
                dve.wait_ge(s_rm, 1)
                link(nc.vector.tensor_copy(before_me, BG[:, 0:E]))
                link(nc.vector.tensor_copy(counts, BG[:, E:2 * E]))
                link(nc.vector.tensor_tensor(cmp, counts.unsqueeze(2).to_broadcast([P, E, J]),
                                             CST[:, K_CAP:K_CAP + J].unsqueeze(1).to_broadcast([P, E, J]), ALU.is_gt))
                link(nc.vector.tensor_reduce(tiles_of, cmp, AX.X, ALU.add))
                link(nc.vector.tensor_tensor_scan(upto, CST[:, K_ONE:K_ONE + E], tiles_of, 0.0, ALU.mult, ALU.add))
                link(nc.vector.tensor_tensor(base, upto, tiles_of, ALU.subtract))
                link(nc.vector.tensor_scalar(base, base, float(P), -1.0, ALU.mult, ALU.add))
                link(nc.vector.tensor_tensor(base, base, before_me, ALU.add))

            def routing_rows():
                link(nc.vector.tensor_tensor(cum, cum, base.unsqueeze(2).to_broadcast([P, E, J]), ALU.add))
                link(nc.vector.tensor_tensor(cum, cum, oh, ALU.mult))
                link(nc.vector.tensor_reduce(POSF[:, :], CUM[:, :].rearrange("p (e j) -> p j e", e=E), AX.X, ALU.add))
                link(nc.vector.tensor_copy(POS[:, :], POSF[:, :]))
                X = 72
                last = CAND[0:1, 0:X * (E - 1)].rearrange("p (n e) -> p n e", e=E - 1)
                link(nc.vector.tensor_tensor(last, CST[0:1, K_TILE:K_TILE + X].unsqueeze(2).to_broadcast([1, X, E - 1]),
                                             upto[0:1, 0:E - 1].unsqueeze(1).to_broadcast([1, X, E - 1]), ALU.is_ge))
                nc.vector.tensor_reduce(CUM[0:1, 0:X], last, AX.X, ALU.add).then_inc(s_oh, 1)
                dve.wait_ge(s_oh, 2)
                link(nc.vector.tensor_copy(ET[0:1, 0:X], CUM[0:1, 0:X]))

            dve.wait_ge(s_w, 16 * 3)
            dve.wait_ge(s_w0, 1)
            nc.vector.tensor_scalar(vec(V_W), vec(V_W), -1.0, None, ALU.mult).then_inc(s_w1, 1)
            dve.wait_ge(s_w1, 1)
            dve.wait_ge(s_init, 4)

            def time_mixes(c):
                dve.wait_ge(s_d1, c + 1)
                if not is_int(c) or c > 0:
                    dve.wait_ge(s_r, c)
                for dst, m in ((XK, V_TMK), (XV, V_TMV), (XR, V_TMR)):
                    nc.vector.scalar_tensor_tensor(batches(dst[:, :]), batches(D1[:, :]), vec(m), before(H1),
                                                   ALU.mult, ALU.add).then_inc(s_mix, 1)

            def running_max(c):
                dve.wait_ge(s_k, c + 1)
                for b in range(BPC):
                    o = b * (SEQ + 1) + 1
                    nc.vector.tensor_tensor_scan(PP[:, o:o + SEQ], vec(V_W).to_broadcast([P, SEQ]),
                                                 BK[:, b * SEQ:(b + 1) * SEQ], NEG, ALU.add, ALU.max)\
                      .then_inc(s_pp, 1)
                dve.wait_ge(s_pp, 2 * c + 2)
                if not is_int(c) or c > 0:
                    dve.wait_ge(s_aa, 2 * c)
                nc.vector.scalar_tensor_tensor(batches(E1[:, :]), before(PP), vec(V_W), now(PP),
                                               ALU.add, ALU.subtract).then_inc(s_a, 1)
                nc.vector.tensor_tensor(batches(E2[:, :]), batches(BK[:, :]), now(PP), ALU.subtract).then_inc(s_b, 1)
                if not is_int(c) or c > 0:
                    dve.wait_ge(s_m, 2 * c)
                nc.vector.scalar_tensor_tensor(batches(DD[:, :]), before(PP), vec(V_FIRST), batches(BK[:, :]),
                                               ALU.subtract, ALU.subtract).then_inc(s_d, 1)

            def wkv_b(c):
                dve.wait_ge(s_e2, c + 1)
                dve.wait_ge(s_v, c + 1)
                nc.vector.tensor_tensor(EV[:, :], E2[:, :], BV[:, :], ALU.mult).then_inc(s_ev, 1)
                dve.wait_ge(s_e1, c + 1)
                if not is_int(c) or c > 0:
                    dve.wait_ge(s_q1, c)
                for b in range(BPC):
                    o = b * (SEQ + 1) + 1
                    nc.vector.tensor_tensor_scan(BB[:, o:o + SEQ], E1[:, b * SEQ:(b + 1) * SEQ],
                                                 E2[:, b * SEQ:(b + 1) * SEQ], 0.0, ALU.mult, ALU.add)\
                      .then_inc(s_bb, 1)

            def wkv_a(c):
                dve.wait_ge(s_ev, c + 1)
                if not is_int(c) or c > 0:
                    dve.wait_ge(s_n1, c)
                for b in range(BPC):
                    o = b * (SEQ + 1) + 1
                    nc.vector.tensor_tensor_scan(AA[:, o:o + SEQ], E1[:, b * SEQ:(b + 1) * SEQ],
                                                 EV[:, b * SEQ:(b + 1) * SEQ], 0.0, ALU.mult, ALU.add)\
                      .then_inc(s_aa, 1)
                dve.wait_ge(s_g, 2 * c + 2)
                if not is_int(c) or c > 0:
                    dve.wait_ge(s_num, c)
                nc.vector.tensor_tensor(N2[:, :], M2[:, :], BV[:, :], ALU.mult).then_inc(s_n2, 1)

            def make_tn(c):
                dve.wait_ge(s_num, c + 1)
                dve.wait_ge(s_tr, c + 1)
                nc.vector.scalar_tensor_tensor(NUM[:, :], TR[:, :], 1.0, NUM[:, :], ALU.add, ALU.mult)\
                  .then_inc(s_tn, 1)

            def make_x2(c):
                dve.wait_ge(s_att, c + 1)
                if not is_int(c) or c > 0:
                    dve.wait_ge(s_s, c)
                    dve.wait_ge(s_z2, TPC * c)
                nc.vector.tensor_tensor(X2[:, :], BO[:, :], chunk(XN, c), ALU.add).then_inc(s_x2, 1)
                dve.wait_ge(s_x2, c + 1)
                for j in range(TPC):
                    nc.vector.bn_stats(BS2[:, j * 6:(j + 1) * 6], X2[:, j * P:(j + 1) * P]).then_inc(s_bn2, 1)
                dve.wait_ge(s_bn2, TPC * c + TPC)
                settle(dve)
                for j in range(TPC):
                    nc.vector.bn_aggr(MV2[:, j * 2:(j + 1) * 2], BS2[:, j * 6:(j + 1) * 6]).then_inc(s_mv2, 1)

            def make_z2(c):
                mean, var = stats(MV2)
                dve.wait_ge(s_rs2, c + 1)
                if not is_int(c) or c > 0:
                    dve.wait_ge(s_z2t, c)
                for j in range(TPC):
                    nc.vector.tensor_scalar(Z2[:, j * P:(j + 1) * P], X2[:, j * P:(j + 1) * P], mean[:, j:j + 1],
                                            SM2[:, TPC + j:TPC + j + 1], ALU.subtract, ALU.mult).then_inc(s_z2, 1)

            def rows_to_scatter(i, q):
                u, c = q % 2, i * CPS + q
                if is_int(i) and i == 0 and q == 0:
                    dve.wait_ge(s_sc, 1)
                    dve.wait_ge(s_init, 5)
                if q >= 2 or not is_int(i) or i > 0:
                    dve.wait_ge(s_sct[u], 16 * TPC * (i * (CPS // 2) + q // 2))
                rows = XSS[u][:, :].rearrange("p (j c) -> p j c", j=TPC)
                nc.vector.tensor_tensor(rows[:, :, 0:CH], tiles(chunk(XN, c)), per_tile(chunk(SC, c, TPC)),
                                        ALU.mult).then_inc(s_xss, 1)
                nc.vector.tensor_copy(rows[:, :, CH], CST[:, ds(K_TOK + c * TPC, TPC)]).then_inc(s_xss, 1)
                nc.vector.tensor_copy(PIX[u][:, :], chunk(POS, c, TPC)).then_inc(s_xss, 1)

            def channel_mixes(c):
                dve.wait_ge(s_h2, c + 1)
                if not is_int(c) or c > 0:
                    dve.wait_ge(s_mix2, 2 * c)
                    dve.wait_ge(s_fk, 4 * c)
                nc.vector.tensor_tensor(batches(D2[:, :]), now(H2), before(H2), ALU.subtract).then_inc(s_d2, 1)
                dve.wait_ge(s_d2, c + 1)
                for dst, m in ((XR2, V_FTMR), (XK2, V_FTMK)):
                    nc.vector.scalar_tensor_tensor(batches(dst[:, :]), batches(D2[:, :]), vec(m), before(H2),
                                                   ALU.mult, ALU.add).then_inc(s_mix2, 1)

            def make_s(c):
                dve.wait_ge(s_kv, c + 1)
                dve.wait_ge(s_tf, c + 1)
                nc.vector.scalar_tensor_tensor(UU[:, :], TF[:, :], 1.0, BO[:, :], ALU.add, ALU.mult).then_inc(s_u, 1)
                dve.wait_ge(s_u, c + 1)
                nc.vector.scalar_tensor_tensor(chunk(XN, c), UU[:, :], 0.5, X2[:, :], ALU.mult, ALU.add)\
                  .then_inc(s_s, 1)

            def shared_gated(c, q):
                dve.wait_ge(s_tg, 2 * c + q + 1)
                if not (is_int(c) and c == 0 and q == 0):
                    dve.wait_ge(s_hs, 2 * c + q)
                nc.vector.scalar_tensor_tensor(PS[:, :], TG[:, :], 1.0, SHG[q][:, :], ALU.add, ALU.mult)\
                  .then_inc(s_ps, 1)
                dve.wait_ge(s_ps, 2 * c + q + 1)
                dve.wait_ge(s_su, 2 * c + q + 1)
                if q == 0 and (not is_int(c) or c > 0):
                    dve.wait_ge(s_sd, c)
                nc.vector.tensor_tensor(HS[:, q * CHUNK:(q + 1) * CHUNK], PS[:, :], SHU[q][:, :], ALU.mult)\
                  .then_inc(s_hs, 1)

            def expert_slot(n):
                if exists(n):
                    gu = BGU[parity(n)]
                    dve.wait_ge(s_tx, num(n, 1))
                    if not is_int(n) or n > 0:
                        dve.wait_ge(s_hx, num(n))
                    nc.vector.scalar_tensor_tensor(PX[:, :], TX[:, :], 1.0, gu[:, 0:EF], ALU.add, ALU.mult)\
                      .then_inc(s_px, 1)
                    dve.wait_ge(s_px, num(n, 1))
                    if not is_int(n) or n > 1:
                        dve.wait_ge(s_xht, num(n, 2))
                    nc.vector.tensor_tensor(HX[parity(n)][:, :], PX[:, :], gu[:, EF:2 * EF], ALU.mult)\
                      .then_inc(s_hx, 1)

            def final(c, w, h):
                dve.wait_ge(s_fx[w], 16 * (h + 2))
                nc.vector.tensor_tensor(FY[w % 2], RR4[w][:, :], chunk(XT, c), ALU.add).then_inc(s_fy, 1)

            def final2(c, w, h):
                u = w % 2
                dve.wait_ge(s_ft, c + 1)
                nc.vector.scalar_tensor_tensor(FW[u], FT[u], 1.0, FY[u], ALU.add, ALU.mult).then_inc(s_fw, 1)
                dve.wait_ge(s_fw, c + 1)
                if not is_int(c) or c > 1:
                    dve.wait_ge(s_fo, c - 1)
                nc.vector.scalar_tensor_tensor(FV[u], FW[u], 0.5, chunk(XN, c), ALU.mult, ALU.mult)\
                  .then_inc(s_fv, 1)

            def final_four(h):
                for w in range(4):
                    final(4 * h + w, w, h)
                    if w > 0:
                        final2(4 * h + w - 1, w - 1, h)
                final2(4 * h + 3, 3, h)

            def step_zero(i):
                wkv_a(i)
                shared_gated(CPS * i + 0, 0)
                routing_starts()
                shared_gated(CPS * i + 0, 1)
                routing_rows()
                rows_to_scatter(i, 0)
                shared_gated(CPS * i + 1, 0)
                rows_to_scatter(i, 1)
                make_tn(i)
                shared_gated(CPS * i + 1, 1)
                shared_gated(CPS * i + 2, 0)
                shared_gated(CPS * i + 2, 1)
                rows_to_scatter(i, 2)
                time_mixes(i + 1)
                shared_gated(CPS * i + 3, 0)
                rows_to_scatter(i, 3)
                shared_gated(CPS * i + 3, 1)
                running_max(i + 1)
                wkv_b(i + 1)

            def step_one(i):
                C = has(i, "C")
                wkv_a(i)
                shared_gated(CPS * i + 0, 0)
                if C:
                    make_x2(i - 1)
                shared_gated(CPS * i + 0, 1)
                if C:
                    make_z2(i - 1)
                rows_to_scatter(i, 0)
                shared_gated(CPS * i + 1, 0)
                rows_to_scatter(i, 1)
                shared_gated(CPS * i + 1, 1)
                make_tn(i)
                shared_gated(CPS * i + 2, 0)
                if C:
                    channel_mixes(i - 1)
                shared_gated(CPS * i + 2, 1)
                rows_to_scatter(i, 2)
                time_mixes(i + 1)
                rows_to_scatter(i, 3)
                shared_gated(CPS * i + 3, 0)
                if C:
                    make_s(i - 1)
                shared_gated(CPS * i + 3, 1)
                running_max(i + 1)
                wkv_b(i + 1)

            def step_two(i):
                make_x2(i - 1)
                slots(expert_slot, i, 0)
                if has(i, "T"):
                    wkv_a(i)
                make_z2(i - 1)
                slots(expert_slot, i, 1)
                slots(expert_slot, i, 2)
                channel_mixes(i - 1)
                slots(expert_slot, i, 3)
                if has(i, "P"):
                    time_mixes(i + 1)
                slots(expert_slot, i, 4)
                if has(i, "T"):
                    make_tn(i)
                slots(expert_slot, i, 5)
                if has(i, "P"):
                    running_max(i + 1)
                if is_int(i) and i == CHUNKS:
                    final_four(0)
                make_s(i - 1)
                if has(i, "P"):
                    wkv_b(i + 1)

            def step(i, scatter):
                (step_zero if is_int(i) and i == 0 else step_one if scatter else step_two)(i)

            time_mixes(0)
            routing_choice()
            routing_counts()
            running_max(0)
            wkv_b(0)
            drive(dve, step, lambda: expert_slot(0))

            dve.wait_ge(s_s, CHUNKS)
            with dve.Fori(1, CHUNKS // 4) as h:
                final_four(h)


def constants():
    import numpy as np
    c = np.zeros((P, NCST), np.float32)
    p = np.arange(P)
    c[:, K_ID:K_ID + P] = np.eye(P)
    c[:, K_TRI:K_TRI + P] = p[:, None] < p[None, :]
    c[:, K_ONE:K_ONE + P] = 1.0
    c[:, K_E8:K_E8 + EXPERTS] = EXPERTS - np.arange(EXPERTS)
    c[:, K_CAP:K_CAP + TILES] = P * np.arange(TILES)
    c[:, K_TILE:K_TILE + 80] = np.arange(80)
    c[:, K_TOK:K_TOK + TILES] = P * np.arange(TILES)[None, :] + p[:, None]
    return c


def kernel(**inputs):
    import numpy as np
    import concourse.bacc as bacc
    from concourse.bass_utils import run_bass_kernel_spmd

    a = {k[3:]: np.asarray(v) for k, v in inputs.items()}
    vecs = np.stack([a["attn_" + k] for k in (
        "ln1_w", "ln1_b", "ln2_w", "ln2_b", "time_decay", "time_first", "tmk", "tmv", "tmr", "f_tmk", "f_tmr")], 1)
    att = np.concatenate([a["attn_" + k].T for k in ("att_kw", "att_vw", "att_rw", "att_ow", "f_rw")], 1)
    arrays = {
        "x": a["attn_x"].reshape(TOKENS, CH),
        "vecs": vecs,
        "cst": constants(),
        "att_w": att,
        "f_kw": a["attn_f_kw"].T,
        "f_vw": a["attn_f_vw"].T.reshape(FQ, P, CH).transpose(1, 0, 2).reshape(P, FQ * CH),
        "gate_w": a["ffn_gate_w"].T,
        "sh_up": np.concatenate([a["ffn_shared_gate"].T, a["ffn_shared_up"].T], 1),
        "sh_dn": a["ffn_shared_down"].T.reshape(EQ, P, CH).transpose(1, 0, 2).reshape(P, EQ * CH),
        "ex_up": np.concatenate([a["ffn_r_gate"].transpose(2, 0, 1), a["ffn_r_up"].transpose(2, 0, 1)], 2)
        .reshape(P, EXPERTS * 2 * EF),
        "ex_dn": a["ffn_r_down"].transpose(2, 0, 1).reshape(EQ, P, EXPERTS, CH).transpose(1, 2, 0, 3)
        .reshape(P, EXPERTS * EQ * CH),
    }
    arrays = {k: np.ascontiguousarray(v) for k, v in arrays.items()}
    nc = bacc.Bacc("TRN2", target_bir_lowering=False, num_devices=1)
    args = {k: nc.dram_tensor(k, v.shape, mybir.dt.from_np(v.dtype), kind="ExternalInput").ap()
            for k, v in arrays.items()}
    args["out"] = nc.dram_tensor("out", (TOKENS, CH), mybir.dt.float32, kind="ExternalOutput").ap()
    program(nc, **args)
    r = run_bass_kernel_spmd(nc, [arrays], core_ids=[0])
    return r.results[0]["out"].reshape(BATCH, SEQ, CH)
```
